# Optimizing a Trainium2 kernel written in Bass

```python
import numpy as np
import jax
import jax.numpy as jnp

def _softmax(x, axis=-1):
    return jax.nn.softmax(x, axis=axis)

def _gelu(x):
    return jax.nn.gelu(x, approximate=True)

def _silu(x):
    return jax.nn.silu(x)

def _sigmoid(x):
    return jax.nn.sigmoid(x)

def _layernorm(x, axis=-1, eps=1e-05):
    m = jnp.mean(x, axis=axis, keepdims=True)
    v = jnp.var(x, axis=axis, keepdims=True)
    return (x - m) / jnp.sqrt(v + eps)

def _scatter_add(tgt, idx, src, axis=0):
    return tgt.at[idx].add(src)

def _segment_sum(src, seg, n):
    return jax.ops.segment_sum(src, seg, n)
kernel_name = 'mk_lm_tower_d2_tok_ids1024_r4_e5866e'

def setup_inputs(seed: int=0):
    np.random.seed(seed)
    _w = jnp.asarray

    def _rec_inputs():
        import jax
        import jax.numpy as jnp
        _rk = jax.random.key(seed)
        x = jax.random.randint(jax.random.fold_in(_rk, 1), (4, 512), 0, 31995, jnp.int32)
        return x
    x = _rec_inputs()

    def _L0_tok_setup():
        import jax, jax.numpy as jnp
        import numpy as np
        NUM_EMBEDDINGS = 32000
        EMBEDDING_DIM = 256
        EPS = 1e-05
        key = jax.random.key(seed)
        k_w, k_idx = jax.random.split(key)
        weight = jax.random.normal(k_w, (NUM_EMBEDDINGS, EMBEDDING_DIM), dtype=jnp.float32)
        input = jax.random.randint(k_idx, (4, 1024), 0, NUM_EMBEDDINGS, dtype=jnp.int64)
        return {'input': input, 'weight': weight}
    _L0_tok_all = _L0_tok_setup()
    _L0_tok_in = {k: v for k, v in _L0_tok_all.items() if k in ('weight',)}
    del _L0_tok_all

    def _L0_attn_setup():
        import jax, jax.numpy as jnp
        import numpy as np
        import math
        H = 16
        N_EMBD = 256
        EPS = 1e-05
        key = jax.random.key(seed)
        ks = jax.random.split(key, 6)
        B, T, C = (2, 512, 256)
        x = jax.random.normal(ks[0], (B, T, C), dtype=jnp.float32)
        s = 0.02
        Wq = jax.random.normal(ks[1], (C, N_EMBD), dtype=jnp.float32) * s
        Wk = jax.random.normal(ks[2], (C, N_EMBD), dtype=jnp.float32) * s
        Wv = jax.random.normal(ks[3], (C, N_EMBD), dtype=jnp.float32) * s
        Wo = jax.random.normal(ks[4], (N_EMBD, C), dtype=jnp.float32) * s
        return {'x': x, 'Wq': Wq, 'bq': jnp.zeros((N_EMBD,), jnp.float32), 'Wk': Wk, 'bk': jnp.zeros((N_EMBD,), jnp.float32), 'Wv': Wv, 'bv': jnp.zeros((N_EMBD,), jnp.float32), 'Wo': Wo, 'bo': jnp.zeros((C,), jnp.float32), 'gamma': jnp.ones((C,), jnp.float32), 'beta': jnp.zeros((C,), jnp.float32)}
    _L0_attn_all = _L0_attn_setup()
    _L0_attn_in = {k: v for k, v in _L0_attn_all.items() if k in ('Wq', 'bq', 'Wk', 'bk', 'Wv', 'bv', 'Wo', 'bo', 'gamma', 'beta')}
    del _L0_attn_all

    def _L0_ffn_setup():
        import jax, jax.numpy as jnp
        import numpy as np
        D, H, O, E, TOPK = (256, 1024, 256, 8, 2)
        B, L = (2, 512)
        ROUTE_SCALE = 1.0
        key = jax.random.key(seed)
        ks = jax.random.split(key, 7)
        gb = float(np.sqrt(6.0 / (E + D)))
        return {'x': jax.random.normal(ks[0], (B, L, D), dtype=jnp.float32), 'gate_w': jax.random.uniform(ks[1], (E, D), jnp.float32, -gb, gb), 'gate_b': jnp.zeros((E,), jnp.float32), 'w1': jax.random.normal(ks[2], (E, D, H), jnp.float32) * 0.02, 'b1': jnp.zeros((E, H), jnp.float32), 'w2': jax.random.normal(ks[3], (E, H, O), jnp.float32) * 0.02, 'b2': jnp.zeros((E, O), jnp.float32)}
    _L0_ffn_all = _L0_ffn_setup()
    _L0_ffn_in = {k: v for k, v in _L0_ffn_all.items() if k in ('gate_w', 'gate_b', 'w1', 'b1', 'w2', 'b2')}
    del _L0_ffn_all

    def _L1_attn_setup():
        import jax, jax.numpy as jnp
        import numpy as np
        D_MODEL = 256
        N_HEADS = 16
        HEAD_DIM = D_MODEL // N_HEADS
        MAX_LEN = 512
        BATCH = 2
        SEQ = 512
        key = jax.random.key(seed)
        ks = jax.random.split(key, 6)
        std = 1.0 / np.sqrt(D_MODEL)
        x = jax.random.normal(ks[0], (BATCH, SEQ, D_MODEL), dtype=jnp.float32)
        Wqkv = jax.random.uniform(ks[1], (D_MODEL, 3 * D_MODEL), minval=-std, maxval=std, dtype=jnp.float32)
        bqkv = jax.random.uniform(ks[2], (3 * D_MODEL,), minval=-std, maxval=std, dtype=jnp.float32)
        Wout = jax.random.uniform(ks[3], (D_MODEL, D_MODEL), minval=-std, maxval=std, dtype=jnp.float32)
        bout = jax.random.uniform(ks[4], (D_MODEL,), minval=-std, maxval=std, dtype=jnp.float32)
        rel_pos_bias = 0.02 * jax.random.normal(ks[5], (2 * MAX_LEN - 1,), dtype=jnp.float32)
        return {'x': x, 'Wqkv': Wqkv, 'bqkv': bqkv, 'Wout': Wout, 'bout': bout, 'rel_pos_bias': rel_pos_bias}
    _L1_attn_all = _L1_attn_setup()
    _L1_attn_in = {k: v for k, v in _L1_attn_all.items() if k in ('Wqkv', 'bqkv', 'Wout', 'bout', 'rel_pos_bias')}
    del _L1_attn_all

    def _L1_ffn_setup():
        import jax, jax.numpy as jnp
        import numpy as np
        import math
        D_IN = 256
        FEATURES = (1024, 1024, 256)
        BATCH, SEQ = (8, 512)

        def _conn_dense(kernel_bool, x):
            w = jnp.where(kernel_bool, jnp.float32(1.0), jnp.float32(-1.0))
            return x @ w
        key = jax.random.key(seed)
        kx, kk0, kk1, kk2 = jax.random.split(key, 4)
        x = jax.random.normal(kx, (BATCH, SEQ, D_IN), dtype=jnp.float32)
        k0 = jax.random.randint(kk0, (2 * D_IN, FEATURES[0]), 0, 2).astype(jnp.bool_)
        k1 = jax.random.randint(kk1, (FEATURES[0], FEATURES[1]), 0, 2).astype(jnp.bool_)
        k2 = jax.random.randint(kk2, (FEATURES[1], FEATURES[2]), 0, 2).astype(jnp.bool_)
        s0 = jnp.asarray(1.0 / math.sqrt(2 * D_IN), dtype=jnp.float32)
        s1 = jnp.asarray(1.0 / math.sqrt(FEATURES[0]), dtype=jnp.float32)
        s2 = jnp.asarray(1.0 / math.sqrt(FEATURES[1]), dtype=jnp.float32)
        return {'x': x, 'k0': k0, 'k1': k1, 'k2': k2, 's0': s0, 's1': s1, 's2': s2}
    _L1_ffn_all = _L1_ffn_setup()
    _L1_ffn_in = {k: v for k, v in _L1_ffn_all.items() if k in ('k0', 'k1', 'k2', 's0', 's1', 's2')}
    del _L1_ffn_all
    return {'x': x, 'L0_tok_weight': _L0_tok_in['weight'], 'L0_attn_Wq': _L0_attn_in['Wq'], 'L0_attn_bq': _L0_attn_in['bq'], 'L0_attn_Wk': _L0_attn_in['Wk'], 'L0_attn_bk': _L0_attn_in['bk'], 'L0_attn_Wv': _L0_attn_in['Wv'], 'L0_attn_bv': _L0_attn_in['bv'], 'L0_attn_Wo': _L0_attn_in['Wo'], 'L0_attn_bo': _L0_attn_in['bo'], 'L0_attn_gamma': _L0_attn_in['gamma'], 'L0_attn_beta': _L0_attn_in['beta'], 'L0_ffn_gate_w': _L0_ffn_in['gate_w'], 'L0_ffn_gate_b': _L0_ffn_in['gate_b'], 'L0_ffn_w1': _L0_ffn_in['w1'], 'L0_ffn_b1': _L0_ffn_in['b1'], 'L0_ffn_w2': _L0_ffn_in['w2'], 'L0_ffn_b2': _L0_ffn_in['b2'], 'L1_attn_Wqkv': _L1_attn_in['Wqkv'], 'L1_attn_bqkv': _L1_attn_in['bqkv'], 'L1_attn_Wout': _L1_attn_in['Wout'], 'L1_attn_bout': _L1_attn_in['bout'], 'L1_attn_rel_pos_bias': _L1_attn_in['rel_pos_bias'], 'L1_ffn_k0': _L1_ffn_in['k0'], 'L1_ffn_k1': _L1_ffn_in['k1'], 'L1_ffn_k2': _L1_ffn_in['k2'], 'L1_ffn_s0': _L1_ffn_in['s0'], 'L1_ffn_s1': _L1_ffn_in['s1'], 'L1_ffn_s2': _L1_ffn_in['s2']}

def reference(x, L0_tok_weight, L0_attn_Wq, L0_attn_bq, L0_attn_Wk, L0_attn_bk, L0_attn_Wv, L0_attn_bv, L0_attn_Wo, L0_attn_bo, L0_attn_gamma, L0_attn_beta, L0_ffn_gate_w, L0_ffn_gate_b, L0_ffn_w1, L0_ffn_b1, L0_ffn_w2, L0_ffn_b2, L1_attn_Wqkv, L1_attn_bqkv, L1_attn_Wout, L1_attn_bout, L1_attn_rel_pos_bias, L1_ffn_k0, L1_ffn_k1, L1_ffn_k2, L1_ffn_s0, L1_ffn_s1, L1_ffn_s2):
    import jax
    import jax.numpy as jnp

    def _L0_tok_ref(input, weight):
        import jax, jax.numpy as jnp
        import numpy as np
        NUM_EMBEDDINGS = 32000
        EMBEDDING_DIM = 256
        EPS = 1e-05
        scale = 1.0 / jnp.maximum(jnp.mean(jnp.abs(weight)), EPS)
        quantized_weight = jnp.clip(jnp.round(weight * scale), -1.0, 1.0) / scale
        return quantized_weight[input]

    def _L0_attn_ref(x, Wq, bq, Wk, bk, Wv, bv, Wo, bo, gamma, beta):
        import jax, jax.numpy as jnp
        import numpy as np
        import math
        H = 16
        N_EMBD = 256
        EPS = 1e-05
        B, T, _ = x.shape
        Dh = N_EMBD // H

        def split_heads(y):
            return y.reshape(B, T, H, Dh).transpose(0, 2, 1, 3)
        q = split_heads(x @ Wq + bq)
        k = split_heads(x @ Wk + bk)
        v = split_heads(x @ Wv + bv)
        att = jnp.einsum('bhtd,bhsd->bhts', q, k) * (1.0 / math.sqrt(Dh))
        causal = jnp.tril(jnp.ones((T, T), dtype=bool))
        att = jnp.where(causal[None, None], att, -jnp.inf)
        att = jax.nn.softmax(att, axis=-1)
        o = jnp.einsum('bhts,bhsd->bhtd', att, v)
        o = o.transpose(0, 2, 1, 3).reshape(B, T, N_EMBD)
        y = o @ Wo + bo
        mu = jnp.mean(y, axis=-1, keepdims=True)
        var = jnp.var(y, axis=-1, keepdims=True)
        return (y - mu) * jax.lax.rsqrt(var + EPS) * gamma + beta

    def _L0_ffn_ref(x, gate_w, gate_b, w1, b1, w2, b2):
        import jax, jax.numpy as jnp
        import numpy as np
        D, H, O, E, TOPK = (256, 1024, 256, 8, 2)
        B, L = (2, 512)
        ROUTE_SCALE = 1.0
        Bb, Ll, Dd = x.shape
        N = Bb * Ll
        x_flat = x.reshape(N, Dd)
        logits = x_flat @ gate_w.T + gate_b
        probs = jax.nn.softmax(logits * ROUTE_SCALE, axis=-1)
        topk_vals, topk_idx = jax.lax.top_k(probs, TOPK)
        dense_gate = jnp.zeros((N, E), probs.dtype).at[jnp.arange(N)[:, None], topk_idx].set(topk_vals)
        h = jax.nn.relu(jnp.einsum('nd,edh->neh', x_flat, w1) + b1)
        y = jnp.einsum('neh,eho->neo', h, w2) + b2
        out_flat = jnp.einsum('ne,neo->no', dense_gate, y)
        return out_flat.reshape(Bb, Ll, O)

    def _L1_attn_ref(x, Wqkv, bqkv, Wout, bout, rel_pos_bias):
        import jax, jax.numpy as jnp
        import numpy as np
        D_MODEL = 256
        N_HEADS = 16
        HEAD_DIM = D_MODEL // N_HEADS
        MAX_LEN = 512
        BATCH = 2
        SEQ = 512
        B, S, _ = x.shape
        scale = HEAD_DIM ** (-0.5)
        qkv = x @ Wqkv + bqkv
        qkv = qkv.reshape(B, S, 3, N_HEADS, HEAD_DIM)
        qkv = jnp.transpose(qkv, (2, 0, 3, 1, 4))
        q, k, v = (qkv[0], qkv[1], qkv[2])
        scores = jnp.einsum('bhqd,bhkd->bhqk', q, k) * scale
        pos = jnp.arange(S)
        rel = jnp.clip(pos[:, None] - pos[None, :] + (MAX_LEN - 1), 0, 2 * MAX_LEN - 2)
        scores = scores + rel_pos_bias[rel][None, None]
        probs = jax.nn.softmax(scores, axis=-1)
        out = jnp.einsum('bhqk,bhkd->bhqd', probs, v)
        out = jnp.transpose(out, (0, 2, 1, 3)).reshape(B, S, D_MODEL)
        return out @ Wout + bout

    def _L1_ffn_ref(x, k0, k1, k2, s0, s1, s2):
        import jax, jax.numpy as jnp
        import numpy as np
        import math
        D_IN = 256
        FEATURES = (1024, 1024, 256)
        BATCH, SEQ = (8, 512)

        def _conn_dense(kernel_bool, x):
            w = jnp.where(kernel_bool, jnp.float32(1.0), jnp.float32(-1.0))
            return x @ w
        h = jnp.concatenate([x, -x], axis=-1)
        h = s0 * _conn_dense(k0, h)
        h = jax.nn.relu(h) * 2
        h = s1 * _conn_dense(k1, h)
        h = jax.nn.relu(h) * 2
        h = s2 * _conn_dense(k2, h)
        return h
    h = _L0_tok_ref(x, L0_tok_weight)
    h = h + _L0_attn_ref(_layernorm(h, axis=-1), L0_attn_Wq, L0_attn_bq, L0_attn_Wk, L0_attn_bk, L0_attn_Wv, L0_attn_bv, L0_attn_Wo, L0_attn_bo, L0_attn_gamma, L0_attn_beta)
    h = h + _L0_ffn_ref(_layernorm(h, axis=-1), L0_ffn_gate_w, L0_ffn_gate_b, L0_ffn_w1, L0_ffn_b1, L0_ffn_w2, L0_ffn_b2)
    h = h + _L1_attn_ref(_layernorm(h, axis=-1), L1_attn_Wqkv, L1_attn_bqkv, L1_attn_Wout, L1_attn_bout, L1_attn_rel_pos_bias)
    h = h + _L1_ffn_ref(_layernorm(h, axis=-1), L1_ffn_k0, L1_ffn_k1, L1_ffn_k2, L1_ffn_s0, L1_ffn_s1, L1_ffn_s2)
    return h

_drawn_inputs = setup_inputs


def setup_inputs(seed=0):
    import zlib

    import numpy as np

    out = dict(_drawn_inputs(seed))
    spreads = {'L0_attn_bq': (0.0, 0.8),
     'L0_attn_bk': (0.0, 2.0),
     'L0_attn_bv': (0.0, 0.1),
     'L0_attn_bo': (0.0, 0.1),
     'L0_attn_gamma': (1.0, 0.2),
     'L0_attn_beta': (0.0, 0.1),
     'L0_ffn_gate_b': (0.0, 0.8),
     'L0_ffn_b1': (0.0, 0.326),
     'L0_ffn_b2': (0.0, 0.1)}
    factors = {'L0_attn_Wq': 6.319,
     'L0_attn_Wk': 5.855,
     'L1_attn_bqkv': 3.291,
     'L1_attn_rel_pos_bias': 177.688}
    for name, (base, spread) in spreads.items():
        noise = np.random.default_rng([zlib.crc32(name.encode()), seed]).standard_normal(out[name].shape)
        drawn = base * np.exp(spread * noise) if base else spread * noise
        out[name] = jnp.asarray(drawn.astype(out[name].dtype))
    for name, factor in factors.items():
        out[name] = (out[name] * factor).astype(out[name].dtype)
    return out
```

```python
from contextlib import ExitStack

import concourse.bass as bass
from concourse import mybir

P = 128
SEQS, SEQ, D = 4, 512, 256
TOKENS = SEQS * SEQ
TILES = TOKENS // P
TPS = SEQ // P
DC = D // P
HEADS, HD = 16, 16
PAIRS = TPS // 2
EXPERTS, HIDDEN = 8, 1024
HC = HIDDEN // P
LN_EPS = 1e-5
PARTS = 3
Q_PARTS = (0, 1, 0, 1, 2, 0)
K_PARTS = (0, 0, 1, 1, 0, 2)
STACK = len(Q_PARTS) * HD
SPAN = SEQ + SEQ - P
BIG = 3.0e38
BANK = 512

ALU = mybir.AluOpType
ACT = mybir.ActivationFunctionType
AX = mybir.AxisListType
F32 = mybir.dt.float32
F32R = mybir.dt.float32r
BF16 = mybir.dt.bfloat16
FP16 = mybir.dt.float16
U32 = mybir.dt.uint32
U8 = mybir.dt.uint8

PRODUCTS = ((0, 0), (1, 0), (0, 1))


def row_on_all_partitions(v, n):
    return bass.AP(tensor=v.tensor, offset=v.offset, ap=[[0, P], [1, n]])


def count(n):
    return n + 1


class Stage:

    def __init__(self, nc, name):
        self.nc, self.name = nc, name
        self.ctx, self.sems, self.zero_sems = ExitStack(), [], []

    def __enter__(self):
        return self

    def __exit__(self, kind, value, trace):
        self.ctx.close()
        if kind is None:
            self.nc.clear_and_free_semaphores(self.sems + self.zero_sems)

    def begin(self):
        for s in self.sems:
            self.nc.gpsimd.sem_inc(s, 1)
        self.nc.all_engine_barrier()

    def sb(self, name, shape, dt):
        return self.ctx.enter_context(self.nc.sbuf_tensor(f"{self.name}_{name}", shape, dt))

    def ps(self, name, shape):
        bank = self.ctx.enter_context(self.nc.psum_tensor(f"{self.name}_ps_{name}", [P, BANK], F32))
        n = 1
        for k in shape[1:]:
            n *= k
        view = bank[0:shape[0], 0:n]
        if len(shape) == 2:
            return view
        names = "abcd"[:len(shape) - 1]
        return view.rearrange(f"p ({' '.join(names)}) -> p {' '.join(names)}", **dict(zip(names, shape[1:])))

    def sem(self, name):
        self.sems.append(self.nc.alloc_semaphore(name=f"{self.name}_{name}"))
        return self.sems[-1]

    def zero_sem(self, name):
        self.zero_sems.append(self.nc.alloc_semaphore(name=f"{self.name}_{name}"))
        return self.zero_sems[-1]


def embed_stage(nc, ids, table, resid):
    st = Stage(nc, "embed")
    rows, _ = table.shape
    per = rows * D // P
    SLOTS, PIECE = 4, 4000
    pieces = per // PIECE
    rounds = pieces // SLOTS
    with st:
        ring = st.sb("ring", [P, SLOTS, PIECE], F32)
        junk = st.sb("junk", [P, PIECE], BF16)
        idx = st.sb("idx", [P, TILES], U32)
        part = st.sb("part", [P, rounds, SLOTS], F32)
        total = st.sb("total", [P, 1], F32)
        ones = st.sb("ones", [P, P], F32)
        mean = st.sb("mean", [P, 1], F32)
        scale = st.sb("scale", [P, 1], F32)
        step = st.sb("step", [P, 1], F32)
        scaled = st.sb("scaled", [P, TPS, D], F32)
        below = st.sb("below", [P, TPS, D], F32)
        tern = st.sb("tern", [P, TPS, D], F32)
        pmean = st.ps("pmean", [P, 1])

        piece_in = [st.sem(f"piece_in{s}") for s in range(SLOTS)]
        ids_in = st.sem("ids_in")
        gathered = st.zero_sem("gathered")
        act_summed = st.sem("act_summed")
        dve_summed = st.sem("dve_summed")
        ones_set = st.sem("ones_set")
        total_ready = st.sem("total_ready")
        mean_ps = st.sem("mean_ps")
        chain = st.sem("chain")
        scaled_ready = st.sem("scaled_ready")
        tern_ready = st.sem("tern_ready")
        rows_done = st.sem("rows_done")

        pieces_of = table.rearrange("(p r) d -> p (r d)", p=P).rearrange(
            "p (i s n) -> p i s n", s=SLOTS, n=PIECE)
        chunk = lambda b: resid[:, b * TPS:(b + 1) * TPS, :]

        st.begin()
        with nc.Block() as block:
            @block.sync
            def _(sp):
                sp.dma_start(idx[:].bitcast(ids.dtype), ids.rearrange("b (t p) -> p (b t)", p=P),
                             ).then_inc(ids_in, 16)
                for s in range(SLOTS):
                    sp.dma_start(ring[:, s, :], pieces_of[:, 0, s, :]).then_inc(piece_in[s], 16)
                with sp.Fori(1, rounds) as i:
                    for s in range(SLOTS):
                        sp.wait_ge(act_summed if s % 2 == 0 else dve_summed, count(2 * i - 1 + s // 2))
                        sp.dma_start(ring[:, s, :], pieces_of[:, i, s, :]).then_inc(piece_in[s], 16)

            @block.gpsimd
            def _(pool):
                pool.memset(ones[:], 1.0).then_inc(ones_set, 1)
                pool.wait_ge(ids_in, count(16))
                for t in range(TILES):
                    pool.indirect_dma_start(out=resid[:, t, :], out_offset=None, in_=table,
                                            in_offset=bass.IndirectOffsetOnAxis(ap=idx[:, t:t + 1], axis=0)
                                            ).then_inc(gathered, 16)
                pool.wait_ge(gathered, 16 * TILES)

            @block.scalar
            def _(act):
                with act.Fori(0, rounds) as i:
                    for s in (0, 2):
                        act.wait_ge(piece_in[s], count(16 * i + 16))
                        if s == 2:
                            act.wait_ge(act_summed, count(2 * i + 1))
                        else:
                            act.wait_ge(act_summed, count(2 * i))
                        nc.scalar.activation(junk[:], ring[:, s, :], ACT.Abs,
                                             accum_out=part[:, i, s:s + 1]).then_inc(act_summed, 1)
                act.wait_ge(chain, count(4))
                act.wait_ge(gathered, 16 * TILES)
                for b in range(SEQS):
                    if b:
                        act.wait_ge(tern_ready, count(b))
                    nc.scalar.activation(scaled[:], chunk(b), ACT.Copy, scale=scale[:, 0:1]
                                         ).then_inc(scaled_ready, 1)
                    act.wait_ge(tern_ready, count(b + 1))
                    nc.scalar.activation(chunk(b), tern[:], ACT.Copy, scale=step[:, 0:1]
                                         ).then_inc(rows_done, 1)

            @block.vector
            def _(dve):
                with dve.Fori(0, rounds) as i:
                    for s in (1, 3):
                        dve.wait_ge(piece_in[s], count(16 * i + 16))
                        nc.vector.tensor_reduce(part[:, i, s:s + 1], ring[:, s, :], AX.X, ALU.add,
                                                apply_absolute_value=True).then_inc(dve_summed, 1)
                dve.wait_ge(dve_summed, count(2 * rounds))
                dve.wait_ge(act_summed, count(2 * rounds))
                nc.vector.tensor_reduce(total[:], part[:], AX.XY, ALU.add).then_inc(total_ready, 1)
                dve.wait_ge(mean_ps, count(1))
                nc.vector.tensor_scalar(mean[:], pmean[:], 1.0 / (rows * D), None, ALU.mult
                                        ).then_inc(chain, 1)
                dve.wait_ge(chain, count(1))
                nc.vector.tensor_scalar(total[:], mean[:], LN_EPS, None, ALU.max).then_inc(chain, 1)
                dve.wait_ge(chain, count(2))
                nc.vector.reciprocal(scale[:], total[:]).then_inc(chain, 1)
                dve.wait_ge(chain, count(3))
                nc.vector.reciprocal(step[:], scale[:]).then_inc(chain, 1)
                for b in range(SEQS):
                    dve.wait_ge(scaled_ready, count(b + 1))
                    nc.vector.tensor_scalar(below[:], scaled[:], -0.5, None, ALU.is_lt
                                            ).then_inc(chain, 1)
                    dve.wait_ge(chain, count(5 + b))
                    if b:
                        dve.wait_ge(rows_done, count(b))
                    nc.vector.scalar_tensor_tensor(out=tern[:], in0=scaled[:], scalar=0.5, in1=below[:],
                                                   op0=ALU.is_gt, op1=ALU.subtract
                                                   ).then_inc(tern_ready, 1)

            @block.tensor
            def _(pe):
                pe.wait_ge(ones_set, count(1))
                pe.wait_ge(total_ready, count(1))
                nc.tensor.matmul(pmean[:], ones[:], total[:], start=True, stop=True).then_inc(mean_ps, 1)


class Norm:

    def __init__(self, st, dt):
        self.dt = dt
        self.minus_half = st.sb("minus_half", [P, 1], F32)
        self.stats = st.sb("stats", [P, TILES, 6], F32)
        self.mv = st.sb("mv", [P, TILES, 2], F32)
        self.var_eps = st.sb("var_eps", [P, TILES], F32)
        self.rstd = st.sb("rstd", [P, TILES], F32)
        self.mean_seq = st.sb("mean_seq", [P, TPS], F32)
        self.stats_ready = st.sem("stats_ready")
        self.mv_ready = st.sem("mv_ready")
        self.pool_step = st.sem("pool_step")
        self.rstd_ready = st.sem("rstd_ready")

    def statistics(self, nc, dve, x):
        for t in range(TILES):
            nc.vector.bn_stats(self.stats[:, t, :], x[:, t, :]).then_inc(self.stats_ready, 1)
        for t in range(TILES):
            dve.wait_ge(self.stats_ready, count(t + 1))
            nc.vector.bn_aggr(self.mv[:, t, :], self.stats[:, t, :]).then_inc(self.mv_ready, 1)

    def inverse_deviation(self, nc, pool):
        nc.gpsimd.memset(self.minus_half[:], -0.5).then_inc(self.pool_step, 1)
        pool.wait_ge(self.mv_ready, count(TILES))
        nc.gpsimd.tensor_scalar(self.var_eps[:], self.mv[:, :, 1], LN_EPS, None, ALU.add
                                ).then_inc(self.pool_step, 1)
        pool.wait_ge(self.pool_step, count(2))
        nc.gpsimd.tensor_tensor(self.rstd[:], self.var_eps[:],
                                self.minus_half[:, 0:1].to_broadcast([P, TILES]), ALU.pow
                                ).then_inc(self.rstd_ready, 1)


class Turn:

    def __init__(self, st, dt):
        self.dt = dt
        self.ps = [st.ps(f"turned{c}", [P, SEQ]) for c in range(DC)]
        self.hi = st.sb("x_hi", [P, DC, SEQ], dt)
        self.lo = st.sb("x_lo", [P, DC, SEQ], dt)
        self.row_ready = st.sem("row_ready")
        self.turned = st.sem("x_turned")
        self.hi_ready = st.sem("x_hi_ready")
        self.lo_ready = st.sem("x_lo_ready")

    def plain(self, x):
        return x.bitcast(F32) if self.dt == F32R else x

    def on_tensor(self, nc, pe, b, rows, ident):
        pe.wait_ge(self.lo_ready, count(DC * b))
        for j in range(TPS):
            pe.wait_ge(self.row_ready, count(TPS * b + j + 1))
            for c in range(DC):
                last = nc.tensor.transpose(self.ps[c][:, j * P:(j + 1) * P],
                                           rows(j)[:, c * P:(c + 1) * P], ident[:])
        last.then_inc(self.turned, 1)

    def on_scalar(self, nc, act, b):
        act.wait_ge(self.turned, count(b + 1))
        for c in range(DC):
            nc.scalar.activation(self.hi[:, c, :], self.ps[c][:], ACT.Copy).then_inc(self.hi_ready, 1)

    def on_vector(self, nc, dve, b):
        for c in range(DC):
            dve.wait_ge(self.hi_ready, count(DC * b + c + 1))
            nc.vector.tensor_tensor(self.lo[:, c, :], self.ps[c][:], self.plain(self.hi[:, c, :]),
                                    ALU.subtract).then_inc(self.lo_ready, 1)


def qkv_stage(nc, name, ident, resid, w_parts, b_qk, b_v, qk_scratch, v_parts):
    st = Stage(nc, name)
    QK = 2 * D // P
    with st:
        norm, turn = Norm(st, F32R), Turn(st, F32R)
        wf = st.sb("wf", [P, DC, 3 * D], F32)
        w_hi = st.sb("w_hi", [P, DC, 3 * D], F32R)
        w_lo = st.sb("w_lo", [P, DC, 3 * D], F32R)
        bias = st.sb("bias", [P, QK], F32)
        bias_q = st.sb("bias_q", [P, QK], F32)
        bv = st.sb("bv", [P, D], F32)
        xn = st.sb("xn", [P, TPS, D], F32)
        full = st.sb("full", [P, 2, SEQ], F32)
        rest = st.sb("rest", [P, 2, SEQ], F32)
        qk_parts = st.sb("qk_parts", [P, 2, PARTS, SEQ], BF16)
        v_full = st.sb("v_full", [P, 2, D], F32)
        v_rest = st.sb("v_rest", [P, 2, D], F32)
        ps_qk = [st.ps(f"qk{i}", [P, SEQ]) for i in range(2)]
        ps_v = [st.ps(f"v{i}", [P, D]) for i in range(2)]

        loaded = st.sem("loaded")
        bias_scaled = st.sem("bias_scaled")
        w_hi_ready, w_lo_ready = st.sem("w_hi_ready"), st.sem("w_lo_ready")
        qk_ps, v_ps = st.sem("qk_ps"), st.sem("v_ps")
        qk_full, qk_hi, qk_rest, qk_mid, qk_lo = (
            st.sem(f"qk_{s}") for s in ("full", "hi", "rest", "mid", "lo"))
        v_fulls, v_hi, v_rests, v_mid, v_lo = (
            st.sem(f"v_{s}") for s in ("fulls", "hi", "rests", "mid", "lo"))
        stored = [st.sem(f"stored{i}") for i in range(2)]
        n_loads = len(w_parts) + len(b_qk) + 1

        out_of = qk_scratch.rearrange("b s (m p) t -> b m p s t", p=P)

        st.begin()
        with nc.Block() as block:
            @block.sync
            def _(sp):
                at = 0
                for w in w_parts:
                    n = w.shape[1]
                    sp.dma_start(wf[:, :, at:at + n], w.rearrange("(c p) n -> p c n", p=P)).then_inc(loaded, 16)
                    at += n
                at = 0
                for v in b_qk:
                    m = v.shape[0] // P
                    sp.dma_start(bias[:, at:at + m], v.rearrange("(m p) -> p m", p=P)).then_inc(loaded, 16)
                    at += m
                sp.dma_start(bv[:], row_on_all_partitions(b_v, D)).then_inc(loaded, 16)
                with sp.Fori(0, SEQS) as b:
                    for m in range(QK):
                        sp.wait_ge(qk_lo, count(QK * b + m + 1))
                        sp.dma_start(out_of[b, m], qk_parts[:, m % 2]).then_inc(stored[m % 2], 16)
                for s in stored:
                    sp.wait_ge(s, count(16 * SEQS * QK // 2))

            @block.gpsimd
            def _(pool):
                norm.inverse_deviation(nc, pool)

            @block.tensor
            def _(pe):
                pe.wait_ge(w_lo_ready, count(1))
                with pe.Fori(0, SEQS) as b:
                    turn.on_tensor(nc, pe, b, lambda j: xn[:, j, :], ident)
                    pe.wait_ge(turn.lo_ready, count(DC * b + DC))
                    for m in range(QK):
                        pe.wait_ge(qk_full, count(QK * b + m - 1)) if m >= 2 else pe.wait_ge(qk_full, count(QK * b))
                        n = 0
                        for pw, px in PRODUCTS:
                            for c in range(DC):
                                w = (w_hi, w_lo)[pw][:, c, m * P:(m + 1) * P]
                                last = nc.tensor.matmul(ps_qk[m % 2][:], w, (turn.hi, turn.lo)[px][:, c, :],
                                                        start=n == 0, stop=n == 3 * DC - 1)
                                n += 1
                        last.then_inc(qk_ps, 1)
                    for j in range(TPS):
                        pe.wait_ge(v_fulls, count(TPS * b + j - 1)) if j >= 2 else pe.wait_ge(v_fulls, count(TPS * b))
                        n = 0
                        for pw, px in PRODUCTS:
                            for c in range(DC):
                                x = (turn.hi, turn.lo)[px][:, c, j * P:(j + 1) * P]
                                last = nc.tensor.matmul(ps_v[j % 2][:], x, (w_hi, w_lo)[pw][:, c, 2 * D:3 * D],
                                                        start=n == 0, stop=n == 3 * DC - 1)
                                n += 1
                        last.then_inc(v_ps, 1)

            @block.scalar
            def _(act):
                act.wait_ge(loaded, count(16 * n_loads))
                nc.scalar.activation(w_hi[:], wf[:], ACT.Copy).then_inc(w_hi_ready, 1)
                nc.scalar.activation(bias_q[:, 0:DC], bias[:, 0:DC], ACT.Copy, scale=-0.25).then_inc(bias_scaled, 1)
                nc.scalar.activation(bias_q[:, DC:QK], bias[:, DC:QK], ACT.Copy).then_inc(bias_scaled, 1)
                act.wait_ge(bias_scaled, count(2))
                with act.Fori(0, SEQS) as b:
                    act.wait_ge(v_ps, count(TPS * b))
                    turn.on_scalar(nc, act, b)
                    for m in range(QK):
                        k = m % 2
                        act.wait_ge(qk_ps, count(QK * b + m + 1))
                        act.wait_ge(qk_rest, count(QK * b + m - 1)) if m >= 2 else act.wait_ge(qk_rest, count(QK * b))
                        nc.scalar.activation(full[:, k, :], ps_qk[k][:], ACT.Identity, bias=bias_q[:, m:m + 1],
                                             scale=-0.25 if m < DC else 1.0).then_inc(qk_full, 1)
                        act.wait_ge(qk_full, count(QK * b + m + 1))
                        act.wait_ge(stored[k], count(16 * (2 * b + m // 2)))
                        nc.scalar.activation(qk_parts[:, k, 0, :], full[:, k, :], ACT.Copy).then_inc(qk_hi, 1)
                        act.wait_ge(qk_rest, count(QK * b + m + 1))
                        nc.scalar.activation(qk_parts[:, k, 1, :], rest[:, k, :], ACT.Copy).then_inc(qk_mid, 1)
                    for j in range(TPS):
                        k = j % 2
                        heads = lambda x: x.rearrange("p (h d) -> p h d", d=HD)
                        act.wait_ge(v_fulls, count(TPS * b + j + 1))
                        nc.scalar.activation(v_parts[:, TPS * b + j, :, 0, :], heads(v_full[:, k, :]), ACT.Copy
                                             ).then_inc(v_hi, 1)
                        act.wait_ge(v_rests, count(TPS * b + j + 1))
                        nc.scalar.activation(v_parts[:, TPS * b + j, :, 1, :], heads(v_rest[:, k, :]), ACT.Copy
                                             ).then_inc(v_mid, 1)

            @block.vector
            def _(dve):
                norm.statistics(nc, dve, resid)
                dve.wait_ge(w_hi_ready, count(1))
                nc.vector.tensor_tensor(w_lo[:], wf[:], w_hi[:].bitcast(F32), ALU.subtract).then_inc(w_lo_ready, 1)
                dve.wait_ge(norm.rstd_ready, count(1))
                with dve.Fori(0, SEQS) as b:
                    dve.wait_ge(turn.turned, count(b))
                    for j in range(TPS):
                        nc.vector.tensor_scalar(xn[:, j, :], resid[:, TPS * b + j, :],
                                                norm.mv[:, bass.ds(TPS * b + j, 1), 0], norm.rstd[:, bass.ds(TPS * b + j, 1)],
                                                ALU.subtract, ALU.mult).then_inc(turn.row_ready, 1)
                    dve.wait_ge(v_ps, count(TPS * b))
                    turn.on_vector(nc, dve, b)
                    for m in range(QK):
                        k = m % 2
                        dve.wait_ge(qk_hi, count(QK * b + m + 1))
                        dve.wait_ge(qk_lo, count(QK * b + m - 1)) if m >= 2 else dve.wait_ge(qk_lo, count(QK * b))
                        nc.vector.tensor_tensor(rest[:, k, :], full[:, k, :], qk_parts[:, k, 0, :], ALU.subtract
                                                ).then_inc(qk_rest, 1)
                        dve.wait_ge(qk_mid, count(QK * b + m + 1))
                        nc.vector.tensor_tensor(qk_parts[:, k, 2, :], rest[:, k, :], qk_parts[:, k, 1, :],
                                                ALU.subtract).then_inc(qk_lo, 1)
                    for j in range(TPS):
                        k = j % 2
                        heads = lambda x: x.rearrange("p (h d) -> p h d", d=HD)
                        dve.wait_ge(v_ps, count(TPS * b + j + 1))
                        dve.wait_ge(v_lo, count(TPS * b + j - 1)) if j >= 2 else dve.wait_ge(v_lo, count(TPS * b))
                        nc.vector.tensor_tensor(v_full[:, k, :], ps_v[k][:], bv[:], ALU.add).then_inc(v_fulls, 1)
                        dve.wait_ge(v_hi, count(TPS * b + j + 1))
                        nc.vector.tensor_tensor(heads(v_rest[:, k, :]), heads(v_full[:, k, :]),
                                                v_parts[:, TPS * b + j, :, 0, :], ALU.subtract).then_inc(v_rests, 1)
                        dve.wait_ge(v_mid, count(TPS * b + j + 1))
                        nc.vector.tensor_tensor(v_parts[:, TPS * b + j, :, 2, :], heads(v_rest[:, k, :]),
                                                v_parts[:, TPS * b + j, :, 1, :], ALU.subtract).then_inc(v_lo, 1)


def attention_stage(nc, name, ident, neg_bias, causal, qk_scratch, v_parts, heads_out):
    st = Stage(nc, name)
    width = [(i + 1) * P if causal else SEQ for i in range(TPS)]
    with st:
        q = [st.sb(f"q{s}", [STACK, HEADS, SEQ], BF16) for s in range(2)]
        k = [st.sb(f"k{s}", [STACK, HEADS, SEQ], BF16) for s in range(2)]
        neg = st.sb("neg", [P, 2, SEQ], F32)
        row_min = st.sb("row_min", [P, TPS], F32)
        row_sum = st.sb("row_sum", [P, TPS], F32)
        inv_sum = st.sb("inv_sum", [P, TPS], F32)
        prob = st.sb("prob", [P, 2, SEQ], F32)
        pt_hi = st.sb("pt_hi", [P, 2, SEQ], FP16)
        pt_lo = st.sb("pt_lo", [P, 2, SEQ], FP16)
        mixed = st.sb("mixed", [P, 2, HD], F32)
        settle = st.sb("settle", [P, 1], F32)
        ps_s = [st.ps(f"s{i}", [P, SEQ]) for i in range(TPS)]
        ps_t = [st.ps(f"t{i}", [P, SEQ]) for i in range(2)]
        ps_o = [st.ps(f"o{i}", [P, 2, PARTS * HD]) for i in range(PAIRS)]

        qk_in = [st.sem(f"qk_in{s}") for s in range(2)]
        scored = st.sem("scored")
        lowered = st.sem("lowered")
        exped = st.sem("exped")
        turned = st.sem("turned")
        hi_ready, lo_ready = st.sem("hi_ready"), st.sem("lo_ready")
        mixed_ps = [st.sem(f"mixed_ps{i}") for i in range(2)]
        inverted, summed = st.sem("inverted"), st.sem("summed")
        normed = [st.sem(f"normed{p}") for p in range(PAIRS)]
        LOADS = 2 * len(Q_PARTS)

        st.begin()
        with nc.Block() as block:
            @block.sync
            def _(sp):
                def load(b, s):
                    for r, (pq, pk) in enumerate(zip(Q_PARTS, K_PARTS)):
                        rows = slice(r * HD, (r + 1) * HD)
                        sp.dma_start(q[s][rows], qk_scratch[b, pq, 0:D].rearrange("(h d) t -> d h t", d=HD)
                                     ).then_inc(qk_in[s], 16)
                        sp.dma_start(k[s][rows], qk_scratch[b, pk, D:2 * D].rearrange("(h d) t -> d h t", d=HD)
                                     ).then_inc(qk_in[s], 16)
                for s in range(2):
                    load(s, s)
                with sp.Fori(1, SEQS // 2) as bb:
                    for s in range(2):
                        sp.wait_ge(scored, count(TPS * HEADS * (2 * bb + s - 1)))
                        load(2 * bb + s, s)

            @block.tensor
            def _(pe):
                def score(s, h, i):
                    nc.tensor.matmul(ps_s[i][:, 0:width[i]], q[s][:, h, i * P:(i + 1) * P],
                                     k[s][:, h, 0:width[i]], start=True, stop=True).then_inc(scored, 1)

                def turn(n, i):
                    pe.wait_ge(exped, count(n + 1))
                    for kt in range(width[i] // P):
                        last = nc.tensor.transpose(ps_t[i % 2][:, kt * P:(kt + 1) * P],
                                                   prob[:, i % 2, kt * P:(kt + 1) * P], ident[:])
                    last.then_inc(turned, 1)

                def mix(b, g, h, i):
                    if i % 2 == 0:
                        pe.wait_ge(normed[i // 2], count(g))
                    pe.wait_ge(lo_ready, count(TPS * g + i + 1))
                    tiles = width[i] // P
                    for kt in range(tiles):
                        for x, part in enumerate((pt_hi, pt_lo)):
                            last = nc.tensor.matmul(
                                ps_o[i // 2][:, i % 2], part[:, i % 2, kt * P:(kt + 1) * P],
                                v_parts[:, TPS * b + kt, h].rearrange("p s d -> p (s d)"),
                                start=kt == 0 and x == 0, stop=kt == tiles - 1 and x == 1)
                    last.then_inc(mixed_ps[i % 2], 1)

                with pe.Fori(0, SEQS // 2) as bb:
                    for s in range(2):
                        b = 2 * bb + s
                        g0 = HEADS * b
                        pe.wait_ge(qk_in[s], count(16 * LOADS * (bb + 1)))
                        pe.wait_ge(lowered, count(TPS * g0))
                        for i in range(TPS):
                            score(s, 0, i)
                        pe.wait_ge(lo_ready, count(TPS * g0))
                        turn(TPS * g0, 0)
                        with pe.Fori(0, HEADS - 1) as h:
                            g = g0 + h
                            for i in range(TPS):
                                n = TPS * g + i
                                pe.wait_ge(lo_ready, count(n))
                                turn(n + 1, (i + 1) % TPS)
                                pe.wait_ge(lowered, count(n + 1))
                                score(s, h + 1, i)
                                mix(b, g, h, i)
                        g = g0 + HEADS - 1
                        for i in range(TPS):
                            n = TPS * g + i
                            if i + 1 < TPS:
                                pe.wait_ge(lo_ready, count(n))
                                turn(n + 1, i + 1)
                            mix(b, g, HEADS - 1, i)

            @block.scalar
            def _(act):
                def exponential(n, i):
                    act.wait_ge(lowered, count(n + 1))
                    nc.scalar.activation(prob[:, i % 2, 0:width[i]], neg[:, i % 2, 0:width[i]], ACT.Exp,
                                         bias=row_min[:, i:i + 1], scale=-1.0,
                                         accum_out=row_sum[:, i:i + 1]).then_inc(exped, 1)

                def high(g, i):
                    act.wait_ge(turned, count(TPS * g + i + 1))
                    act.wait_ge(mixed_ps[i % 2], count(2 * g + i // 2))
                    nc.scalar.activation(pt_hi[:, i % 2, 0:width[i]], ps_t[i % 2][:, 0:width[i]], ACT.Copy
                                         ).then_inc(hi_ready, 1)

                def step(g, i, more):
                    n = TPS * g + i
                    if more:
                        act.wait_ge(turned, count(n))
                        if i == TPS - 1:
                            act.wait_ge(normed[0], count(g + 1))
                        if i == 1:
                            act.wait_ge(normed[1], count(g))
                        exponential(n + 1, (i + 1) % TPS)
                    high(g, i)

                with act.Fori(0, SEQS) as b:
                    g0 = HEADS * b
                    act.wait_ge(turned, count(TPS * g0))
                    act.wait_ge(normed[0], count(g0))
                    exponential(TPS * g0, 0)
                    with act.Fori(0, HEADS - 1) as h:
                        for i in range(TPS):
                            step(g0 + h, i, True)
                    for i in range(TPS):
                        step(g0 + HEADS - 1, i, i + 1 < TPS)

            @block.vector
            def _(dve):
                def lower(i):
                    lo = SEQ - P - i * P
                    nc.vector.tensor_tensor_reduce(
                        neg[:, i % 2, 0:width[i]], ps_s[i][:, 0:width[i]], neg_bias[:, lo:lo + width[i]],
                        1.0, BIG, ALU.add, ALU.min, row_min[:, i:i + 1]).then_inc(lowered, 1)

                def low(g, i):
                    dve.wait_ge(hi_ready, count(TPS * g + i + 1))
                    dve.wait_ge(mixed_ps[i % 2], count(2 * g + i // 2))
                    nc.vector.tensor_tensor(pt_lo[:, i % 2, 0:width[i]], ps_t[i % 2][:, 0:width[i]],
                                            pt_hi[:, i % 2, 0:width[i]], ALU.subtract).then_inc(lo_ready, 1)

                def finish(b, g, h, p):
                    two = slice(2 * p, 2 * p + 2)
                    nc.vector.reciprocal(inv_sum[:, two], row_sum[:, two]).then_inc(inverted, 1)
                    dve.wait_ge(mixed_ps[1], count(2 * g + p + 1))
                    nc.vector.tensor_reduce(mixed[:], ps_o[p][:].rearrange("p i (s d) -> p i d s", d=HD),
                                            AX.X, ALU.add).then_inc(summed, 1)
                    dve.wait_ge(summed, count(2 * g + p + 1))
                    dve.wait_ge(inverted, count(2 * g + p + 1))
                    nc.vector.tensor_tensor(heads_out[:, bass.ds(TPS * b + 2 * p, 2), bass.ds(h * HD, HD)], mixed[:],
                                            inv_sum[:, two].unsqueeze(2).to_broadcast([P, 2, HD]), ALU.mult
                                            ).then_inc(normed[p], 1)

                def step(b, g, h, i, more):
                    n = TPS * g + i
                    if more:
                        dve.wait_ge(exped, count(n + 1))
                        dve.wait_ge(scored, count(n + 3))
                    low(g, i)
                    if more:
                        lower((i + 2) % TPS)
                    if i % 2 == 1:
                        finish(b, g, h, i // 2)

                with dve.Fori(0, SEQS) as b:
                    g0 = HEADS * b
                    dve.wait_ge(exped, count(TPS * g0))
                    dve.wait_ge(scored, count(TPS * g0 + 2))
                    nc.vector.memset(settle[:], 0.0)
                    for i in range(2):
                        lower(i)
                    with dve.Fori(0, HEADS - 1) as h:
                        for i in range(TPS):
                            step(b, g0 + h, h, i, True)
                    for i in range(TPS):
                        step(b, g0 + HEADS - 1, HEADS - 1, i, i < 2)


def rows_out_stage(nc, name, ident, heads_out, w, bias, norm_after, gamma, beta, resid):
    st = Stage(nc, name)
    with st:
        turn = Turn(st, F32R)
        wf = st.sb("wf", [P, DC, D], F32)
        w_hi = st.sb("w_hi", [P, DC, D], F32R)
        w_lo = st.sb("w_lo", [P, DC, D], F32R)
        rows_in = st.sb("rows_in", [P, TPS, D], F32)
        rows = {n: st.sb(n, [P, D], F32) for n in ("bias", "gamma", "beta")}
        y = st.sb("y", [P, TILES, D], F32)
        ps_y = [st.ps(f"y{i}", [P, D]) for i in range(2)]
        norm = Norm(st, F32R) if norm_after else None
        loaded = st.sem("loaded")
        w_hi_ready, w_lo_ready = st.sem("w_hi_ready"), st.sem("w_lo_ready")
        y_ps, y_ready = st.sem("y_ps"), st.sem("y_ready")
        normed, scaled, added, moved = st.sem("normed"), st.sem("scaled"), st.sem("added"), st.sem("moved")
        vectors = [("bias", bias)] + ([("gamma", gamma), ("beta", beta)] if norm_after else [])

        st.begin()
        with nc.Block() as block:
            @block.sync
            def _(sp):
                sp.dma_start(wf[:], w.rearrange("(c p) n -> p c n", p=P)).then_inc(loaded, 16)
                for n, v in vectors:
                    sp.dma_start(rows[n][:], row_on_all_partitions(v, D)).then_inc(loaded, 16)

            @block.gpsimd
            def _(pool):
                with pool.Fori(0, SEQS) as b:
                    pool.wait_ge(turn.turned, count(b))
                    for j in range(TPS):
                        nc.gpsimd.tensor_copy(rows_in[:, j, :], heads_out[:, TPS * b + j, :]
                                              ).then_inc(turn.row_ready, 1)
                if norm_after:
                    norm.inverse_deviation(nc, pool)

            @block.tensor
            def _(pe):
                pe.wait_ge(w_lo_ready, count(1))
                with pe.Fori(0, SEQS) as b:
                    turn.on_tensor(nc, pe, b, lambda j: rows_in[:, j, :], ident)
                    pe.wait_ge(turn.lo_ready, count(DC * b + DC))
                    for j in range(TPS):
                        pe.wait_ge(y_ready, count(TPS * b + max(j - 1, 0)))
                        n = 0
                        for pw, px in PRODUCTS:
                            for c in range(DC):
                                x = (turn.hi, turn.lo)[px][:, c, j * P:(j + 1) * P]
                                last = nc.tensor.matmul(ps_y[j % 2][:], x, (w_hi, w_lo)[pw][:, c, :],
                                                        start=n == 0, stop=n == 3 * DC - 1)
                                n += 1
                        last.then_inc(y_ps, 1)

            @block.scalar
            def _(act):
                act.wait_ge(loaded, count(16 * (1 + len(vectors))))
                nc.scalar.activation(w_hi[:], wf[:], ACT.Copy).then_inc(w_hi_ready, 1)
                with act.Fori(0, SEQS) as b:
                    act.wait_ge(y_ps, count(TPS * b))
                    turn.on_scalar(nc, act, b)

            @block.vector
            def _(dve):
                dve.wait_ge(w_hi_ready, count(1))
                nc.vector.tensor_tensor(w_lo[:], wf[:], w_hi[:].bitcast(F32), ALU.subtract).then_inc(w_lo_ready, 1)
                with dve.Fori(0, SEQS) as b:
                    dve.wait_ge(y_ps, count(TPS * b))
                    turn.on_vector(nc, dve, b)
                    for j in range(TPS):
                        t = TPS * b + j
                        dve.wait_ge(y_ps, count(t + 1))
                        nc.vector.tensor_tensor(y[:, t, :], ps_y[j % 2][:], rows["bias"][:], ALU.add
                                                ).then_inc(y_ready, 1)
                dve.wait_ge(y_ready, count(TILES))
                if norm_after:
                    norm.statistics(nc, dve, y)
                    dve.wait_ge(norm.rstd_ready, count(1))
                    for t in range(TILES):
                        nc.vector.tensor_scalar(y[:, t, :], y[:, t, :], norm.mv[:, t, 0:1], norm.rstd[:, t:t + 1],
                                                ALU.subtract, ALU.mult).then_inc(normed, 1)
                    dve.wait_ge(normed, count(TILES))
                    across = lambda n: rows[n][:].unsqueeze(1).to_broadcast([P, TILES, D])
                    nc.vector.tensor_tensor(y[:], y[:], across("gamma"), ALU.mult).then_inc(scaled, 1)
                    dve.wait_ge(scaled, count(1))
                    nc.vector.tensor_tensor(y[:], y[:], across("beta"), ALU.add).then_inc(moved, 1)
                    dve.wait_ge(moved, count(1))
                nc.vector.tensor_tensor(resid[:], resid[:], y[:], ALU.add).then_inc(added, 1)


def route_stage(nc, name, ident, resid, gate_w, gate_b, w1, w2, wts, slots, gates, tile_expert,
                x_slots, weights_in):
    st = Stage(nc, name)
    n_tiles = tile_expert.shape[1]
    E = EXPERTS
    with st:
        norm = Norm(st, F32)
        xn = st.sb("xn", [P, TILES, D], F32)
        x_t = st.sb("x_t", [P, DC, SEQ], F32)
        gw = st.sb("gw", [E, D], F32)
        gw_t = st.sb("gw_t", [P, DC, E], F32)
        gb = st.sb("gb", [P, E], F32)
        eid = st.sb("eid", [P, E], F32)
        tau = st.sb("tau", [P, n_tiles], F32)
        before = st.sb("before", [P, P], F32)
        ones = st.sb("ones", [P, P], F32)
        t8 = {n: st.sb(n, [P, TILES, E], F32) for n in (
            "logits", "shifted", "expd", "probs", "best", "wheref", "first", "second", "both", "tile_sum",
            "run_a", "run_b", "ahead", "based", "slot", "slot1", "slot2")}
        where = st.sb("where", [P, TILES, 8], U32)
        t1 = {n: st.sb(n, [P, TILES], F32) for n in ("gmax", "gsum", "ginv", "slot1f", "slot2f")}
        e1 = {n: st.sb(n, [P, E], F32) for n in ("tiles_f", "tiles", "start_a", "start_b", "start", "start_p")}
        tiles_i = st.sb("tiles_i", [P, E], mybir.dt.int32)
        passed = st.sb("passed", [P, n_tiles, E], F32)
        expert_f = st.sb("expert_f", [P, n_tiles], F32)
        ps_x = [st.ps(f"x{c}", [P, SEQ]) for c in range(DC)]
        ps_w = st.ps("w", [P, DC, E])
        ps_l = st.ps("l", [P, TILES, E])
        ps_r = st.ps("r", [P, TILES, E])
        ps_c = st.ps("c", [P, TILES, E])

        loaded, const, step = st.sem("loaded"), st.sem("const"), st.sem("step")
        gw_ps, gw_ready = st.sem("gw_ps"), st.sem("gw_ready")
        row_ready, turned, x_ready, logit_ps = (st.sem(x) for x in ("row_ready", "turned", "x_ready", "logit_ps"))
        shifted_ready, expd_ready = st.sem("shifted_ready"), st.sem("expd_ready")
        picked, counted, slots_ready = (st.sem(x) for x in ("picked", "counted", "slots_ready"))
        scattered = st.zero_sem("scattered")

        st.begin()
        with nc.Block() as block:
            @block.sync
            def _(sp):
                sp.dma_start(gw[:], gate_w).then_inc(loaded, 16)
                sp.dma_start(gb[:], row_on_all_partitions(gate_b, E)).then_inc(loaded, 16)
                for e in range(E):
                    sp.dma_start(wts[0][:, e], w1[e].rearrange("(c p) n -> p c n", p=P)).then_inc(weights_in, 16)
                    sp.dma_start(wts[1][:, e], w2[e].rearrange("(m p) n -> p m n", p=P)).then_inc(weights_in, 16)

            @block.gpsimd
            def _(pool):
                pool.memset(ones[:], 1.0).then_inc(const, 1)
                pool.wait_ge(const, count(1))
                pool.affine_select(out=before[:], in_=ones[:], compare_op=ALU.is_gt, fill=0.0, base=0,
                                   pattern=[[1, P]], channel_multiplier=-1).then_inc(const, 1)
                pool.iota(eid[:], pattern=[[1, E]], base=0, channel_multiplier=0,
                          allow_small_or_imprecise_dtypes=True).then_inc(const, 1)
                pool.iota(tau[:], pattern=[[1, n_tiles]], base=0, channel_multiplier=0,
                          allow_small_or_imprecise_dtypes=True).then_inc(const, 1)
                norm.inverse_deviation(nc, pool)
                pool.wait_ge(slots_ready, count(2))
                for t in range(TILES):
                    for which in range(2):
                        pool.indirect_dma_start(
                            out=x_slots, out_offset=bass.IndirectOffsetOnAxis(ap=slots[which][:, t:t + 1], axis=0),
                            in_=xn[:, t, :], in_offset=None).then_inc(scattered, 16)
                pool.wait_ge(scattered, 32 * TILES)

            @block.tensor
            def _(pe):
                pe.wait_ge(loaded, count(32))
                for c in range(DC):
                    last = nc.tensor.transpose(ps_w[:, c, :], gw[:, c * P:(c + 1) * P], ident[0:E, 0:E])
                last.then_inc(gw_ps, 1)
                pe.wait_ge(gw_ready, count(1))
                for b in range(SEQS):
                    pe.wait_ge(x_ready, count(DC * b))
                    pe.wait_ge(row_ready, count(TPS * b + TPS))
                    for j in range(TPS):
                        for c in range(DC):
                            last = nc.tensor.transpose(ps_x[c][:, j * P:(j + 1) * P],
                                                       xn[:, TPS * b + j, c * P:(c + 1) * P], ident[:])
                    last.then_inc(turned, 1)
                    pe.wait_ge(x_ready, count(DC * b + DC))
                    for j in range(TPS):
                        for c in range(DC):
                            last = nc.tensor.matmul(ps_l[:, TPS * b + j, :], x_t[:, c, j * P:(j + 1) * P],
                                                    gw_t[:, c, :], start=c == 0, stop=c == DC - 1)
                    last.then_inc(logit_ps, 1)
                pe.wait_ge(picked, count(1))
                pe.wait_ge(const, count(2))
                flat = lambda x: x.rearrange("p t e -> p (t e)")
                nc.tensor.matmul(flat(ps_r[:]), before[:], flat(t8["both"][:]), start=True, stop=True
                                 ).then_inc(counted, 1)
                nc.tensor.matmul(flat(ps_c[:]), ones[:], flat(t8["both"][:]), start=True, stop=True
                                 ).then_inc(counted, 1)

            @block.scalar
            def _(act):
                act.wait_ge(gw_ps, count(1))
                nc.scalar.activation(gw_t[:], ps_w[:], ACT.Copy).then_inc(gw_ready, 1)
                for b in range(SEQS):
                    act.wait_ge(turned, count(b + 1))
                    act.wait_ge(logit_ps, count(b))
                    for c in range(DC):
                        nc.scalar.activation(x_t[:, c, :], ps_x[c][:], ACT.Copy).then_inc(x_ready, 1)
                act.wait_ge(shifted_ready, count(1))
                nc.scalar.activation(t8["expd"][:], t8["shifted"][:], ACT.Exp).then_inc(expd_ready, 1)

            @block.vector
            def _(dve):
                v = nc.vector
                norm.statistics(nc, dve, resid)
                dve.wait_ge(norm.rstd_ready, count(1))
                for t in range(TILES):
                    v.tensor_scalar(xn[:, t, :], resid[:, t, :], norm.mv[:, t, 0:1], norm.rstd[:, t:t + 1],
                                    ALU.subtract, ALU.mult).then_inc(row_ready, 1)
                over_e = lambda x: x.unsqueeze(2).to_broadcast([P, TILES, E])
                over_t = lambda x: x.unsqueeze(1).to_broadcast([P, TILES, E])
                done = 0

                def chain(ins):
                    nonlocal done
                    done += 1
                    ins.then_inc(step, 1)
                    dve.wait_ge(step, count(done))

                dve.wait_ge(logit_ps, count(SEQS))
                dve.wait_ge(loaded, count(32))
                chain(v.tensor_tensor(t8["logits"][:], ps_l[:], over_t(gb[:]), ALU.add))
                chain(v.tensor_reduce(t1["gmax"][:], t8["logits"][:], AX.X, ALU.max))
                v.tensor_tensor(t8["shifted"][:], t8["logits"][:], over_e(t1["gmax"][:]), ALU.subtract
                                ).then_inc(shifted_ready, 1)
                dve.wait_ge(expd_ready, count(1))
                chain(v.tensor_reduce(t1["gsum"][:], t8["expd"][:], AX.X, ALU.add))
                chain(v.reciprocal(t1["ginv"][:], t1["gsum"][:]))
                chain(v.tensor_tensor(t8["probs"][:], t8["expd"][:], over_e(t1["ginv"][:]), ALU.mult))
                for t in range(TILES):
                    chain(v.max(out=t8["best"][:, t, :], in_=t8["probs"][:, t, :]))
                    chain(v.max_index(out=where[:, t, :], in_max=t8["best"][:, t, :], in_values=t8["probs"][:, t, :]))
                chain(v.tensor_copy(t8["wheref"][:], where[:]))
                chain(v.tensor_copy(gates[0][:], t8["best"][:, :, 0]))
                chain(v.tensor_copy(gates[1][:], t8["best"][:, :, 1]))
                dve.wait_ge(const, count(4))
                for k, n in enumerate(("first", "second")):
                    chain(v.tensor_tensor(t8[n][:], over_t(eid[:]), over_e(t8["wheref"][:, :, k]), ALU.is_equal))
                v.tensor_tensor(t8["both"][:], t8["first"][:], t8["second"][:], ALU.add).then_inc(picked, 1)
                dve.wait_ge(counted, count(2))
                chain(v.tensor_copy(t8["tile_sum"][:], ps_c[:]))
                src, dst = "tile_sum", "run_a"
                for d in (1, 2, 4, 8):
                    chain(v.tensor_copy(t8[dst][:, 0:d], t8[src][:, 0:d]))
                    chain(v.tensor_tensor(t8[dst][:, d:], t8[src][:, d:], t8[src][:, :TILES - d], ALU.add))
                    src, dst = dst, "run_b" if dst == "run_a" else "run_a"
                chain(v.tensor_tensor(t8["ahead"][:], t8[src][:], t8["tile_sum"][:], ALU.subtract))
                chain(v.tensor_scalar(e1["tiles_f"][:], t8[src][:, TILES - 1, :], 1.0 / P, 0.5 - 0.5 / P,
                                      ALU.mult, ALU.add))
                chain(v.tensor_copy(tiles_i[:], e1["tiles_f"][:]))
                chain(v.tensor_copy(e1["tiles"][:], tiles_i[:]))
                src, dst = "tiles", "start_a"
                for d in (1, 2, 4):
                    chain(v.tensor_copy(e1[dst][:, 0:d], e1[src][:, 0:d]))
                    chain(v.tensor_tensor(e1[dst][:, d:], e1[src][:, d:], e1[src][:, :E - d], ALU.add))
                    src, dst = dst, "start_b" if dst == "start_a" else "start_a"
                chain(v.tensor_tensor(e1["start"][:], e1[src][:], e1["tiles"][:], ALU.subtract))
                chain(v.tensor_scalar(e1["start_p"][:], e1["start"][:], float(P), None, ALU.mult))
                chain(v.tensor_tensor(t8["based"][:], t8["ahead"][:], over_t(e1["start_p"][:]), ALU.add))
                chain(v.tensor_tensor(t8["slot"][:], ps_r[:], t8["based"][:], ALU.add))
                for k, n in enumerate(("first", "second")):
                    chain(v.tensor_tensor(t8[f"slot{k + 1}"][:], t8[n][:], t8["slot"][:], ALU.mult))
                    chain(v.tensor_reduce(t1[f"slot{k + 1}f"][:], t8[f"slot{k + 1}"][:], AX.X, ALU.add))
                    v.tensor_copy(slots[k][:], t1[f"slot{k + 1}f"][:]).then_inc(slots_ready, 1)
                chain(v.tensor_tensor(passed[:], tau[:].unsqueeze(2).to_broadcast([P, n_tiles, E]),
                                      e1["start"][:].unsqueeze(1).to_broadcast([P, n_tiles, E]), ALU.is_ge))
                chain(v.tensor_reduce(expert_f[:], passed[:, :, 1:E], AX.X, ALU.add))
                chain(v.tensor_copy(tile_expert[:], expert_f[:]))


def experts_stage(nc, name, ident, wts, b1, b2, tile_expert, x_slots, y_slots, weights_in):
    st = Stage(nc, name)
    n_tiles = tile_expert.shape[1]
    HALF = 512
    with st:
        x_in = st.sb("x_in", [P, 2, D], F32)
        x_t = st.sb("x_t", [P, 2, DC, P], F32)
        h = st.sb("h", [P, 2, HIDDEN], F32)
        h_t = st.sb("h_t", [P, 2, HC, P], F32)
        y = st.sb("y", [P, 2, D], F32)
        b1c = st.sb("b1c", [P, EXPERTS * HC], F32)
        b2r = st.sb("b2r", [P, EXPERTS, D], F32)
        ps_x = st.ps("x", [P, DC, P])
        ps_h = [st.ps(f"h{i}", [P, HALF]) for i in range(2)]
        ps_t = [st.ps(f"t{i}", [P, HC // 2, P]) for i in range(2)]
        ps_y = st.ps("y", [P, D])
        loaded = st.sem("loaded")
        x_loaded = [st.sem(f"x_loaded{s}") for s in range(2)]
        x_ps, x_ready = st.sem("x_ps"), st.sem("x_ready")
        h_ps, h_ready = st.sem("h_ps"), st.sem("h_ready")
        t_ps, t_ready = st.sem("t_ps"), st.sem("t_ready")
        y_ps, y_ready = st.sem("y_ps"), st.sem("y_ready")
        y_stored = [st.sem(f"y_stored{s}") for s in range(2)]
        w1, w2 = wts
        rows = lambda dram, t: dram.rearrange("(t p) d -> t p d", p=P)[t]

        st.begin()
        with nc.Block() as block:
            @block.sync
            def _(sp):
                sp.dma_start(b1c[:], b1.rearrange("e (m p) -> p (e m)", p=P)).then_inc(loaded, 16)
                sp.dma_start(b2r[:], bass.AP(tensor=b2.tensor, offset=b2.offset, ap=[[0, P], [D, EXPERTS], [1, D]])
                             ).then_inc(loaded, 16)
                for s in range(2):
                    sp.dma_start(x_in[:, s, :], rows(x_slots, s)).then_inc(x_loaded[s], 16)

                def step(t, s, u, more):
                    if more:
                        sp.wait_ge(x_ps, count(t + 1))
                        sp.dma_start(x_in[:, s, :], rows(x_slots, t + 2)).then_inc(x_loaded[s], 16)
                    sp.wait_ge(y_ready, count(t + 1))
                    sp.dma_start(rows(y_slots, t), y[:, s, :]).then_inc(y_stored[s], 16)

                with sp.Fori(0, n_tiles // 2 - 1) as u:
                    for s in range(2):
                        step(2 * u + s, s, u, True)
                for t in range(n_tiles // 2 * 2 - 2, n_tiles):
                    step(t, t % 2, t // 2, t + 2 < n_tiles)
                sp.wait_ge(y_stored[0], count(16 * ((n_tiles + 1) // 2)))
                sp.wait_ge(y_stored[1], count(16 * (n_tiles // 2)))

            @block.tensor
            def _(pe):
                def expert(t):
                    return pe.value_load(tile_expert[0:1, bass.ds(t, 1)], min_val=0, max_val=EXPERTS - 1)

                def turn_x(t, s, u):
                    pe.wait_ge(x_loaded[s], count(16 * u + 16))
                    pe.wait_ge(x_ready, count(t))
                    for c in range(DC):
                        last = nc.tensor.transpose(ps_x[:, c, :], x_in[:, s, c * P:(c + 1) * P], ident[:])
                    last.then_inc(x_ps, 1)

                def hidden(t, s, e):
                    pe.wait_ge(x_ready, count(t + 1))
                    pe.wait_ge(h_ready, count(2 * t))
                    for half in range(2):
                        for c in range(DC):
                            last = nc.tensor.matmul(
                                ps_h[half][:], x_t[:, s, c, :],
                                w1[:, bass.ds(e, 1), c, half * HALF:(half + 1) * HALF].rearrange("p a n -> p (a n)"),
                                start=c == 0, stop=c == DC - 1)
                        last.then_inc(h_ps, 1)

                def turn_h(t, s):
                    pe.wait_ge(t_ready, count(t))
                    for half in range(2):
                        pe.wait_ge(h_ready, count(2 * t + half + 1))
                        for m in range(HC // 2):
                            at = (half * HC // 2 + m) * P
                            last = nc.tensor.transpose(ps_t[half][:, m, :], h[:, s, at:at + P], ident[:])
                        last.then_inc(t_ps, 1)

                def output(t, s, e):
                    pe.wait_ge(t_ready, count(t + 1))
                    pe.wait_ge(y_ready, count(t))
                    for m in range(HC):
                        last = nc.tensor.matmul(ps_y[:], h_t[:, s, m, :],
                                                w2[:, bass.ds(e, 1), m, :].rearrange("p a n -> p (a n)"),
                                                start=m == 0, stop=m == HC - 1)
                    last.then_inc(y_ps, 1)

                pe.wait_ge(weights_in, 32 * EXPERTS)
                turn_x(0, 0, 0)
                hidden(0, 0, expert(0))
                turn_h(0, 0)
                turn_x(1, 1, 0)
                with pe.Fori(0, (n_tiles - 2) // 2) as u:
                    for s in range(2):
                        t = 2 * u + s + 1
                        hidden(t, 1 - s, expert(t))
                        output(t - 1, s, expert(t - 1))
                        turn_h(t, 1 - s)
                        turn_x(t + 1, s, u + 1)
                for t in range((n_tiles - 2) // 2 * 2 + 1, n_tiles):
                    hidden(t, t % 2, expert(t))
                    output(t - 1, (t - 1) % 2, expert(t - 1))
                    turn_h(t, t % 2)
                    if t + 1 < n_tiles:
                        turn_x(t + 1, (t + 1) % 2, (t + 1) // 2)
                output(n_tiles - 1, (n_tiles - 1) % 2, expert(n_tiles - 1))

            @block.scalar
            def _(act):
                act.wait_ge(loaded, count(32))

                def step(t, s):
                    act.wait_ge(x_ps, count(t + 1))
                    act.wait_ge(h_ps, count(2 * t))
                    nc.scalar.activation(x_t[:, s, :, :], ps_x[:], ACT.Copy).then_inc(x_ready, 1)

                def relu(t, s, after_first=True):
                    e = act.value_load(tile_expert[0:1, bass.ds(t, 1)], min_val=0, max_val=EXPERTS - 1)
                    if after_first:
                        act.wait_ge(y_ps, count(t - 1))
                    for m in range(HC):
                        if m % (HC // 2) == 0:
                            act.wait_ge(t_ps, count(2 * t + m // (HC // 2) + 1))
                        last = nc.scalar.activation(h_t[:, s, m, :], ps_t[m // (HC // 2)][:, m % (HC // 2), :],
                                                    ACT.Relu, bias=b1c[:, bass.ds(e * HC + m, 1)])
                    last.then_inc(t_ready, 1)

                step(0, 0)
                step(1, 1)
                relu(0, 0, False)
                with act.Fori(0, (n_tiles - 2) // 2) as u:
                    for s in range(2):
                        t = 2 * u + s + 1
                        step(t + 1, s)
                        relu(t, 1 - s)
                for t in range((n_tiles - 2) // 2 * 2 + 1, n_tiles):
                    if t + 1 < n_tiles:
                        step(t + 1, (t + 1) % 2)
                    relu(t, t % 2)

            @block.vector
            def _(dve):
                dve.wait_ge(loaded, count(32))

                def rows_of_hidden(t, s):
                    for half in range(2):
                        dve.wait_ge(h_ps, count(2 * t + half + 1))
                        nc.vector.tensor_copy(h[:, s, half * HALF:(half + 1) * HALF], ps_h[half][:]
                                              ).then_inc(h_ready, 1)

                def rows_of_output(t, s, u):
                    e = dve.value_load(tile_expert[0:1, bass.ds(t, 1)], min_val=0, max_val=EXPERTS - 1)
                    dve.wait_ge(y_ps, count(t + 1))
                    dve.wait_ge(y_stored[s], count(16 * u))
                    nc.vector.tensor_tensor(y[:, s, :], ps_y[:],
                                            b2r[:, bass.ds(e, 1), :].rearrange("p a n -> p (a n)"), ALU.add
                                            ).then_inc(y_ready, 1)

                rows_of_hidden(0, 0)
                with dve.Fori(0, (n_tiles - 1) // 2) as u:
                    for s in range(2):
                        t = 2 * u + s + 1
                        dve.wait_ge(t_ps, count(2 * t - 2))
                        rows_of_hidden(t, 1 - s)
                        rows_of_output(t - 1, s, u)
                for t in range((n_tiles - 1) // 2 * 2 + 1, n_tiles):
                    dve.wait_ge(t_ps, count(2 * t - 2))
                    rows_of_hidden(t, t % 2)
                    rows_of_output(t - 1, (t - 1) % 2, (t - 1) // 2)
                rows_of_output(n_tiles - 1, (n_tiles - 1) % 2, (n_tiles - 1) // 2)


def combine_stage(nc, name, slots, gates, y_slots, resid):
    st = Stage(nc, name)
    with st:
        y = [st.sb(f"y{k}", [P, TILES, D], F32) for k in range(2)]
        gathered = [st.zero_sem(f"gathered{k}") for k in range(2)]
        added = st.sem("added")
        st.begin()
        with nc.Block() as block:
            @block.gpsimd
            def _(pool):
                for k in range(2):
                    for t in range(TILES):
                        pool.indirect_dma_start(
                            out=y[k][:, t, :], out_offset=None, in_=y_slots,
                            in_offset=bass.IndirectOffsetOnAxis(ap=slots[k][:, t:t + 1], axis=0)
                        ).then_inc(gathered[k], 16)

            @block.vector
            def _(dve):
                for k in range(2):
                    dve.wait_ge(gathered[k], 16 * TILES)
                    for t in range(TILES):
                        if k:
                            dve.wait_ge(added, count(t + 1))
                        nc.vector.scalar_tensor_tensor(out=resid[:, t, :], in0=y[k][:, t, :],
                                                       scalar=gates[k][:, t:t + 1], in1=resid[:, t, :],
                                                       op0=ALU.mult, op1=ALU.add).then_inc(added, 1)


def signs_stage(nc, name, ident, resid, k0, k1, k2, s0, s1, s2, out):
    st = Stage(nc, name)
    EIGHTH = 0.125
    with st:
        norm, turn = Norm(st, FP16), Turn(st, FP16)
        xn = st.sb("xn", [P, TPS, D], F32)
        bits0 = st.sb("bits0", [P, 2, DC, HIDDEN], U8)
        bits1 = st.sb("bits1", [P, HC, HIDDEN], U8)
        bits2 = st.sb("bits2", [P, HC, D], U8)
        diff = st.sb("diff", [P, DC, HIDDEN], FP16)
        wa = st.sb("wa", [P, DC, HIDDEN], FP16)
        wb0 = st.sb("wb0", [P, HC, HIDDEN], FP16)
        wb = st.sb("wb", [P, HC, HIDDEN], FP16)
        wc = st.sb("wc", [P, HC, D], FP16)
        s_all = st.sb("s_all", [P, 3], F32)
        pos, neg = st.sb("pos", [P, 3], F32), st.sb("neg", [P, 3], F32)
        sign, size = st.sb("sign", [P, 3], F32), st.sb("size", [P, 3], F32)
        size01, factor = st.sb("size01", [P, 1], F32), st.sb("factor", [P, 1], F32)
        factor64 = st.sb("factor64", [P, 1], F32)
        ga = [st.sb(f"ga_{x}", [P, HC, SEQ], FP16) for x in ("hi", "lo")]
        gb = [st.sb(f"gb_{x}", [P, HC, SEQ], FP16) for x in ("hi", "lo")]
        rows = st.sb("rows", [P, TPS, D], F32)
        ps = [st.ps(f"layer{i}", [P, SEQ]) for i in range(4)]
        ps_y = [st.ps(f"y{i}", [P, D]) for i in range(2)]

        loaded, step, wa_r, wb_r, wc_r, factor_r = (
            st.sem(x) for x in ("loaded", "step", "wa_r", "wb_r", "wc_r", "factor_r"))
        layer_ps, hi_ready, lo_ready = (st.sem(x) for x in ("layer_ps", "hi_ready", "lo_ready"))
        y_ps, y_ready, stored = st.sem("y_ps"), st.sem("y_ready"), st.sem("stored")
        out_t = out.rearrange("b (j p) d -> b p j d", p=P)

        st.begin()
        with nc.Block() as block:
            @block.sync
            def _(sp):
                sp.dma_start(bits0[:], k0.rearrange("(h c p) n -> p h c n", h=2, p=P)).then_inc(loaded, 16)
                sp.dma_start(bits1[:], k1.rearrange("(m p) n -> p m n", p=P)).then_inc(loaded, 16)
                sp.dma_start(bits2[:], k2.rearrange("(m p) n -> p m n", p=P)).then_inc(loaded, 16)
                for i, s in enumerate((s0, s1, s2)):
                    sp.dma_start(s_all[:, i:i + 1], bass.AP(tensor=s.tensor, offset=s.offset, ap=[[0, P], [1, 1]])
                                 ).then_inc(loaded, 16)
                with sp.Fori(0, SEQS) as b:
                    sp.wait_ge(y_ready, count(TPS * b + TPS))
                    sp.dma_start(out_t[b], rows[:]).then_inc(stored, 16)
                sp.wait_ge(stored, count(16 * SEQS))

            @block.gpsimd
            def _(pool):
                norm.inverse_deviation(nc, pool)

            @block.tensor
            def _(pe):
                def layer(b, which, src, w, chunks):
                    for m in range(HC):
                        n = 2 * HC * b + HC * which + m
                        if which == 0 and m < 4:
                            pe.wait_ge(lo_ready, count(2 * HC * b))
                        else:
                            pe.wait_ge(lo_ready, count(n - 3))
                        for k in range(chunks):
                            for x in range(2):
                                last = nc.tensor.matmul(ps[m % 4][:], w[:, k, m * P:(m + 1) * P], src[x][:, k, :],
                                                        start=k == 0 and x == 0, stop=k == chunks - 1 and x == 1)
                        last.then_inc(layer_ps, 1)

                pe.wait_ge(wc_r, count(1))
                with pe.Fori(0, SEQS) as b:
                    turn.on_tensor(nc, pe, b, lambda j: xn[:, j, :], ident)
                    pe.wait_ge(turn.lo_ready, count(DC * b + DC))
                    layer(b, 0, (turn.hi, turn.lo), wa, DC)
                    pe.wait_ge(lo_ready, count(2 * HC * b + HC))
                    layer(b, 1, ga, wb, HC)
                    pe.wait_ge(lo_ready, count(2 * HC * b + 2 * HC))
                    for j in range(TPS):
                        pe.wait_ge(y_ready, count(TPS * b + max(j - 1, 0)))
                        for k in range(HC):
                            for x in range(2):
                                last = nc.tensor.matmul(ps_y[j % 2][:], gb[x][:, k, j * P:(j + 1) * P], wc[:, k, :],
                                                        start=k == 0 and x == 0, stop=k == HC - 1 and x == 1)
                        last.then_inc(y_ps, 1)

            @block.scalar
            def _(act):
                with act.Fori(0, SEQS) as b:
                    act.wait_ge(layer_ps, count(2 * HC * b))
                    turn.on_scalar(nc, act, b)
                    for which, g in enumerate((ga, gb)):
                        if which:
                            act.wait_ge(y_ps, count(TPS * b))
                        else:
                            act.wait_ge(layer_ps, count(2 * HC * b))
                        for m in range(HC):
                            act.wait_ge(layer_ps, count(2 * HC * b + HC * which + m + 1))
                            nc.scalar.activation(g[0][:, m, :], ps[m % 4][:], ACT.Relu).then_inc(hi_ready, 1)

            @block.vector
            def _(dve):
                v = nc.vector
                norm.statistics(nc, dve, resid)
                dve.wait_ge(loaded, count(96))
                done = 0

                def chain(ins):
                    nonlocal done
                    done += 1
                    ins.then_inc(step, 1)
                    dve.wait_ge(step, count(done))

                chain(v.tensor_scalar(pos[:], s_all[:], 0.0, None, ALU.is_gt))
                chain(v.tensor_scalar(neg[:], s_all[:], 0.0, None, ALU.is_lt))
                chain(v.tensor_tensor(sign[:], pos[:], neg[:], ALU.subtract))
                chain(v.tensor_tensor(size[:], sign[:], s_all[:], ALU.mult))
                chain(v.tensor_tensor(size01[:], size[:, 0:1], size[:, 1:2], ALU.mult))
                chain(v.tensor_tensor(factor[:], size01[:], s_all[:, 2:3], ALU.mult))
                v.tensor_scalar(factor64[:], factor[:], 8.0 / EIGHTH, None, ALU.mult).then_inc(factor_r, 1)
                chain(v.tensor_tensor(diff[:], bits0[:, 0], bits0[:, 1], ALU.subtract))
                v.tensor_scalar(wa[:], diff[:], sign[:, 0:1], None, ALU.mult).then_inc(wa_r, 1)
                chain(v.tensor_scalar(wb0[:], bits1[:], 2 * EIGHTH, -EIGHTH, ALU.mult, ALU.add))
                v.tensor_scalar(wb[:], wb0[:], sign[:, 1:2], None, ALU.mult).then_inc(wb_r, 1)
                v.tensor_scalar(wc[:], bits2[:], 2.0, -1.0, ALU.mult, ALU.add).then_inc(wc_r, 1)
                dve.wait_ge(norm.rstd_ready, count(1))
                dve.wait_ge(factor_r, count(1))
                with dve.Fori(0, SEQS) as b:
                    dve.wait_ge(turn.turned, count(b))
                    for j in range(TPS):
                        v.tensor_scalar(xn[:, j, :], resid[:, TPS * b + j, :], norm.mv[:, bass.ds(TPS * b + j, 1), 0],
                                        norm.rstd[:, bass.ds(TPS * b + j, 1)], ALU.subtract, ALU.mult
                                        ).then_inc(turn.row_ready, 1)
                    dve.wait_ge(layer_ps, count(2 * HC * b))
                    turn.on_vector(nc, dve, b)
                    for which, g in enumerate((ga, gb)):
                        if which:
                            dve.wait_ge(y_ps, count(TPS * b))
                        for m in range(HC):
                            dve.wait_ge(hi_ready, count(2 * HC * b + HC * which + m + 1))
                            v.scalar_tensor_tensor(out=g[1][:, m, :], in0=ps[m % 4][:], scalar=0.0, in1=g[0][:, m, :],
                                                   op0=ALU.max, op1=ALU.subtract).then_inc(lo_ready, 1)
                    dve.wait_ge(stored, count(16 * b))
                    for j in range(TPS):
                        dve.wait_ge(y_ps, count(TPS * b + j + 1))
                        v.scalar_tensor_tensor(out=rows[:, j, :], in0=ps_y[j % 2][:], scalar=factor64[:, 0:1],
                                               in1=resid[:, TPS * b + j, :], op0=ALU.mult, op1=ALU.add
                                               ).then_inc(y_ready, 1)


def constants_stage(nc, ident, neg_causal, neg_rel, rel_bias, x_slots):
    st = Stage(nc, "constants")
    with st:
        rel = st.sb("rel", [P, SPAN], F32)
        zeros = st.sb("zeros", [P, D], F32)
        made, rel_in, zeroed, negated = (st.sem(x) for x in ("made", "rel_in", "zeroed", "negated"))
        n = x_slots.shape[0] // P
        st.begin()
        with nc.Block() as block:
            @block.sync
            def _(sp):
                sp.dma_start(rel[:], bass.AP(tensor=rel_bias.tensor, offset=rel_bias.offset, ap=[[1, P], [1, SPAN]])
                             ).then_inc(rel_in, 16)
                sp.wait_ge(made, count(3))
                for t in range(n):
                    sp.dma_start(x_slots.rearrange("(t p) d -> t p d", p=P)[t], zeros[:]).then_inc(zeroed, 16)
                sp.wait_ge(zeroed, count(16 * n))

            @block.gpsimd
            def _(pool):
                pool.memset(ident[:], 0.0).then_inc(made, 1)
                pool.memset(neg_causal[:], 0.0).then_inc(made, 1)
                pool.memset(zeros[:], 0.0).then_inc(made, 1)
                pool.wait_ge(made, count(3))
                pool.affine_select(out=ident[:], in_=ident[:], compare_op=ALU.not_equal, fill=1.0, base=0,
                                   pattern=[[-1, P]], channel_multiplier=1).then_inc(made, 1)
                pool.affine_select(out=neg_causal[:], in_=neg_causal[:], compare_op=ALU.is_ge, fill=BIG,
                                   base=SEQ - P, pattern=[[-1, SEQ]], channel_multiplier=1).then_inc(made, 1)

            @block.vector
            def _(dve):
                dve.wait_ge(rel_in, count(16))
                nc.vector.tensor_scalar(neg_rel[:], rel[:, ::-1], -1.0, None, ALU.mult).then_inc(negated, 1)


def tower(nc, x, L0_tok_weight, L0_attn_Wq, L0_attn_bq, L0_attn_Wk, L0_attn_bk, L0_attn_Wv, L0_attn_bv,
          L0_attn_Wo, L0_attn_bo, L0_attn_gamma, L0_attn_beta, L0_ffn_gate_w, L0_ffn_gate_b, L0_ffn_w1,
          L0_ffn_b1, L0_ffn_w2, L0_ffn_b2, L1_attn_Wqkv, L1_attn_bqkv, L1_attn_Wout, L1_attn_bout,
          L1_attn_rel_pos_bias, L1_ffn_k0, L1_ffn_k1, L1_ffn_k2, L1_ffn_s0, L1_ffn_s1, L1_ffn_s2, out):
    n_tiles = (2 * TOKENS + EXPERTS * (P - 1)) // P
    scratch = [nc.dram_tensor(f"qk_scratch{i}", (SEQS, PARTS, 2 * D, SEQ), BF16).ap() for i in range(2)]
    x_slots = nc.dram_tensor("x_slots", (n_tiles * P, D), F32).ap()
    y_slots = nc.dram_tensor("y_slots", (n_tiles * P, D), F32).ap()
    with ExitStack() as forever:
        forever.enter_context(nc.allow_non_contiguous_dma(reason="token ids and bias columns, a few KB"))
        sb = lambda n, shape, dt: forever.enter_context(nc.sbuf_tensor(n, shape, dt))
        resid = sb("resid", [P, TILES, D], F32)
        ident = sb("ident", [P, P], F32)
        neg_causal = sb("neg_causal", [P, SEQ], F32)
        neg_rel = sb("neg_rel", [P, SPAN], F32)

        constants_stage(nc, ident, neg_causal, neg_rel, L1_attn_rel_pos_bias, x_slots)
        embed_stage(nc, x, L0_tok_weight, resid)

        def attention(name, i, w_parts, b_qk, b_v, neg_bias, causal, w_out, b_out, norm_after, gamma, beta):
            with ExitStack() as ctx:
                v_parts = ctx.enter_context(nc.sbuf_tensor(f"{name}_v_parts", [P, TILES, HEADS, PARTS, HD], BF16))
                heads_out = ctx.enter_context(nc.sbuf_tensor(f"{name}_heads_out", [P, TILES, D], F32))
                qkv_stage(nc, f"{name}_qkv", ident, resid, w_parts, b_qk, b_v, scratch[i], v_parts)
                attention_stage(nc, f"{name}_core", ident, neg_bias, causal, scratch[i], v_parts, heads_out)
                rows_out_stage(nc, f"{name}_out", ident, heads_out, w_out, b_out, norm_after,
                               gamma, beta, resid)

        attention("attn0", 0, [L0_attn_Wq, L0_attn_Wk, L0_attn_Wv], [L0_attn_bq, L0_attn_bk], L0_attn_bv,
                  neg_causal, True, L0_attn_Wo, L0_attn_bo, True, L0_attn_gamma, L0_attn_beta)

        slots = [sb(f"slots{k}", [P, TILES], U32) for k in range(2)]
        gates = [sb(f"gates{k}", [P, TILES], F32) for k in range(2)]
        tile_expert = sb("tile_expert", [P, n_tiles], mybir.dt.int32)
        weights_in = forever.enter_context(nc.semaphore("weights_in"))
        with ExitStack() as ctx:
            wts = [ctx.enter_context(nc.sbuf_tensor("w1_all", [P, EXPERTS, DC, HIDDEN], F32)),
                   ctx.enter_context(nc.sbuf_tensor("w2_all", [P, EXPERTS, HC, D], F32))]
            route_stage(nc, "route", ident, resid, L0_ffn_gate_w, L0_ffn_gate_b, L0_ffn_w1, L0_ffn_w2,
                        wts, slots, gates, tile_expert, x_slots, weights_in)
            experts_stage(nc, "experts", ident, wts, L0_ffn_b1, L0_ffn_b2, tile_expert, x_slots, y_slots,
                          weights_in)
        combine_stage(nc, "combine", slots, gates, y_slots, resid)

        attention("attn1", 1, [L1_attn_Wqkv], [L1_attn_bqkv[0:2 * D]], L1_attn_bqkv[2 * D:3 * D],
                  neg_rel, False, L1_attn_Wout, L1_attn_bout, False, None, None)
        signs_stage(nc, "signs", ident, resid, L1_ffn_k0, L1_ffn_k1, L1_ffn_k2,
                    L1_ffn_s0, L1_ffn_s1, L1_ffn_s2, out)


_INS = ["x", "L0_tok_weight", "L0_attn_Wq", "L0_attn_bq", "L0_attn_Wk", "L0_attn_bk", "L0_attn_Wv", "L0_attn_bv",
        "L0_attn_Wo", "L0_attn_bo", "L0_attn_gamma", "L0_attn_beta", "L0_ffn_gate_w", "L0_ffn_gate_b", "L0_ffn_w1",
        "L0_ffn_b1", "L0_ffn_w2", "L0_ffn_b2", "L1_attn_Wqkv", "L1_attn_bqkv", "L1_attn_Wout", "L1_attn_bout",
        "L1_attn_rel_pos_bias", "L1_ffn_k0", "L1_ffn_k1", "L1_ffn_k2", "L1_ffn_s0", "L1_ffn_s1", "L1_ffn_s2"]


def kernel(**inputs):
    import numpy as _np
    import concourse.bacc as _bacc
    from concourse import mybir as _mybir
    from concourse.bass_utils import run_bass_kernel_spmd as _run

    nc = _bacc.Bacc("TRN2", target_bir_lowering=False, num_devices=1)
    arrays, args = {}, []
    for name in _INS:
        a = _np.ascontiguousarray(inputs[name])
        if a.ndim == 0:
            a = a.reshape(1)
        arrays[f"in_{name}"] = a
        args.append(nc.dram_tensor(f"in_{name}", a.shape, _mybir.dt.from_np(a.dtype), kind="ExternalInput").ap())
    out = nc.dram_tensor("out_0", (SEQS, SEQ, D), _mybir.dt.float32, kind="ExternalOutput").ap()
    tower(nc, *args, out)
    r = _run(nc, [arrays], core_ids=[0])
    return r.results[0]["out_0"]
```

```python
from contextlib import ExitStack

import concourse.bass as bass
from concourse import mybir

P = 128
SEQS, SEQ, D = 4, 512, 256
TOKENS = SEQS * SEQ
TILES = TOKENS // P
TPS = SEQ // P
DC = D // P
HEADS, HD = 16, 16
PAIRS = TPS // 2
EXPERTS, HIDDEN = 8, 1024
HC = HIDDEN // P
LN_EPS = 1e-5
PARTS = 3
VC = HD + 1
Q_PARTS = (0, 1, 0, 1, 2, 0)
K_PARTS = (0, 0, 1, 1, 0, 2)
STACK = len(Q_PARTS) * HD
SPAN = SEQ + SEQ - P
BIG = 3.0e38
BANK = 512

ALU = mybir.AluOpType
ACT = mybir.ActivationFunctionType
AX = mybir.AxisListType
F32 = mybir.dt.float32
F32R = mybir.dt.float32r
BF16 = mybir.dt.bfloat16
FP16 = mybir.dt.float16
U32 = mybir.dt.uint32
U8 = mybir.dt.uint8

PRODUCTS = ((0, 0), (1, 0), (0, 1))


def row_on_all_partitions(v, n):
    return bass.AP(tensor=v.tensor, offset=v.offset, ap=[[0, P], [1, n]])


def count(n):
    return n + 1


class Stage:

    def __init__(self, nc, name):
        self.nc, self.name = nc, name
        self.ctx, self.sems, self.zero_sems = ExitStack(), [], []

    def __enter__(self):
        return self

    def __exit__(self, kind, value, trace):
        self.ctx.close()
        if kind is None:
            self.nc.clear_and_free_semaphores(self.sems + self.zero_sems)

    def begin(self):
        for s in self.sems:
            self.nc.gpsimd.sem_inc(s, 1)
        self.nc.all_engine_barrier()

    def sb(self, name, shape, dt):
        return self.ctx.enter_context(self.nc.sbuf_tensor(f"{self.name}_{name}", shape, dt))

    def ps(self, name, shape):
        bank = self.ctx.enter_context(self.nc.psum_tensor(f"{self.name}_ps_{name}", [P, BANK], F32))
        n = 1
        for k in shape[1:]:
            n *= k
        view = bank[0:shape[0], 0:n]
        if len(shape) == 2:
            return view
        names = "abcd"[:len(shape) - 1]
        return view.rearrange(f"p ({' '.join(names)}) -> p {' '.join(names)}", **dict(zip(names, shape[1:])))

    def sem(self, name):
        self.sems.append(self.nc.alloc_semaphore(name=f"{self.name}_{name}"))
        return self.sems[-1]

    def zero_sem(self, name):
        self.zero_sems.append(self.nc.alloc_semaphore(name=f"{self.name}_{name}"))
        return self.zero_sems[-1]


def embed_stage(nc, ids, table, resid, x_slots):
    st = Stage(nc, "embed")
    rows, _ = table.shape
    per = rows * D // P
    SLOTS, PIECE = 4, 4000
    pieces = per // PIECE
    rounds = pieces // SLOTS
    with st:
        ring = st.sb("ring", [P, SLOTS, PIECE], F32)
        junk = st.sb("junk", [P, PIECE], BF16)
        idx = st.sb("idx", [P, TILES], U32)
        part = st.sb("part", [P, rounds, SLOTS], F32)
        total = st.sb("total", [P, 1], F32)
        ones = st.sb("ones", [P, P], F32)
        mean = st.sb("mean", [P, 1], F32)
        scale = st.sb("scale", [P, 1], F32)
        step = st.sb("step", [P, 1], F32)
        scaled = st.sb("scaled", [P, TPS, D], F32)
        below = st.sb("below", [P, TPS, D], F32)
        tern = st.sb("tern", [P, TPS, D], F32)
        zeros = st.sb("zeros", [P, D], F32)
        pmean = st.ps("pmean", [P, 1])

        piece_in = [st.sem(f"piece_in{s}") for s in range(SLOTS)]
        ids_in = st.sem("ids_in")
        gathered = st.zero_sem("gathered")
        act_summed = st.sem("act_summed")
        dve_summed = st.sem("dve_summed")
        ones_set = st.sem("ones_set")
        zeroed = st.sem("zeroed")
        total_ready = st.sem("total_ready")
        mean_ps = st.sem("mean_ps")
        chain = st.sem("chain")
        scaled_ready = st.sem("scaled_ready")
        tern_ready = st.sem("tern_ready")
        rows_done = st.sem("rows_done")

        pieces_of = table.rearrange("(p r) d -> p (r d)", p=P).rearrange(
            "p (i s n) -> p i s n", s=SLOTS, n=PIECE)
        chunk = lambda b: resid[:, b * TPS:(b + 1) * TPS, :]

        st.begin()
        with nc.Block() as block:
            @block.sync
            def _(sp):
                sp.dma_start(idx[:].bitcast(ids.dtype), ids.rearrange("b (t p) -> p (b t)", p=P),
                             ).then_inc(ids_in, 16)
                for s in range(SLOTS):
                    sp.dma_start(ring[:, s, :], pieces_of[:, 0, s, :]).then_inc(piece_in[s], 16)
                with sp.Fori(1, rounds) as i:
                    for s in range(SLOTS):
                        sp.wait_ge(act_summed if s % 2 == 0 else dve_summed, count(2 * i - 1 + s // 2))
                        sp.dma_start(ring[:, s, :], pieces_of[:, i, s, :]).then_inc(piece_in[s], 16)
                sp.wait_ge(ones_set, count(2))
                zero_rows = x_slots.rearrange("(t p) d -> t p d", p=P)
                for t in range(zero_rows.shape[0]):
                    sp.dma_start(zero_rows[t], zeros[:]).then_inc(zeroed, 16)
                sp.wait_ge(zeroed, count(16 * zero_rows.shape[0]))

            @block.gpsimd
            def _(pool):
                pool.memset(ones[:], 1.0).then_inc(ones_set, 1)
                pool.memset(zeros[:], 0.0).then_inc(ones_set, 1)
                pool.wait_ge(ids_in, count(16))
                for t in range(TILES):
                    pool.indirect_dma_start(out=resid[:, t, :], out_offset=None, in_=table,
                                            in_offset=bass.IndirectOffsetOnAxis(ap=idx[:, t:t + 1], axis=0)
                                            ).then_inc(gathered, 16)
                pool.wait_ge(gathered, 16 * TILES)

            @block.scalar
            def _(act):
                with act.Fori(0, rounds) as i:
                    for s in (0, 2):
                        act.wait_ge(piece_in[s], count(16 * i + 16))
                        if s == 2:
                            act.wait_ge(act_summed, count(2 * i + 1))
                        else:
                            act.wait_ge(act_summed, count(2 * i))
                        nc.scalar.activation(junk[:], ring[:, s, :], ACT.Abs,
                                             accum_out=part[:, i, s:s + 1]).then_inc(act_summed, 1)
                act.wait_ge(chain, count(4))
                act.wait_ge(gathered, 16 * TILES)
                for b in range(SEQS):
                    if b:
                        act.wait_ge(tern_ready, count(b))
                    nc.scalar.activation(scaled[:], chunk(b), ACT.Copy, scale=scale[:, 0:1]
                                         ).then_inc(scaled_ready, 1)
                    act.wait_ge(tern_ready, count(b + 1))
                    nc.scalar.activation(chunk(b), tern[:], ACT.Copy, scale=step[:, 0:1]
                                         ).then_inc(rows_done, 1)

            @block.vector
            def _(dve):
                with dve.Fori(0, rounds) as i:
                    for s in (1, 3):
                        dve.wait_ge(piece_in[s], count(16 * i + 16))
                        nc.vector.tensor_reduce(part[:, i, s:s + 1], ring[:, s, :], AX.X, ALU.add,
                                                apply_absolute_value=True).then_inc(dve_summed, 1)
                dve.wait_ge(dve_summed, count(2 * rounds))
                dve.wait_ge(act_summed, count(2 * rounds))
                nc.vector.tensor_reduce(total[:], part[:], AX.XY, ALU.add).then_inc(total_ready, 1)
                dve.wait_ge(mean_ps, count(1))
                nc.vector.tensor_scalar(mean[:], pmean[:], 1.0 / (rows * D), None, ALU.mult
                                        ).then_inc(chain, 1)
                dve.wait_ge(chain, count(1))
                nc.vector.tensor_scalar(total[:], mean[:], LN_EPS, None, ALU.max).then_inc(chain, 1)
                dve.wait_ge(chain, count(2))
                nc.vector.reciprocal(scale[:], total[:]).then_inc(chain, 1)
                dve.wait_ge(chain, count(3))
                nc.vector.reciprocal(step[:], scale[:]).then_inc(chain, 1)
                for b in range(SEQS):
                    dve.wait_ge(scaled_ready, count(b + 1))
                    nc.vector.tensor_scalar(below[:], scaled[:], -0.5, None, ALU.is_lt
                                            ).then_inc(chain, 1)
                    dve.wait_ge(chain, count(5 + b))
                    if b:
                        dve.wait_ge(rows_done, count(b))
                    nc.vector.scalar_tensor_tensor(out=tern[:], in0=scaled[:], scalar=0.5, in1=below[:],
                                                   op0=ALU.is_gt, op1=ALU.subtract
                                                   ).then_inc(tern_ready, 1)

            @block.tensor
            def _(pe):
                pe.wait_ge(ones_set, count(1))
                pe.wait_ge(total_ready, count(1))
                nc.tensor.matmul(pmean[:], ones[:], total[:], start=True, stop=True).then_inc(mean_ps, 1)


class Norm:

    def __init__(self, st, dt):
        self.dt = dt
        self.minus_half = st.sb("minus_half", [P, 1], F32)
        self.stats = st.sb("stats", [P, TILES, 6], F32)
        self.mv = st.sb("mv", [P, TILES, 2], F32)
        self.var_eps = st.sb("var_eps", [P, TILES], F32)
        self.rstd = st.sb("rstd", [P, TILES], F32)
        self.mean_seq = st.sb("mean_seq", [P, TPS], F32)
        self.stats_ready = st.sem("stats_ready")
        self.mv_ready = st.sem("mv_ready")
        self.pool_step = st.sem("pool_step")
        self.rstd_ready = st.sem("rstd_ready")

    def statistics(self, nc, dve, x):
        for t in range(TILES):
            nc.vector.bn_stats(self.stats[:, t, :], x[:, t, :]).then_inc(self.stats_ready, 1)
        for t in range(TILES):
            dve.wait_ge(self.stats_ready, count(t + 1))
            nc.vector.bn_aggr(self.mv[:, t, :], self.stats[:, t, :]).then_inc(self.mv_ready, 1)

    def inverse_deviation(self, nc, pool):
        nc.gpsimd.memset(self.minus_half[:], -0.5).then_inc(self.pool_step, 1)
        pool.wait_ge(self.mv_ready, count(TILES))
        nc.gpsimd.tensor_scalar(self.var_eps[:], self.mv[:, :, 1], LN_EPS, None, ALU.add
                                ).then_inc(self.pool_step, 1)
        pool.wait_ge(self.pool_step, count(2))
        nc.gpsimd.tensor_tensor(self.rstd[:], self.var_eps[:],
                                self.minus_half[:, 0:1].to_broadcast([P, TILES]), ALU.pow
                                ).then_inc(self.rstd_ready, 1)


class Turn:

    def __init__(self, st, dt):
        self.dt = dt
        self.ps = [st.ps(f"turned{c}", [P, SEQ]) for c in range(DC)]
        self.hi = st.sb("x_hi", [P, DC, SEQ], dt)
        self.lo = st.sb("x_lo", [P, DC, SEQ], dt)
        self.row_ready = st.sem("row_ready")
        self.turned = st.sem("x_turned")
        self.hi_ready = st.sem("x_hi_ready")
        self.lo_ready = st.sem("x_lo_ready")

    def plain(self, x):
        return x.bitcast(F32) if self.dt == F32R else x

    def on_tensor(self, nc, pe, b, rows, ident):
        pe.wait_ge(self.lo_ready, count(DC * b))
        for j in range(TPS):
            pe.wait_ge(self.row_ready, count(TPS * b + j + 1))
            for c in range(DC):
                last = nc.tensor.transpose(self.ps[c][:, j * P:(j + 1) * P],
                                           rows(j)[:, c * P:(c + 1) * P], ident[:])
        last.then_inc(self.turned, 1)

    def on_scalar(self, nc, act, b):
        act.wait_ge(self.turned, count(b + 1))
        for c in range(DC):
            nc.scalar.activation(self.hi[:, c, :], self.ps[c][:], ACT.Copy).then_inc(self.hi_ready, 1)

    def on_vector(self, nc, dve, b):
        for c in range(DC):
            dve.wait_ge(self.hi_ready, count(DC * b + c + 1))
            nc.vector.tensor_tensor(self.lo[:, c, :], self.ps[c][:], self.plain(self.hi[:, c, :]),
                                    ALU.subtract).then_inc(self.lo_ready, 1)


def qkv_stage(nc, name, ident, resid, w_parts, b_qk, b_v, qk_scratch, v_parts):
    st = Stage(nc, name)
    QK = 2 * D // P
    with st:
        norm, turn = Norm(st, F32R), Turn(st, F32R)
        wf = st.sb("wf", [P, DC, 3 * D], F32)
        w_hi = st.sb("w_hi", [P, DC, 3 * D], F32R)
        w_lo = st.sb("w_lo", [P, DC, 3 * D], F32R)
        bias = st.sb("bias", [P, QK], F32)
        bias_q = st.sb("bias_q", [P, QK], F32)
        bv = st.sb("bv", [P, D], F32)
        xn = st.sb("xn", [P, TPS, D], F32)
        full = st.sb("full", [P, 2, SEQ], F32)
        rest = st.sb("rest", [P, 2, SEQ], F32)
        qk_parts = st.sb("qk_parts", [P, QK, PARTS, SEQ], BF16)
        v_full = st.sb("v_full", [P, 2, D], F32)
        v_rest = st.sb("v_rest", [P, 2, D], F32)
        ps_qk = [st.ps(f"qk{i}", [P, SEQ]) for i in range(2)]
        ps_v = [st.ps(f"v{i}", [P, D]) for i in range(2)]

        loaded, ones_set = st.sem("loaded"), st.sem("ones_set")
        bias_scaled = st.sem("bias_scaled")
        w_hi_ready, w_lo_ready = st.sem("w_hi_ready"), st.sem("w_lo_ready")
        qk_ps, v_ps = st.sem("qk_ps"), st.sem("v_ps")
        qk_full, qk_hi, qk_rest, qk_mid, qk_lo = (
            st.sem(f"qk_{s}") for s in ("full", "hi", "rest", "mid", "lo"))
        v_fulls, v_hi, v_rests, v_mid, v_lo = (
            st.sem(f"v_{s}") for s in ("fulls", "hi", "rests", "mid", "lo"))
        stored = [st.sem(f"stored{m}") for m in range(QK)]
        n_loads = len(w_parts) + len(b_qk) + 1

        out_of = qk_scratch.rearrange("b s (m p) t -> b m p s t", p=P)

        st.begin()
        with nc.Block() as block:
            @block.sync
            def _(sp):
                at = 0
                for w in w_parts:
                    n = w.shape[1]
                    sp.dma_start(wf[:, :, at:at + n], w.rearrange("(c p) n -> p c n", p=P)).then_inc(loaded, 16)
                    at += n
                at = 0
                for v in b_qk:
                    m = v.shape[0] // P
                    sp.dma_start(bias[:, at:at + m], v.rearrange("(m p) -> p m", p=P)).then_inc(loaded, 16)
                    at += m
                sp.dma_start(bv[:], row_on_all_partitions(b_v, D)).then_inc(loaded, 16)
                with sp.Fori(0, SEQS) as b:
                    for m in range(QK):
                        sp.wait_ge(qk_lo, count(QK * b + m + 1))
                        sp.dma_start(out_of[b, m], qk_parts[:, m]).then_inc(stored[m], 16)
                for s in stored:
                    sp.wait_ge(s, count(16 * SEQS))

            @block.gpsimd
            def _(pool):
                for x in range(PARTS):
                    nc.gpsimd.memset(v_parts[:, :, :, x, HD], 1.0 if x == 0 else 0.0).then_inc(ones_set, 1)
                norm.inverse_deviation(nc, pool)

            @block.tensor
            def _(pe):
                pe.wait_ge(w_lo_ready, count(1))
                with pe.Fori(0, SEQS) as b:
                    turn.on_tensor(nc, pe, b, lambda j: xn[:, j, :], ident)
                    pe.wait_ge(turn.lo_ready, count(DC * b + DC))
                    for m in range(QK):
                        pe.wait_ge(qk_full, count(QK * b + m - 1)) if m >= 2 else pe.wait_ge(qk_full, count(QK * b))
                        n = 0
                        for pw, px in PRODUCTS:
                            for c in range(DC):
                                w = (w_hi, w_lo)[pw][:, c, m * P:(m + 1) * P]
                                last = nc.tensor.matmul(ps_qk[m % 2][:], w, (turn.hi, turn.lo)[px][:, c, :],
                                                        start=n == 0, stop=n == 3 * DC - 1)
                                n += 1
                        last.then_inc(qk_ps, 1)
                    for j in range(TPS):
                        pe.wait_ge(v_fulls, count(TPS * b + j - 1)) if j >= 2 else pe.wait_ge(v_fulls, count(TPS * b))
                        n = 0
                        for pw, px in PRODUCTS:
                            for c in range(DC):
                                x = (turn.hi, turn.lo)[px][:, c, j * P:(j + 1) * P]
                                last = nc.tensor.matmul(ps_v[j % 2][:], x, (w_hi, w_lo)[pw][:, c, 2 * D:3 * D],
                                                        start=n == 0, stop=n == 3 * DC - 1)
                                n += 1
                        last.then_inc(v_ps, 1)

            @block.scalar
            def _(act):
                act.wait_ge(loaded, count(16 * n_loads))
                nc.scalar.activation(w_hi[:], wf[:], ACT.Copy).then_inc(w_hi_ready, 1)
                nc.scalar.activation(bias_q[:, 0:DC], bias[:, 0:DC], ACT.Copy, scale=-0.25).then_inc(bias_scaled, 1)
                nc.scalar.activation(bias_q[:, DC:QK], bias[:, DC:QK], ACT.Copy).then_inc(bias_scaled, 1)
                act.wait_ge(bias_scaled, count(2))
                with act.Fori(0, SEQS) as b:
                    act.wait_ge(v_ps, count(TPS * b))
                    turn.on_scalar(nc, act, b)

                    def full_and_high(m):
                        k = m % 2
                        act.wait_ge(qk_ps, count(QK * b + m + 1))
                        act.wait_ge(qk_rest, count(QK * b + max(m - 1, 0)))
                        nc.scalar.activation(full[:, k, :], ps_qk[k][:], ACT.Identity, bias=bias_q[:, m:m + 1],
                                             scale=-0.25 if m < DC else 1.0).then_inc(qk_full, 1)
                        act.wait_ge(qk_full, count(QK * b + m + 1))
                        act.wait_ge(stored[m], count(16 * b))
                        nc.scalar.activation(qk_parts[:, m, 0, :], full[:, k, :], ACT.Copy).then_inc(qk_hi, 1)

                    def middle(m):
                        act.wait_ge(qk_rest, count(QK * b + m + 1))
                        nc.scalar.activation(qk_parts[:, m, 1, :], rest[:, m % 2, :], ACT.Copy).then_inc(qk_mid, 1)

                    heads = lambda x: x.rearrange("p (h d) -> p h d", d=HD)

                    def v_high(j):
                        act.wait_ge(v_fulls, count(TPS * b + j + 1))
                        nc.scalar.activation(v_parts[:, TPS * b + j, :, 0, 0:HD], heads(v_full[:, j % 2, :]), ACT.Copy
                                             ).then_inc(v_hi, 1)

                    def v_middle(j):
                        act.wait_ge(v_rests, count(TPS * b + j + 1))
                        nc.scalar.activation(v_parts[:, TPS * b + j, :, 1, 0:HD], heads(v_rest[:, j % 2, :]), ACT.Copy
                                             ).then_inc(v_mid, 1)

                    for m in range(QK + 1):
                        if m < QK:
                            full_and_high(m)
                        if m:
                            middle(m - 1)
                    for j in range(TPS + 1):
                        if j < TPS:
                            v_high(j)
                        if j:
                            v_middle(j - 1)

            @block.vector
            def _(dve):
                norm.statistics(nc, dve, resid)
                dve.wait_ge(w_hi_ready, count(1))
                nc.vector.tensor_tensor(w_lo[:], wf[:], w_hi[:].bitcast(F32), ALU.subtract).then_inc(w_lo_ready, 1)
                dve.wait_ge(norm.rstd_ready, count(1))
                with dve.Fori(0, SEQS) as b:
                    def normalise(b):
                        dve.wait_ge(turn.turned, count(b))
                        for j in range(TPS):
                            nc.vector.tensor_scalar(xn[:, j, :], resid[:, TPS * b + j, :],
                                                    norm.mv[:, bass.ds(TPS * b + j, 1), 0],
                                                    norm.rstd[:, bass.ds(TPS * b + j, 1)],
                                                    ALU.subtract, ALU.mult).then_inc(turn.row_ready, 1)

                    normalise(b)
                    dve.wait_ge(v_ps, count(TPS * b))
                    turn.on_vector(nc, dve, b)

                    def remainder(m):
                        dve.wait_ge(qk_hi, count(QK * b + m + 1))
                        dve.wait_ge(qk_lo, count(QK * b + max(m - 1, 0)))
                        nc.vector.tensor_tensor(rest[:, m % 2, :], full[:, m % 2, :], qk_parts[:, m, 0, :],
                                                ALU.subtract).then_inc(qk_rest, 1)

                    def lowest(m):
                        dve.wait_ge(qk_mid, count(QK * b + m + 1))
                        nc.vector.tensor_tensor(qk_parts[:, m, 2, :], rest[:, m % 2, :], qk_parts[:, m, 1, :],
                                                ALU.subtract).then_inc(qk_lo, 1)

                    heads = lambda x: x.rearrange("p (h d) -> p h d", d=HD)

                    def v_whole(j):
                        dve.wait_ge(v_ps, count(TPS * b + j + 1))
                        dve.wait_ge(v_rests, count(TPS * b + max(j - 1, 0)))
                        nc.vector.tensor_tensor(v_full[:, j % 2, :], ps_v[j % 2][:], bv[:], ALU.add
                                                ).then_inc(v_fulls, 1)

                    def v_remainder(j):
                        dve.wait_ge(v_hi, count(TPS * b + j + 1))
                        dve.wait_ge(v_lo, count(TPS * b + max(j - 1, 0)))
                        nc.vector.tensor_tensor(heads(v_rest[:, j % 2, :]), heads(v_full[:, j % 2, :]),
                                                v_parts[:, TPS * b + j, :, 0, 0:HD], ALU.subtract).then_inc(v_rests, 1)

                    def v_lowest(j):
                        dve.wait_ge(v_mid, count(TPS * b + j + 1))
                        nc.vector.tensor_tensor(v_parts[:, TPS * b + j, :, 2, 0:HD], heads(v_rest[:, j % 2, :]),
                                                v_parts[:, TPS * b + j, :, 1, 0:HD], ALU.subtract).then_inc(v_lo, 1)

                    for m in range(QK + 1):
                        if m < QK:
                            remainder(m)
                        if m:
                            lowest(m - 1)
                    for j in range(TPS + 2):
                        if j < TPS:
                            v_whole(j)
                        if 1 <= j <= TPS:
                            v_remainder(j - 1)
                        if j >= 2:
                            v_lowest(j - 2)


def attention_stage(nc, name, ident, neg_bias, causal, qk_scratch, v_parts, heads_out):
    st = Stage(nc, name)
    width = [(i + 1) * P if causal else SEQ for i in range(TPS)]
    ALL_HEADS = SEQS * HEADS
    with st:
        q = [st.sb(f"q{s}", [STACK, HEADS, SEQ], BF16) for s in range(2)]
        k = [st.sb(f"k{s}", [STACK, HEADS, SEQ], BF16) for s in range(2)]
        neg = st.sb("neg", [P, TPS, SEQ], F32)
        row_min = st.sb("row_min", [P, TPS], F32)
        prob = st.sb("prob", [P, TPS, SEQ], F32)
        pt_hi = st.sb("pt_hi", [P, TPS, SEQ], FP16)
        pt_lo = st.sb("pt_lo", [P, TPS, SEQ], FP16)
        ps_s = [st.ps(f"s{i}", [P, SEQ]) for i in range(2)]
        ps_t = [st.ps(f"t{i}", [P, SEQ]) for i in range(TPS)]
        ps_o = [st.ps(f"o{i}", [P, 2, PARTS * VC]) for i in range(PAIRS)]

        qk_in = [st.sem(f"qk_in{s}") for s in range(2)]
        scored = st.sem("scored")
        lowered = st.sem("lowered")
        exped = st.sem("exped")
        turned = st.sem("turned")
        hi_ready, lo_ready = st.sem("hi_ready"), st.sem("lo_ready")
        mixed = [st.sem(f"mixed{i}") for i in range(TPS)]
        summed = [st.sem(f"summed{p}") for p in range(PAIRS)]
        LOADS = 2 * len(Q_PARTS)

        st.begin()
        with nc.Block() as block:
            @block.sync
            def _(sp):
                def load(b, s):
                    for r, (pq, pk) in enumerate(zip(Q_PARTS, K_PARTS)):
                        rows = slice(r * HD, (r + 1) * HD)
                        sp.dma_start(q[s][rows], qk_scratch[b, pq, 0:D].rearrange("(h d) t -> d h t", d=HD)
                                     ).then_inc(qk_in[s], 16)
                        sp.dma_start(k[s][rows], qk_scratch[b, pk, D:2 * D].rearrange("(h d) t -> d h t", d=HD)
                                     ).then_inc(qk_in[s], 16)
                for s in range(2):
                    load(s, s)
                with sp.Fori(1, SEQS // 2) as bb:
                    for s in range(2):
                        sp.wait_ge(scored, count(TPS * HEADS * (2 * bb + s - 1)))
                        load(2 * bb + s, s)

            @block.tensor
            def _(pe):
                def score(s, h, i):
                    nc.tensor.matmul(ps_s[i % 2][:, 0:width[i]], q[s][:, h, i * P:(i + 1) * P],
                                     k[s][:, h, 0:width[i]], start=True, stop=True).then_inc(scored, 1)

                def turn(n, i):
                    pe.wait_ge(exped, count(n + 1))
                    for kt in range(width[i] // P):
                        last = nc.tensor.transpose(ps_t[i][:, kt * P:(kt + 1) * P],
                                                   prob[:, i, kt * P:(kt + 1) * P], ident[:])
                    last.then_inc(turned, 1)

                def mix(b, g, h, i):
                    if i % 2 == 0:
                        pe.wait_ge(summed[i // 2], count(g))
                    pe.wait_ge(lo_ready, count(TPS * g + i + 1))
                    tiles = width[i] // P
                    for kt in range(tiles):
                        for x, part in enumerate((pt_hi, pt_lo)):
                            last = nc.tensor.matmul(
                                ps_o[i // 2][:, i % 2], part[:, i, kt * P:(kt + 1) * P],
                                v_parts[:, TPS * b + kt, h].rearrange("p s d -> p (s d)"),
                                start=kt == 0 and x == 0, stop=kt == tiles - 1 and x == 1)
                    last.then_inc(mixed[i], 1)

                def step(b, h, i, scored_b, scored_h, turns=True):
                    g = HEADS * b + h
                    n = TPS * g + i
                    if scored_b < SEQS:
                        pe.wait_ge(lowered, count(n + 4))
                        score(scored_b % 2, scored_h, (i + 1) % TPS)
                    if turns:
                        turn(n + 2, (i + 2) % TPS)
                    mix(b, g, h, i)

                pe.wait_ge(qk_in[0], count(16 * LOADS))
                for n in range(5):
                    if n >= 2:
                        pe.wait_ge(lowered, count(n - 1))
                    score(0, n // TPS, n % TPS)
                for i in range(2):
                    turn(i, i)
                for b in range(SEQS):
                    with pe.Fori(0, HEADS - 2) as h:
                        for i in range(TPS):
                            step(b, h, i, b, h + 1 + (i + 1) // TPS)
                    for h in range(HEADS - 2, HEADS):
                        for i in range(TPS):
                            ahead = HEADS * b + h + 1 + (i + 1) // TPS
                            if ahead == HEADS * (b + 1) and i == TPS - 1 and b + 1 < SEQS:
                                pe.wait_ge(qk_in[(b + 1) % 2], count(16 * LOADS * ((b + 1) // 2 + 1)))
                            step(b, h, i, ahead // HEADS, ahead % HEADS,
                                 turns=TPS * (HEADS * b + h) + i + 2 < TPS * ALL_HEADS)

            @block.scalar
            def _(act):
                def exponential(n, i):
                    act.wait_ge(lowered, count(n + 1))
                    nc.scalar.activation(prob[:, i, 0:width[i]], neg[:, i, 0:width[i]], ACT.Exp,
                                         bias=row_min[:, i:i + 1], scale=-1.0).then_inc(exped, 1)

                def high(g, i):
                    act.wait_ge(turned, count(TPS * g + i + 1))
                    act.wait_ge(mixed[i], count(g))
                    nc.scalar.activation(pt_hi[:, i, 0:width[i]], ps_t[i][:, 0:width[i]], ACT.Copy
                                         ).then_inc(hi_ready, 1)

                for i in range(2):
                    exponential(i, i)
                with act.Fori(0, ALL_HEADS - 1) as g:
                    for i in range(TPS):
                        high(g, i)
                        exponential(TPS * g + i + 2, (i + 2) % TPS)
                for i in range(TPS):
                    high(ALL_HEADS - 1, i)
                    if i + 2 < TPS:
                        exponential(TPS * (ALL_HEADS - 1) + i + 2, i + 2)

            @block.vector
            def _(dve):
                def lower(i):
                    lo = SEQ - P - i * P
                    nc.vector.tensor_tensor_reduce(
                        neg[:, i, 0:width[i]], ps_s[i % 2][:, 0:width[i]], neg_bias[:, lo:lo + width[i]],
                        1.0, BIG, ALU.add, ALU.min, row_min[:, i:i + 1]).then_inc(lowered, 1)

                def low(g, i):
                    dve.wait_ge(hi_ready, count(TPS * g + i + 1))
                    dve.wait_ge(mixed[i], count(g))
                    nc.vector.tensor_tensor(pt_lo[:, i, 0:width[i]], ps_t[i][:, 0:width[i]],
                                            pt_hi[:, i, 0:width[i]], ALU.subtract).then_inc(lo_ready, 1)

                def finish(g, p):
                    dve.wait_ge(mixed[2 * p + 1], count(g + 1))
                    nc.vector.tensor_reduce(heads_out[:, bass.ds(g, 1), 2 * p:2 * p + 2],
                                            ps_o[p][:].rearrange("p i (s d) -> p i d s", d=VC),
                                            AX.X, ALU.add).then_inc(summed[p], 1)

                def head(g, first, last):
                    for i in range(TPS):
                        n = TPS * g + i
                        if not last:
                            dve.wait_ge(exped, count(n + 1))
                            dve.wait_ge(scored, count(n + 5))
                        low(g, i)
                        if not last:
                            lower(i)
                        if i == 1 and not first:
                            finish(g - 1, 1)
                        if i == 3:
                            finish(g, 0)

                for i in range(TPS):
                    dve.wait_ge(scored, count(i + 1))
                    lower(i)
                head(0, True, False)
                with dve.Fori(1, ALL_HEADS - 1) as g:
                    head(g, False, False)
                head(ALL_HEADS - 1, False, True)
                finish(ALL_HEADS - 1, 1)


def rows_out_stage(nc, name, ident, heads_out, w, bias, norm_after, gamma, beta, resid, prefetch=()):
    st = Stage(nc, name)
    with st:
        turn = Turn(st, F32R)
        wf = st.sb("wf", [P, DC, D], F32)
        w_hi = st.sb("w_hi", [P, DC, D], F32R)
        w_lo = st.sb("w_lo", [P, DC, D], F32R)
        rows_in = st.sb("rows_in", [P, TPS, D], F32)
        inv_sum = st.sb("inv_sum", [P, SEQS * HEADS, TPS], F32)
        rows = {n: st.sb(n, [P, D], F32) for n in ("bias", "gamma", "beta")}
        y = st.sb("y", [P, TILES, D], F32)
        ps_y = [st.ps(f"y{i}", [P, D]) for i in range(2)]
        norm = Norm(st, F32R) if norm_after else None
        loaded, inverted = st.sem("loaded"), st.sem("inverted")
        w_hi_ready, w_lo_ready = st.sem("w_hi_ready"), st.sem("w_lo_ready")
        y_ps, y_ready = st.sem("y_ps"), st.sem("y_ready")
        normed, scaled, added, moved = st.sem("normed"), st.sem("scaled"), st.sem("added"), st.sem("moved")
        vectors = [("bias", bias)] + ([("gamma", gamma), ("beta", beta)] if norm_after else [])

        st.begin()
        with nc.Block() as block:
            @block.sync
            def _(sp):
                sp.dma_start(wf[:], w.rearrange("(c p) n -> p c n", p=P)).then_inc(loaded, 16)
                for n, v in vectors:
                    sp.dma_start(rows[n][:], row_on_all_partitions(v, D)).then_inc(loaded, 16)
                for on_chip, dram, arrived in prefetch:
                    sp.dma_start(on_chip, dram).then_inc(arrived, 16)

            @block.gpsimd
            def _(pool):
                pool.wait_ge(inverted, count(1))
                with pool.Fori(0, SEQS) as b:
                    pool.wait_ge(turn.turned, count(b))
                    for j in range(TPS):
                        heads = bass.ds(HEADS * b, HEADS)
                        nc.gpsimd.tensor_tensor(rows_in[:, j].rearrange("p (h d) -> p h d", d=HD),
                                                heads_out[:, heads, j, 0:HD],
                                                inv_sum[:, heads, j].unsqueeze(2).to_broadcast([P, HEADS, HD]),
                                                ALU.mult).then_inc(turn.row_ready, 1)
                if norm_after:
                    norm.inverse_deviation(nc, pool)

            @block.tensor
            def _(pe):
                pe.wait_ge(w_lo_ready, count(1))
                with pe.Fori(0, SEQS) as b:
                    turn.on_tensor(nc, pe, b, lambda j: rows_in[:, j, :], ident)
                    pe.wait_ge(turn.lo_ready, count(DC * b + DC))
                    for j in range(TPS):
                        pe.wait_ge(y_ready, count(TPS * b + max(j - 1, 0)))
                        n = 0
                        for pw, px in PRODUCTS:
                            for c in range(DC):
                                x = (turn.hi, turn.lo)[px][:, c, j * P:(j + 1) * P]
                                last = nc.tensor.matmul(ps_y[j % 2][:], x, (w_hi, w_lo)[pw][:, c, :],
                                                        start=n == 0, stop=n == 3 * DC - 1)
                                n += 1
                        last.then_inc(y_ps, 1)

            @block.scalar
            def _(act):
                act.wait_ge(loaded, count(16 * (1 + len(vectors))))
                nc.scalar.activation(w_hi[:], wf[:], ACT.Copy).then_inc(w_hi_ready, 1)
                with act.Fori(0, SEQS) as b:
                    act.wait_ge(y_ps, count(TPS * b))
                    turn.on_scalar(nc, act, b)

            @block.vector
            def _(dve):
                nc.vector.reciprocal(inv_sum[:], heads_out[:, :, :, HD]).then_inc(inverted, 1)
                dve.wait_ge(w_hi_ready, count(1))
                nc.vector.tensor_tensor(w_lo[:], wf[:], w_hi[:].bitcast(F32), ALU.subtract).then_inc(w_lo_ready, 1)
                with dve.Fori(0, SEQS) as b:
                    dve.wait_ge(y_ps, count(TPS * b))
                    turn.on_vector(nc, dve, b)
                    for j in range(TPS):
                        t = TPS * b + j
                        dve.wait_ge(y_ps, count(t + 1))
                        nc.vector.tensor_tensor(y[:, t, :], ps_y[j % 2][:], rows["bias"][:], ALU.add
                                                ).then_inc(y_ready, 1)
                dve.wait_ge(y_ready, count(TILES))
                if norm_after:
                    norm.statistics(nc, dve, y)
                    dve.wait_ge(norm.rstd_ready, count(1))
                    for t in range(TILES):
                        nc.vector.tensor_scalar(y[:, t, :], y[:, t, :], norm.mv[:, t, 0:1], norm.rstd[:, t:t + 1],
                                                ALU.subtract, ALU.mult).then_inc(normed, 1)
                    dve.wait_ge(normed, count(TILES))
                    across = lambda n: rows[n][:].unsqueeze(1).to_broadcast([P, TILES, D])
                    nc.vector.tensor_tensor(y[:], y[:], across("gamma"), ALU.mult).then_inc(scaled, 1)
                    dve.wait_ge(scaled, count(1))
                    nc.vector.tensor_tensor(y[:], y[:], across("beta"), ALU.add).then_inc(moved, 1)
                    dve.wait_ge(moved, count(1))
                nc.vector.tensor_tensor(resid[:], resid[:], y[:], ALU.add).then_inc(added, 1)


def route_stage(nc, name, ident, resid, gate_w, gate_b, slots, gates, tile_expert, x_slots):
    st = Stage(nc, name)
    n_tiles = tile_expert.shape[1]
    E = EXPERTS
    with st:
        norm = Norm(st, F32)
        xn = st.sb("xn", [P, TILES, D], F32)
        x_t = st.sb("x_t", [P, DC, SEQ], F32)
        gw = st.sb("gw", [E, D], F32)
        gw_t = st.sb("gw_t", [P, DC, E], F32)
        gb = st.sb("gb", [P, E], F32)
        eid = st.sb("eid", [P, E], F32)
        tau = st.sb("tau", [P, n_tiles], F32)
        before = st.sb("before", [P, P], F32)
        ones = st.sb("ones", [P, P], F32)
        t8 = {n: st.sb(n, [P, TILES, E], F32) for n in (
            "logits", "shifted", "expd", "probs", "best", "wheref", "first", "second", "both", "tile_sum",
            "run_a", "run_b", "ahead", "based", "slot", "slot1", "slot2")}
        where = st.sb("where", [P, TILES, 8], U32)
        t1 = {n: st.sb(n, [P, TILES], F32) for n in ("gmax", "gsum", "ginv", "slot1f", "slot2f")}
        e1 = {n: st.sb(n, [P, E], F32) for n in ("tiles_f", "tiles", "start_a", "start_b", "start", "start_p")}
        tiles_i = st.sb("tiles_i", [P, E], mybir.dt.int32)
        passed = st.sb("passed", [P, n_tiles, E], F32)
        expert_f = st.sb("expert_f", [P, n_tiles], F32)
        ps_x = [st.ps(f"x{c}", [P, SEQ]) for c in range(DC)]
        ps_w = st.ps("w", [P, DC, E])
        ps_l = st.ps("l", [P, TILES, E])
        ps_r = st.ps("r", [P, TILES, E])
        ps_c = st.ps("c", [P, TILES, E])

        loaded, const, step = st.sem("loaded"), st.sem("const"), st.sem("step")
        gw_ps, gw_ready = st.sem("gw_ps"), st.sem("gw_ready")
        row_ready, turned, x_ready, logit_ps = (st.sem(x) for x in ("row_ready", "turned", "x_ready", "logit_ps"))
        shifted_ready, expd_ready = st.sem("shifted_ready"), st.sem("expd_ready")
        picked, counted, slots_ready = (st.sem(x) for x in ("picked", "counted", "slots_ready"))
        scattered = st.zero_sem("scattered")

        st.begin()
        with nc.Block() as block:
            @block.sync
            def _(sp):
                sp.dma_start(gw[:], gate_w).then_inc(loaded, 16)
                sp.dma_start(gb[:], row_on_all_partitions(gate_b, E)).then_inc(loaded, 16)

            @block.gpsimd
            def _(pool):
                pool.memset(ones[:], 1.0).then_inc(const, 1)
                pool.wait_ge(const, count(1))
                pool.affine_select(out=before[:], in_=ones[:], compare_op=ALU.is_gt, fill=0.0, base=0,
                                   pattern=[[1, P]], channel_multiplier=-1).then_inc(const, 1)
                pool.iota(eid[:], pattern=[[1, E]], base=0, channel_multiplier=0,
                          allow_small_or_imprecise_dtypes=True).then_inc(const, 1)
                pool.iota(tau[:], pattern=[[1, n_tiles]], base=0, channel_multiplier=0,
                          allow_small_or_imprecise_dtypes=True).then_inc(const, 1)
                norm.inverse_deviation(nc, pool)
                pool.wait_ge(slots_ready, count(2))
                for t in range(TILES):
                    for which in range(2):
                        pool.indirect_dma_start(
                            out=x_slots, out_offset=bass.IndirectOffsetOnAxis(ap=slots[which][:, t:t + 1], axis=0),
                            in_=xn[:, t, :], in_offset=None).then_inc(scattered, 16)
                pool.wait_ge(scattered, 32 * TILES)

            @block.tensor
            def _(pe):
                pe.wait_ge(loaded, count(32))
                for c in range(DC):
                    last = nc.tensor.transpose(ps_w[:, c, :], gw[:, c * P:(c + 1) * P], ident[0:E, 0:E])
                last.then_inc(gw_ps, 1)
                pe.wait_ge(gw_ready, count(1))
                for b in range(SEQS):
                    pe.wait_ge(x_ready, count(DC * b))
                    pe.wait_ge(row_ready, count(TPS * b + TPS))
                    for j in range(TPS):
                        for c in range(DC):
                            last = nc.tensor.transpose(ps_x[c][:, j * P:(j + 1) * P],
                                                       xn[:, TPS * b + j, c * P:(c + 1) * P], ident[:])
                    last.then_inc(turned, 1)
                    pe.wait_ge(x_ready, count(DC * b + DC))
                    for j in range(TPS):
                        for c in range(DC):
                            last = nc.tensor.matmul(ps_l[:, TPS * b + j, :], x_t[:, c, j * P:(j + 1) * P],
                                                    gw_t[:, c, :], start=c == 0, stop=c == DC - 1)
                    last.then_inc(logit_ps, 1)
                pe.wait_ge(picked, count(1))
                pe.wait_ge(const, count(2))
                flat = lambda x: x.rearrange("p t e -> p (t e)")
                nc.tensor.matmul(flat(ps_r[:]), before[:], flat(t8["both"][:]), start=True, stop=True
                                 ).then_inc(counted, 1)
                nc.tensor.matmul(flat(ps_c[:]), ones[:], flat(t8["both"][:]), start=True, stop=True
                                 ).then_inc(counted, 1)

            @block.scalar
            def _(act):
                act.wait_ge(gw_ps, count(1))
                nc.scalar.activation(gw_t[:], ps_w[:], ACT.Copy).then_inc(gw_ready, 1)
                for b in range(SEQS):
                    act.wait_ge(turned, count(b + 1))
                    act.wait_ge(logit_ps, count(b))
                    for c in range(DC):
                        nc.scalar.activation(x_t[:, c, :], ps_x[c][:], ACT.Copy).then_inc(x_ready, 1)
                act.wait_ge(shifted_ready, count(1))
                nc.scalar.activation(t8["expd"][:], t8["shifted"][:], ACT.Exp).then_inc(expd_ready, 1)

            @block.vector
            def _(dve):
                v = nc.vector
                norm.statistics(nc, dve, resid)
                dve.wait_ge(norm.rstd_ready, count(1))
                for t in range(TILES):
                    v.tensor_scalar(xn[:, t, :], resid[:, t, :], norm.mv[:, t, 0:1], norm.rstd[:, t:t + 1],
                                    ALU.subtract, ALU.mult).then_inc(row_ready, 1)
                over_e = lambda x: x.unsqueeze(2).to_broadcast([P, TILES, E])
                over_t = lambda x: x.unsqueeze(1).to_broadcast([P, TILES, E])
                done = 0

                def chain(ins):
                    nonlocal done
                    done += 1
                    ins.then_inc(step, 1)
                    dve.wait_ge(step, count(done))

                dve.wait_ge(logit_ps, count(SEQS))
                dve.wait_ge(loaded, count(32))
                chain(v.tensor_tensor(t8["logits"][:], ps_l[:], over_t(gb[:]), ALU.add))
                chain(v.tensor_reduce(t1["gmax"][:], t8["logits"][:], AX.X, ALU.max))
                v.tensor_tensor(t8["shifted"][:], t8["logits"][:], over_e(t1["gmax"][:]), ALU.subtract
                                ).then_inc(shifted_ready, 1)
                dve.wait_ge(expd_ready, count(1))
                chain(v.tensor_reduce(t1["gsum"][:], t8["expd"][:], AX.X, ALU.add))
                chain(v.reciprocal(t1["ginv"][:], t1["gsum"][:]))
                chain(v.tensor_tensor(t8["probs"][:], t8["expd"][:], over_e(t1["ginv"][:]), ALU.mult))
                for t in range(TILES):
                    chain(v.max(out=t8["best"][:, t, :], in_=t8["probs"][:, t, :]))
                    chain(v.max_index(out=where[:, t, :], in_max=t8["best"][:, t, :], in_values=t8["probs"][:, t, :]))
                chain(v.tensor_copy(t8["wheref"][:], where[:]))
                chain(v.tensor_copy(gates[0][:], t8["best"][:, :, 0]))
                chain(v.tensor_copy(gates[1][:], t8["best"][:, :, 1]))
                dve.wait_ge(const, count(4))
                for k, n in enumerate(("first", "second")):
                    chain(v.tensor_tensor(t8[n][:], over_t(eid[:]), over_e(t8["wheref"][:, :, k]), ALU.is_equal))
                v.tensor_tensor(t8["both"][:], t8["first"][:], t8["second"][:], ALU.add).then_inc(picked, 1)
                dve.wait_ge(counted, count(2))
                chain(v.tensor_copy(t8["tile_sum"][:], ps_c[:]))
                src, dst = "tile_sum", "run_a"
                for d in (1, 2, 4, 8):
                    chain(v.tensor_copy(t8[dst][:, 0:d], t8[src][:, 0:d]))
                    chain(v.tensor_tensor(t8[dst][:, d:], t8[src][:, d:], t8[src][:, :TILES - d], ALU.add))
                    src, dst = dst, "run_b" if dst == "run_a" else "run_a"
                chain(v.tensor_tensor(t8["ahead"][:], t8[src][:], t8["tile_sum"][:], ALU.subtract))
                chain(v.tensor_scalar(e1["tiles_f"][:], t8[src][:, TILES - 1, :], 1.0 / P, 0.5 - 0.5 / P,
                                      ALU.mult, ALU.add))
                chain(v.tensor_copy(tiles_i[:], e1["tiles_f"][:]))
                chain(v.tensor_copy(e1["tiles"][:], tiles_i[:]))
                src, dst = "tiles", "start_a"
                for d in (1, 2, 4):
                    chain(v.tensor_copy(e1[dst][:, 0:d], e1[src][:, 0:d]))
                    chain(v.tensor_tensor(e1[dst][:, d:], e1[src][:, d:], e1[src][:, :E - d], ALU.add))
                    src, dst = dst, "start_b" if dst == "start_a" else "start_a"
                chain(v.tensor_tensor(e1["start"][:], e1[src][:], e1["tiles"][:], ALU.subtract))
                chain(v.tensor_scalar(e1["start_p"][:], e1["start"][:], float(P), None, ALU.mult))
                chain(v.tensor_tensor(t8["based"][:], t8["ahead"][:], over_t(e1["start_p"][:]), ALU.add))
                chain(v.tensor_tensor(t8["slot"][:], ps_r[:], t8["based"][:], ALU.add))
                for k, n in enumerate(("first", "second")):
                    chain(v.tensor_tensor(t8[f"slot{k + 1}"][:], t8[n][:], t8["slot"][:], ALU.mult))
                    chain(v.tensor_reduce(t1[f"slot{k + 1}f"][:], t8[f"slot{k + 1}"][:], AX.X, ALU.add))
                    v.tensor_copy(slots[k][:], t1[f"slot{k + 1}f"][:]).then_inc(slots_ready, 1)
                chain(v.tensor_tensor(passed[:], tau[:].unsqueeze(2).to_broadcast([P, n_tiles, E]),
                                      e1["start"][:].unsqueeze(1).to_broadcast([P, n_tiles, E]), ALU.is_ge))
                chain(v.tensor_reduce(expert_f[:], passed[:, :, 1:E], AX.X, ALU.add))
                chain(v.tensor_copy(tile_expert[:], expert_f[:]))


def experts_stage(nc, name, ident, wts, b1, b2, tile_expert, x_slots, y_slots, weights_in):
    st = Stage(nc, name)
    n_tiles = tile_expert.shape[1]
    HALF = 512
    with st:
        x_in = st.sb("x_in", [P, 2, D], F32)
        x_t = st.sb("x_t", [P, 2, DC, P], F32)
        h = st.sb("h", [P, 2, HIDDEN], F32)
        h_t = st.sb("h_t", [P, 2, HC, P], F32)
        y = st.sb("y", [P, 2, D], F32)
        b1c = st.sb("b1c", [P, EXPERTS * HC], F32)
        b2r = st.sb("b2r", [P, EXPERTS, D], F32)
        ps_x = st.ps("x", [P, DC, P])
        ps_h = [st.ps(f"h{i}", [P, HALF]) for i in range(2)]
        ps_t = [st.ps(f"t{i}", [P, HC // 2, P]) for i in range(2)]
        ps_y = st.ps("y", [P, D])
        loaded = st.sem("loaded")
        x_loaded = [st.sem(f"x_loaded{s}") for s in range(2)]
        x_ps, x_ready = st.sem("x_ps"), st.sem("x_ready")
        h_ps, h_ready = st.sem("h_ps"), st.sem("h_ready")
        t_ps, t_ready = st.sem("t_ps"), st.sem("t_ready")
        y_ps, y_ready = st.sem("y_ps"), st.sem("y_ready")
        y_stored = [st.sem(f"y_stored{s}") for s in range(2)]
        w1, w2 = wts
        rows = lambda dram, t: dram.rearrange("(t p) d -> t p d", p=P)[t]

        st.begin()
        with nc.Block() as block:
            @block.sync
            def _(sp):
                sp.dma_start(b1c[:], b1.rearrange("e (m p) -> p (e m)", p=P)).then_inc(loaded, 16)
                sp.dma_start(b2r[:], bass.AP(tensor=b2.tensor, offset=b2.offset, ap=[[0, P], [D, EXPERTS], [1, D]])
                             ).then_inc(loaded, 16)
                for s in range(2):
                    sp.dma_start(x_in[:, s, :], rows(x_slots, s)).then_inc(x_loaded[s], 16)

                def step(t, s, u, more):
                    if more:
                        sp.wait_ge(x_ps, count(t + 1))
                        sp.dma_start(x_in[:, s, :], rows(x_slots, t + 2)).then_inc(x_loaded[s], 16)
                    sp.wait_ge(y_ready, count(t + 1))
                    sp.dma_start(rows(y_slots, t), y[:, s, :]).then_inc(y_stored[s], 16)

                with sp.Fori(0, n_tiles // 2 - 1) as u:
                    for s in range(2):
                        step(2 * u + s, s, u, True)
                for t in range(n_tiles // 2 * 2 - 2, n_tiles):
                    step(t, t % 2, t // 2, t + 2 < n_tiles)
                sp.wait_ge(y_stored[0], count(16 * ((n_tiles + 1) // 2)))
                sp.wait_ge(y_stored[1], count(16 * (n_tiles // 2)))

            @block.tensor
            def _(pe):
                def expert(t):
                    return pe.value_load(tile_expert[0:1, bass.ds(t, 1)], min_val=0, max_val=EXPERTS - 1)

                def turn_x(t, s, u):
                    pe.wait_ge(x_loaded[s], count(16 * u + 16))
                    pe.wait_ge(x_ready, count(t))
                    for c in range(DC):
                        last = nc.tensor.transpose(ps_x[:, c, :], x_in[:, s, c * P:(c + 1) * P], ident[:])
                    last.then_inc(x_ps, 1)

                def hidden(t, s, e):
                    pe.wait_ge(x_ready, count(t + 1))
                    pe.wait_ge(h_ready, count(2 * t))
                    for half in range(2):
                        for c in range(DC):
                            last = nc.tensor.matmul(
                                ps_h[half][:], x_t[:, s, c, :],
                                w1[:, bass.ds(e, 1), c, half * HALF:(half + 1) * HALF].rearrange("p a n -> p (a n)"),
                                start=c == 0, stop=c == DC - 1)
                        last.then_inc(h_ps, 1)

                def turn_h(t, s):
                    pe.wait_ge(t_ready, count(t))
                    for half in range(2):
                        pe.wait_ge(h_ready, count(2 * t + half + 1))
                        for m in range(HC // 2):
                            at = (half * HC // 2 + m) * P
                            last = nc.tensor.transpose(ps_t[half][:, m, :], h[:, s, at:at + P], ident[:])
                        last.then_inc(t_ps, 1)

                def output(t, s, e):
                    pe.wait_ge(t_ready, count(t + 1))
                    pe.wait_ge(y_ready, count(t))
                    for m in range(HC):
                        last = nc.tensor.matmul(ps_y[:], h_t[:, s, m, :],
                                                w2[:, bass.ds(e, 1), m, :].rearrange("p a n -> p (a n)"),
                                                start=m == 0, stop=m == HC - 1)
                    last.then_inc(y_ps, 1)

                pe.wait_ge(weights_in, 32 * EXPERTS)
                turn_x(0, 0, 0)
                hidden(0, 0, expert(0))
                turn_h(0, 0)
                turn_x(1, 1, 0)
                with pe.Fori(0, (n_tiles - 2) // 2) as u:
                    for s in range(2):
                        t = 2 * u + s + 1
                        hidden(t, 1 - s, expert(t))
                        output(t - 1, s, expert(t - 1))
                        turn_h(t, 1 - s)
                        turn_x(t + 1, s, u + 1)
                for t in range((n_tiles - 2) // 2 * 2 + 1, n_tiles):
                    hidden(t, t % 2, expert(t))
                    output(t - 1, (t - 1) % 2, expert(t - 1))
                    turn_h(t, t % 2)
                    if t + 1 < n_tiles:
                        turn_x(t + 1, (t + 1) % 2, (t + 1) // 2)
                output(n_tiles - 1, (n_tiles - 1) % 2, expert(n_tiles - 1))

            @block.scalar
            def _(act):
                act.wait_ge(loaded, count(32))

                def step(t, s):
                    act.wait_ge(x_ps, count(t + 1))
                    act.wait_ge(h_ps, count(2 * t))
                    nc.scalar.activation(x_t[:, s, :, :], ps_x[:], ACT.Copy).then_inc(x_ready, 1)

                def relu(t, s, after_first=True):
                    e = act.value_load(tile_expert[0:1, bass.ds(t, 1)], min_val=0, max_val=EXPERTS - 1)
                    if after_first:
                        act.wait_ge(y_ps, count(t - 1))
                    for m in range(HC):
                        if m % (HC // 2) == 0:
                            act.wait_ge(t_ps, count(2 * t + m // (HC // 2) + 1))
                        last = nc.scalar.activation(h_t[:, s, m, :], ps_t[m // (HC // 2)][:, m % (HC // 2), :],
                                                    ACT.Relu, bias=b1c[:, bass.ds(e * HC + m, 1)])
                    last.then_inc(t_ready, 1)

                step(0, 0)
                step(1, 1)
                relu(0, 0, False)
                with act.Fori(0, (n_tiles - 2) // 2) as u:
                    for s in range(2):
                        t = 2 * u + s + 1
                        step(t + 1, s)
                        relu(t, 1 - s)
                for t in range((n_tiles - 2) // 2 * 2 + 1, n_tiles):
                    if t + 1 < n_tiles:
                        step(t + 1, (t + 1) % 2)
                    relu(t, t % 2)

            @block.vector
            def _(dve):
                dve.wait_ge(loaded, count(32))

                def rows_of_hidden(t, s):
                    for half in range(2):
                        dve.wait_ge(h_ps, count(2 * t + half + 1))
                        nc.vector.tensor_copy(h[:, s, half * HALF:(half + 1) * HALF], ps_h[half][:]
                                              ).then_inc(h_ready, 1)

                def rows_of_output(t, s, u):
                    e = dve.value_load(tile_expert[0:1, bass.ds(t, 1)], min_val=0, max_val=EXPERTS - 1)
                    dve.wait_ge(y_ps, count(t + 1))
                    dve.wait_ge(y_stored[s], count(16 * u))
                    nc.vector.tensor_tensor(y[:, s, :], ps_y[:],
                                            b2r[:, bass.ds(e, 1), :].rearrange("p a n -> p (a n)"), ALU.add
                                            ).then_inc(y_ready, 1)

                rows_of_hidden(0, 0)
                with dve.Fori(0, (n_tiles - 1) // 2) as u:
                    for s in range(2):
                        t = 2 * u + s + 1
                        dve.wait_ge(t_ps, count(2 * t - 2))
                        rows_of_hidden(t, 1 - s)
                        rows_of_output(t - 1, s, u)
                for t in range((n_tiles - 1) // 2 * 2 + 1, n_tiles):
                    dve.wait_ge(t_ps, count(2 * t - 2))
                    rows_of_hidden(t, t % 2)
                    rows_of_output(t - 1, (t - 1) % 2, (t - 1) // 2)
                rows_of_output(n_tiles - 1, (n_tiles - 1) % 2, (n_tiles - 1) // 2)


def combine_stage(nc, name, slots, gates, y_slots, resid):
    st = Stage(nc, name)
    with st:
        y = [st.sb(f"y{k}", [P, TILES, D], F32) for k in range(2)]
        gathered = [st.zero_sem(f"gathered{k}") for k in range(2)]
        added = st.sem("added")
        st.begin()
        with nc.Block() as block:
            @block.gpsimd
            def _(pool):
                for k in range(2):
                    for t in range(TILES):
                        pool.indirect_dma_start(
                            out=y[k][:, t, :], out_offset=None, in_=y_slots,
                            in_offset=bass.IndirectOffsetOnAxis(ap=slots[k][:, t:t + 1], axis=0)
                        ).then_inc(gathered[k], 16)

            @block.vector
            def _(dve):
                for k in range(2):
                    dve.wait_ge(gathered[k], 16 * TILES)
                    for t in range(TILES):
                        if k:
                            dve.wait_ge(added, count(t + 1))
                        nc.vector.scalar_tensor_tensor(out=resid[:, t, :], in0=y[k][:, t, :],
                                                       scalar=gates[k][:, t:t + 1], in1=resid[:, t, :],
                                                       op0=ALU.mult, op1=ALU.add).then_inc(added, 1)


def signs_stage(nc, name, ident, resid, k0, k1, k2, s0, s1, s2, out):
    st = Stage(nc, name)
    EIGHTH = 0.125
    with st:
        norm, turn = Norm(st, FP16), Turn(st, FP16)
        xn = st.sb("xn", [P, TPS, D], F32)
        bits0 = st.sb("bits0", [P, 2, DC, HIDDEN], U8)
        bits1 = st.sb("bits1", [P, HC, HIDDEN], U8)
        bits2 = st.sb("bits2", [P, HC, D], U8)
        diff = st.sb("diff", [P, DC, HIDDEN], FP16)
        wa = st.sb("wa", [P, DC, HIDDEN], FP16)
        wb0 = st.sb("wb0", [P, HC, HIDDEN], FP16)
        wb = st.sb("wb", [P, HC, HIDDEN], FP16)
        wc = st.sb("wc", [P, HC, D], FP16)
        s_all = st.sb("s_all", [P, 3], F32)
        pos, neg = st.sb("pos", [P, 3], F32), st.sb("neg", [P, 3], F32)
        sign, size = st.sb("sign", [P, 3], F32), st.sb("size", [P, 3], F32)
        size01, factor = st.sb("size01", [P, 1], F32), st.sb("factor", [P, 1], F32)
        factor64 = st.sb("factor64", [P, 1], F32)
        ga = [st.sb(f"ga_{x}", [P, HC, SEQ], FP16) for x in ("hi", "lo")]
        gb = [st.sb(f"gb_{x}", [P, HC, SEQ], FP16) for x in ("hi", "lo")]
        rows = st.sb("rows", [P, TPS, D], F32)
        ps = [st.ps(f"layer{i}", [P, SEQ]) for i in range(4)]
        ps_y = [st.ps(f"y{i}", [P, D]) for i in range(2)]

        loaded, step, wa_r, wb_r, wc_r, factor_r = (
            st.sem(x) for x in ("loaded", "step", "wa_r", "wb_r", "wc_r", "factor_r"))
        layer_ps, hi_ready, lo_ready = (st.sem(x) for x in ("layer_ps", "hi_ready", "lo_ready"))
        y_ps, y_ready, stored = st.sem("y_ps"), st.sem("y_ready"), st.sem("stored")
        out_t = out.rearrange("b (j p) d -> b p j d", p=P)

        st.begin()
        with nc.Block() as block:
            @block.sync
            def _(sp):
                sp.dma_start(bits0[:], k0.rearrange("(h c p) n -> p h c n", h=2, p=P)).then_inc(loaded, 16)
                sp.dma_start(bits1[:], k1.rearrange("(m p) n -> p m n", p=P)).then_inc(loaded, 16)
                sp.dma_start(bits2[:], k2.rearrange("(m p) n -> p m n", p=P)).then_inc(loaded, 16)
                for i, s in enumerate((s0, s1, s2)):
                    sp.dma_start(s_all[:, i:i + 1], bass.AP(tensor=s.tensor, offset=s.offset, ap=[[0, P], [1, 1]])
                                 ).then_inc(loaded, 16)
                with sp.Fori(0, SEQS) as b:
                    sp.wait_ge(y_ready, count(TPS * b + TPS))
                    sp.dma_start(out_t[b], rows[:]).then_inc(stored, 16)
                sp.wait_ge(stored, count(16 * SEQS))

            @block.gpsimd
            def _(pool):
                norm.inverse_deviation(nc, pool)

            @block.tensor
            def _(pe):
                def layer(b, which, src, w, chunks):
                    for m in range(HC):
                        n = 2 * HC * b + HC * which + m
                        if which == 0 and m < 4:
                            pe.wait_ge(lo_ready, count(2 * HC * b))
                        else:
                            pe.wait_ge(lo_ready, count(n - 3))
                        for k in range(chunks):
                            for x in range(2):
                                last = nc.tensor.matmul(ps[m % 4][:], w[:, k, m * P:(m + 1) * P], src[x][:, k, :],
                                                        start=k == 0 and x == 0, stop=k == chunks - 1 and x == 1)
                        last.then_inc(layer_ps, 1)

                pe.wait_ge(wc_r, count(1))
                with pe.Fori(0, SEQS) as b:
                    turn.on_tensor(nc, pe, b, lambda j: xn[:, j, :], ident)
                    pe.wait_ge(turn.lo_ready, count(DC * b + DC))
                    layer(b, 0, (turn.hi, turn.lo), wa, DC)
                    pe.wait_ge(lo_ready, count(2 * HC * b + HC))
                    layer(b, 1, ga, wb, HC)
                    pe.wait_ge(lo_ready, count(2 * HC * b + 2 * HC))
                    for j in range(TPS):
                        pe.wait_ge(y_ready, count(TPS * b + max(j - 1, 0)))
                        for k in range(HC):
                            for x in range(2):
                                last = nc.tensor.matmul(ps_y[j % 2][:], gb[x][:, k, j * P:(j + 1) * P], wc[:, k, :],
                                                        start=k == 0 and x == 0, stop=k == HC - 1 and x == 1)
                        last.then_inc(y_ps, 1)

            @block.scalar
            def _(act):
                with act.Fori(0, SEQS) as b:
                    act.wait_ge(layer_ps, count(2 * HC * b))
                    turn.on_scalar(nc, act, b)
                    for which, g in enumerate((ga, gb)):
                        if which:
                            act.wait_ge(y_ps, count(TPS * b))
                        else:
                            act.wait_ge(layer_ps, count(2 * HC * b))
                        for m in range(HC):
                            act.wait_ge(layer_ps, count(2 * HC * b + HC * which + m + 1))
                            nc.scalar.activation(g[0][:, m, :], ps[m % 4][:], ACT.Relu).then_inc(hi_ready, 1)

            @block.vector
            def _(dve):
                v = nc.vector
                norm.statistics(nc, dve, resid)
                dve.wait_ge(loaded, count(96))
                done = 0

                def chain(ins):
                    nonlocal done
                    done += 1
                    ins.then_inc(step, 1)
                    dve.wait_ge(step, count(done))

                chain(v.tensor_scalar(pos[:], s_all[:], 0.0, None, ALU.is_gt))
                chain(v.tensor_scalar(neg[:], s_all[:], 0.0, None, ALU.is_lt))
                chain(v.tensor_tensor(sign[:], pos[:], neg[:], ALU.subtract))
                chain(v.tensor_tensor(size[:], sign[:], s_all[:], ALU.mult))
                chain(v.tensor_tensor(size01[:], size[:, 0:1], size[:, 1:2], ALU.mult))
                chain(v.tensor_tensor(factor[:], size01[:], s_all[:, 2:3], ALU.mult))
                v.tensor_scalar(factor64[:], factor[:], 8.0 / EIGHTH, None, ALU.mult).then_inc(factor_r, 1)
                chain(v.tensor_tensor(diff[:], bits0[:, 0], bits0[:, 1], ALU.subtract))
                v.tensor_scalar(wa[:], diff[:], sign[:, 0:1], None, ALU.mult).then_inc(wa_r, 1)
                chain(v.tensor_scalar(wb0[:], bits1[:], 2 * EIGHTH, -EIGHTH, ALU.mult, ALU.add))
                v.tensor_scalar(wb[:], wb0[:], sign[:, 1:2], None, ALU.mult).then_inc(wb_r, 1)
                v.tensor_scalar(wc[:], bits2[:], 2.0, -1.0, ALU.mult, ALU.add).then_inc(wc_r, 1)
                dve.wait_ge(norm.rstd_ready, count(1))
                dve.wait_ge(factor_r, count(1))
                with dve.Fori(0, SEQS) as b:
                    dve.wait_ge(turn.turned, count(b))
                    for j in range(TPS):
                        v.tensor_scalar(xn[:, j, :], resid[:, TPS * b + j, :], norm.mv[:, bass.ds(TPS * b + j, 1), 0],
                                        norm.rstd[:, bass.ds(TPS * b + j, 1)], ALU.subtract, ALU.mult
                                        ).then_inc(turn.row_ready, 1)
                    dve.wait_ge(layer_ps, count(2 * HC * b))
                    turn.on_vector(nc, dve, b)
                    for which, g in enumerate((ga, gb)):
                        if which:
                            dve.wait_ge(y_ps, count(TPS * b))
                        for m in range(HC):
                            dve.wait_ge(hi_ready, count(2 * HC * b + HC * which + m + 1))
                            v.scalar_tensor_tensor(out=g[1][:, m, :], in0=ps[m % 4][:], scalar=0.0, in1=g[0][:, m, :],
                                                   op0=ALU.max, op1=ALU.subtract).then_inc(lo_ready, 1)
                    dve.wait_ge(stored, count(16 * b))
                    for j in range(TPS):
                        dve.wait_ge(y_ps, count(TPS * b + j + 1))
                        v.scalar_tensor_tensor(out=rows[:, j, :], in0=ps_y[j % 2][:], scalar=factor64[:, 0:1],
                                               in1=resid[:, TPS * b + j, :], op0=ALU.mult, op1=ALU.add
                                               ).then_inc(y_ready, 1)


def constants_stage(nc, ident, neg_causal, neg_rel, rel_bias):
    st = Stage(nc, "constants")
    with st:
        rel = st.sb("rel", [P, SPAN], F32)
        made, rel_in, negated = (st.sem(x) for x in ("made", "rel_in", "negated"))
        st.begin()
        with nc.Block() as block:
            @block.sync
            def _(sp):
                sp.dma_start(rel[:], bass.AP(tensor=rel_bias.tensor, offset=rel_bias.offset, ap=[[1, P], [1, SPAN]])
                             ).then_inc(rel_in, 16)
            @block.gpsimd
            def _(pool):
                pool.memset(ident[:], 0.0).then_inc(made, 1)
                pool.memset(neg_causal[:], 0.0).then_inc(made, 1)
                pool.wait_ge(made, count(2))
                pool.affine_select(out=ident[:], in_=ident[:], compare_op=ALU.not_equal, fill=1.0, base=0,
                                   pattern=[[-1, P]], channel_multiplier=1).then_inc(made, 1)
                pool.affine_select(out=neg_causal[:], in_=neg_causal[:], compare_op=ALU.is_ge, fill=BIG,
                                   base=SEQ - P, pattern=[[-1, SEQ]], channel_multiplier=1).then_inc(made, 1)

            @block.vector
            def _(dve):
                dve.wait_ge(rel_in, count(16))
                nc.vector.tensor_scalar(neg_rel[:], rel[:, ::-1], -1.0, None, ALU.mult).then_inc(negated, 1)


def tower(nc, x, L0_tok_weight, L0_attn_Wq, L0_attn_bq, L0_attn_Wk, L0_attn_bk, L0_attn_Wv, L0_attn_bv,
          L0_attn_Wo, L0_attn_bo, L0_attn_gamma, L0_attn_beta, L0_ffn_gate_w, L0_ffn_gate_b, L0_ffn_w1,
          L0_ffn_b1, L0_ffn_w2, L0_ffn_b2, L1_attn_Wqkv, L1_attn_bqkv, L1_attn_Wout, L1_attn_bout,
          L1_attn_rel_pos_bias, L1_ffn_k0, L1_ffn_k1, L1_ffn_k2, L1_ffn_s0, L1_ffn_s1, L1_ffn_s2, out):
    n_tiles = (2 * TOKENS + EXPERTS * (P - 1)) // P
    scratch = [nc.dram_tensor(f"qk_scratch{i}", (SEQS, PARTS, 2 * D, SEQ), BF16).ap() for i in range(2)]
    x_slots = nc.dram_tensor("x_slots", (n_tiles * P, D), F32).ap()
    y_slots = nc.dram_tensor("y_slots", (n_tiles * P, D), F32).ap()
    with ExitStack() as forever:
        forever.enter_context(nc.allow_non_contiguous_dma(reason="token ids and bias columns, a few KB"))
        sb = lambda n, shape, dt: forever.enter_context(nc.sbuf_tensor(n, shape, dt))
        resid = sb("resid", [P, TILES, D], F32)
        ident = sb("ident", [P, P], F32)
        neg_causal = sb("neg_causal", [P, SEQ], F32)
        neg_rel = sb("neg_rel", [P, SPAN], F32)

        constants_stage(nc, ident, neg_causal, neg_rel, L1_attn_rel_pos_bias)
        embed_stage(nc, x, L0_tok_weight, resid, x_slots)

        heads_out = sb("heads_out", [P, SEQS * HEADS, TPS, VC], F32)

        def attention(name, i, w_parts, b_qk, b_v, neg_bias, causal):
            with nc.sbuf_tensor(f"{name}_v_parts", [P, TILES, HEADS, PARTS, VC], BF16) as v_parts:
                qkv_stage(nc, f"{name}_qkv", ident, resid, w_parts, b_qk, b_v, scratch[i], v_parts)
                attention_stage(nc, f"{name}_core", ident, neg_bias, causal, scratch[i], v_parts, heads_out)

        attention("attn0", 0, [L0_attn_Wq, L0_attn_Wk, L0_attn_Wv], [L0_attn_bq, L0_attn_bk], L0_attn_bv,
                  neg_causal, True)

        slots = [sb(f"slots{k}", [P, TILES], U32) for k in range(2)]
        gates = [sb(f"gates{k}", [P, TILES], F32) for k in range(2)]
        tile_expert = sb("tile_expert", [P, n_tiles], mybir.dt.int32)
        weights_in = forever.enter_context(nc.semaphore("weights_in"))
        with ExitStack() as ctx:
            wts = [ctx.enter_context(nc.sbuf_tensor("w1_all", [P, EXPERTS, DC, HIDDEN], F32)),
                   ctx.enter_context(nc.sbuf_tensor("w2_all", [P, EXPERTS, HC, D], F32))]
            loads = [(on_chip[:, e], w[e].rearrange("(c p) n -> p c n", p=P), weights_in)
                     for e in range(EXPERTS) for on_chip, w in zip(wts, (L0_ffn_w1, L0_ffn_w2))]
            rows_out_stage(nc, "attn0_out", ident, heads_out, L0_attn_Wo, L0_attn_bo, True, L0_attn_gamma,
                           L0_attn_beta, resid, prefetch=loads)
            route_stage(nc, "route", ident, resid, L0_ffn_gate_w, L0_ffn_gate_b, slots, gates, tile_expert, x_slots)
            experts_stage(nc, "experts", ident, wts, L0_ffn_b1, L0_ffn_b2, tile_expert, x_slots, y_slots,
                          weights_in)
        combine_stage(nc, "combine", slots, gates, y_slots, resid)

        attention("attn1", 1, [L1_attn_Wqkv], [L1_attn_bqkv[0:2 * D]], L1_attn_bqkv[2 * D:3 * D], neg_rel, False)
        rows_out_stage(nc, "attn1_out", ident, heads_out, L1_attn_Wout, L1_attn_bout, False, None, None, resid)
        signs_stage(nc, "signs", ident, resid, L1_ffn_k0, L1_ffn_k1, L1_ffn_k2, L1_ffn_s0, L1_ffn_s1, L1_ffn_s2, out)


_INS = ["x", "L0_tok_weight", "L0_attn_Wq", "L0_attn_bq", "L0_attn_Wk", "L0_attn_bk", "L0_attn_Wv", "L0_attn_bv",
        "L0_attn_Wo", "L0_attn_bo", "L0_attn_gamma", "L0_attn_beta", "L0_ffn_gate_w", "L0_ffn_gate_b", "L0_ffn_w1",
        "L0_ffn_b1", "L0_ffn_w2", "L0_ffn_b2", "L1_attn_Wqkv", "L1_attn_bqkv", "L1_attn_Wout", "L1_attn_bout",
        "L1_attn_rel_pos_bias", "L1_ffn_k0", "L1_ffn_k1", "L1_ffn_k2", "L1_ffn_s0", "L1_ffn_s1", "L1_ffn_s2"]


def kernel(**inputs):
    import numpy as _np
    import concourse.bacc as _bacc
    from concourse import mybir as _mybir
    from concourse.bass_utils import run_bass_kernel_spmd as _run

    nc = _bacc.Bacc("TRN2", target_bir_lowering=False, num_devices=1)
    arrays, args = {}, []
    for name in _INS:
        a = _np.ascontiguousarray(inputs[name])
        if a.ndim == 0:
            a = a.reshape(1)
        arrays[f"in_{name}"] = a
        args.append(nc.dram_tensor(f"in_{name}", a.shape, _mybir.dt.from_np(a.dtype), kind="ExternalInput").ap())
    out = nc.dram_tensor("out_0", (SEQS, SEQ, D), _mybir.dt.float32, kind="ExternalOutput").ap()
    tower(nc, *args, out)
    r = _run(nc, [arrays], core_ids=[0])
    return r.results[0]["out_0"]
```

```python
from contextlib import ExitStack

import concourse.bass as bass
from concourse import mybir

P = 128
SEQS, SEQ, D = 4, 512, 256
TOKENS = SEQS * SEQ
TILES = TOKENS // P
TPS = SEQ // P
DC = D // P
HEADS, HD = 16, 16
PAIRS = TPS // 2
EXPERTS, HIDDEN = 8, 1024
HC = HIDDEN // P
LN_EPS = 1e-5
PARTS = 3
VC = HD + 1
Q_PARTS = (0, 1, 0, 1, 2, 0)
K_PARTS = (0, 0, 1, 1, 0, 2)
STACK = len(Q_PARTS) * HD
SPAN = SEQ + SEQ - P
BIG = 3.0e38
BANK = 512

ALU = mybir.AluOpType
ACT = mybir.ActivationFunctionType
AX = mybir.AxisListType
F32 = mybir.dt.float32
F32R = mybir.dt.float32r
BF16 = mybir.dt.bfloat16
FP16 = mybir.dt.float16
U32 = mybir.dt.uint32
U8 = mybir.dt.uint8

PRODUCTS = ((0, 0), (1, 0), (0, 1))


def row_on_all_partitions(v, n):
    return bass.AP(tensor=v.tensor, offset=v.offset, ap=[[0, P], [1, n]])


def count(n):
    return n + 1


class Stage:

    def __init__(self, nc, name):
        self.nc, self.name = nc, name
        self.ctx, self.sems, self.zero_sems = ExitStack(), [], []

    def __enter__(self):
        return self

    def __exit__(self, kind, value, trace):
        self.ctx.close()
        if kind is None:
            self.nc.clear_and_free_semaphores(self.sems + self.zero_sems)

    def begin(self):
        for s in self.sems:
            self.nc.gpsimd.sem_inc(s, 1)
        self.nc.all_engine_barrier()

    def sb(self, name, shape, dt):
        return self.ctx.enter_context(self.nc.sbuf_tensor(f"{self.name}_{name}", shape, dt))

    def ps(self, name, shape):
        bank = self.ctx.enter_context(self.nc.psum_tensor(f"{self.name}_ps_{name}", [P, BANK], F32))
        n = 1
        for k in shape[1:]:
            n *= k
        view = bank[0:shape[0], 0:n]
        if len(shape) == 2:
            return view
        names = "abcd"[:len(shape) - 1]
        return view.rearrange(f"p ({' '.join(names)}) -> p {' '.join(names)}", **dict(zip(names, shape[1:])))

    def sem(self, name):
        self.sems.append(self.nc.alloc_semaphore(name=f"{self.name}_{name}"))
        return self.sems[-1]

    def zero_sem(self, name):
        self.zero_sems.append(self.nc.alloc_semaphore(name=f"{self.name}_{name}"))
        return self.zero_sems[-1]


def embed_stage(nc, ids, table, resid, rel_bias, ident, neg_causal, neg_rel):
    st = Stage(nc, "embed")
    rows, _ = table.shape
    per = rows * D // P
    SLOTS, PIECE = 4, 4000
    pieces = per // PIECE
    rounds = pieces // SLOTS
    with st:
        ring = st.sb("ring", [P, SLOTS, PIECE], F32)
        junk = st.sb("junk", [P, PIECE], BF16)
        idx = st.sb("idx", [P, TILES], U32)
        part = st.sb("part", [P, rounds, SLOTS], F32)
        total = st.sb("total", [P, 1], F32)
        ones = st.sb("ones", [P, P], F32)
        mean = st.sb("mean", [P, 1], F32)
        rel = st.sb("rel", [P, SPAN], F32)
        scale = st.sb("scale", [P, 1], F32)
        step = st.sb("step", [P, 1], F32)
        scaled = st.sb("scaled", [P, 2, TPS, D], F32)
        below = st.sb("below", [P, 2, TPS, D], F32)
        tern = st.sb("tern", [P, 2, TPS, D], F32)
        pmean = st.ps("pmean", [P, 1])

        piece_in = [st.sem(f"piece_in{s}") for s in range(SLOTS)]
        ids_in = st.sem("ids_in")
        made, rel_in, negated = (st.sem(x) for x in ("made", "rel_in", "negated"))
        gathered = st.zero_sem("gathered")
        act_summed = st.sem("act_summed")
        dve_summed = st.sem("dve_summed")
        ones_set = st.sem("ones_set")
        total_ready = st.sem("total_ready")
        mean_ps = st.sem("mean_ps")
        chain = st.sem("chain")
        scaled_ready = st.sem("scaled_ready")
        tern_ready = st.sem("tern_ready")
        rows_done = st.sem("rows_done")

        pieces_of = table.rearrange("(p r) d -> p (r d)", p=P).rearrange(
            "p (i s n) -> p i s n", s=SLOTS, n=PIECE)
        chunk = lambda b: resid[:, b * TPS:(b + 1) * TPS, :]

        st.begin()
        with nc.Block() as block:
            @block.sync
            def _(sp):
                sp.dma_start(idx[:].bitcast(ids.dtype), ids.rearrange("b (t p) -> p (b t)", p=P),
                             ).then_inc(ids_in, 16)
                for s in range(SLOTS):
                    sp.dma_start(ring[:, s, :], pieces_of[:, 0, s, :]).then_inc(piece_in[s], 16)
                sp.dma_start(rel[:], bass.AP(tensor=rel_bias.tensor, offset=rel_bias.offset, ap=[[1, P], [1, SPAN]])
                             ).then_inc(rel_in, 16)
                with sp.Fori(1, rounds) as i:
                    for s in range(SLOTS):
                        sp.wait_ge(act_summed if s % 2 == 0 else dve_summed, count(2 * i - 1 + s // 2))
                        sp.dma_start(ring[:, s, :], pieces_of[:, i, s, :]).then_inc(piece_in[s], 16)

            @block.gpsimd
            def _(pool):
                pool.memset(ones[:], 1.0).then_inc(ones_set, 1)
                pool.wait_ge(ids_in, count(16))
                for t in range(TILES):
                    pool.indirect_dma_start(out=resid[:, t, :], out_offset=None, in_=table,
                                            in_offset=bass.IndirectOffsetOnAxis(ap=idx[:, t:t + 1], axis=0)
                                            ).then_inc(gathered, 16)
                pool.memset(ident[:], 0.0).then_inc(made, 1)
                pool.memset(neg_causal[:], 0.0).then_inc(made, 1)
                pool.wait_ge(made, count(2))
                pool.affine_select(out=ident[:], in_=ident[:], compare_op=ALU.not_equal, fill=1.0, base=0,
                                   pattern=[[-1, P]], channel_multiplier=1).then_inc(made, 1)
                pool.affine_select(out=neg_causal[:], in_=neg_causal[:], compare_op=ALU.is_ge, fill=BIG,
                                   base=SEQ - P, pattern=[[-1, SEQ]], channel_multiplier=1).then_inc(made, 1)
                pool.wait_ge(gathered, 16 * TILES)

            @block.scalar
            def _(act):
                with act.Fori(0, rounds) as i:
                    for s in (0, 2):
                        act.wait_ge(piece_in[s], count(16 * i + 16))
                        if s == 2:
                            act.wait_ge(act_summed, count(2 * i + 1))
                        else:
                            act.wait_ge(act_summed, count(2 * i))
                        nc.scalar.activation(junk[:], ring[:, s, :], ACT.Abs,
                                             accum_out=part[:, i, s:s + 1]).then_inc(act_summed, 1)
                act.wait_ge(chain, count(4))
                act.wait_ge(gathered, 16 * TILES)
                for b in range(SEQS + 1):
                    if b < SEQS:
                        if b >= 2:
                            act.wait_ge(tern_ready, count(b - 1))
                        nc.scalar.activation(scaled[:, b % 2], chunk(b), ACT.Copy, scale=scale[:, 0:1]
                                             ).then_inc(scaled_ready, 1)
                    if b:
                        act.wait_ge(tern_ready, count(b))
                        nc.scalar.activation(chunk(b - 1), tern[:, (b - 1) % 2], ACT.Copy, scale=step[:, 0:1]
                                             ).then_inc(rows_done, 1)

            @block.vector
            def _(dve):
                with dve.Fori(0, rounds) as i:
                    for s in (1, 3):
                        dve.wait_ge(piece_in[s], count(16 * i + 16))
                        nc.vector.tensor_reduce(part[:, i, s:s + 1], ring[:, s, :], AX.X, ALU.add,
                                                apply_absolute_value=True).then_inc(dve_summed, 1)
                dve.wait_ge(dve_summed, count(2 * rounds))
                dve.wait_ge(act_summed, count(2 * rounds))
                nc.vector.tensor_reduce(total[:], part[:], AX.XY, ALU.add).then_inc(total_ready, 1)
                dve.wait_ge(rel_in, count(16))
                nc.vector.tensor_scalar(neg_rel[:], rel[:, ::-1], -1.0, None, ALU.mult).then_inc(negated, 1)
                dve.wait_ge(mean_ps, count(1))
                nc.vector.tensor_scalar(mean[:], pmean[:], 1.0 / (rows * D), None, ALU.mult
                                        ).then_inc(chain, 1)
                dve.wait_ge(chain, count(1))
                nc.vector.tensor_scalar(total[:], mean[:], LN_EPS, None, ALU.max).then_inc(chain, 1)
                dve.wait_ge(chain, count(2))
                nc.vector.reciprocal(scale[:], total[:]).then_inc(chain, 1)
                dve.wait_ge(chain, count(3))
                nc.vector.reciprocal(step[:], scale[:]).then_inc(chain, 1)
                for b in range(SEQS):
                    dve.wait_ge(scaled_ready, count(b + 1))
                    nc.vector.tensor_scalar(below[:, b % 2], scaled[:, b % 2], -0.5, None, ALU.is_lt
                                            ).then_inc(chain, 1)
                    dve.wait_ge(chain, count(5 + b))
                    if b >= 2:
                        dve.wait_ge(rows_done, count(b - 1))
                    nc.vector.scalar_tensor_tensor(out=tern[:, b % 2], in0=scaled[:, b % 2], scalar=0.5,
                                                   in1=below[:, b % 2], op0=ALU.is_gt, op1=ALU.subtract
                                                   ).then_inc(tern_ready, 1)

            @block.tensor
            def _(pe):
                pe.wait_ge(ones_set, count(1))
                pe.wait_ge(total_ready, count(1))
                nc.tensor.matmul(pmean[:], ones[:], total[:], start=True, stop=True).then_inc(mean_ps, 1)


class Norm:

    def __init__(self, st):
        self.minus_half = st.sb("minus_half", [P, 1], F32)
        self.stats = st.sb("stats", [P, TILES, 6], F32)
        self.mv = st.sb("mv", [P, TILES, 2], F32)
        self.var_eps = st.sb("var_eps", [P, TILES], F32)
        self.rstd = st.sb("rstd", [P, TILES], F32)
        self.stats_ready = st.sem("stats_ready")
        self.mv_ready = st.sem("mv_ready")
        self.pool_step = st.sem("pool_step")
        self.rstd_ready = st.sem("rstd_ready")

    def statistics(self, nc, dve, x, b):
        seq = range(TPS * b, TPS * b + TPS)
        for t in seq:
            nc.vector.bn_stats(self.stats[:, t, :], x(t)).then_inc(self.stats_ready, 1)
        for t in seq:
            dve.wait_ge(self.stats_ready, count(t + 1))
            nc.vector.bn_aggr(self.mv[:, t, :], self.stats[:, t, :]).then_inc(self.mv_ready, 1)

    def inverse_deviation(self, nc, pool):
        nc.gpsimd.memset(self.minus_half[:], -0.5).then_inc(self.pool_step, 1)
        for b in range(SEQS):
            seq = slice(TPS * b, TPS * b + TPS)
            pool.wait_ge(self.mv_ready, count(TPS * b + TPS))
            nc.gpsimd.tensor_scalar(self.var_eps[:, seq], self.mv[:, seq, 1], LN_EPS, None, ALU.add
                                    ).then_inc(self.pool_step, 1)
            pool.wait_ge(self.pool_step, count(b + 2))
            nc.gpsimd.tensor_tensor(self.rstd[:, seq], self.var_eps[:, seq],
                                    self.minus_half[:, 0:1].to_broadcast([P, TPS]), ALU.pow
                                    ).then_inc(self.rstd_ready, 1)

    def rows(self, nc, dve, x, xn, b, ready):
        for j in range(TPS):
            nc.vector.tensor_scalar(xn(j), x[:, TPS * b + j, :], self.mv[:, bass.ds(TPS * b + j, 1), 0],
                                    self.rstd[:, bass.ds(TPS * b + j, 1)], ALU.subtract, ALU.mult
                                    ).then_inc(ready, 1)


class Turn:

    def __init__(self, st, dt):
        self.dt = dt
        self.ps = [st.ps(f"turned{c}", [P, SEQ]) for c in range(DC)]
        self.hi = st.sb("x_hi", [P, DC, SEQ], dt)
        self.lo = st.sb("x_lo", [P, DC, SEQ], dt)
        self.row_ready = st.sem("row_ready")
        self.turned = st.sem("x_turned")
        self.hi_ready = st.sem("x_hi_ready")
        self.lo_ready = st.sem("x_lo_ready")

    def plain(self, x):
        return x.bitcast(F32) if self.dt == F32R else x

    def on_tensor(self, nc, pe, b, rows, ident):
        pe.wait_ge(self.lo_ready, count(DC * b))
        for j in range(TPS):
            pe.wait_ge(self.row_ready, count(TPS * b + j + 1))
            for c in range(DC):
                last = nc.tensor.transpose(self.ps[c][:, j * P:(j + 1) * P],
                                           rows(j)[:, c * P:(c + 1) * P], ident[:])
        last.then_inc(self.turned, 1)

    def on_scalar(self, nc, act, b):
        act.wait_ge(self.turned, count(b + 1))
        for c in range(DC):
            nc.scalar.activation(self.hi[:, c, :], self.ps[c][:], ACT.Copy).then_inc(self.hi_ready, 1)

    def on_vector(self, nc, dve, b):
        for c in range(DC):
            dve.wait_ge(self.hi_ready, count(DC * b + c + 1))
            nc.vector.tensor_tensor(self.lo[:, c, :], self.ps[c][:], self.plain(self.hi[:, c, :]),
                                    ALU.subtract).then_inc(self.lo_ready, 1)


def qkv_stage(nc, name, ident, resid, w_parts, b_qk, b_v, qk_scratch, v_parts, stacks):
    st = Stage(nc, name)
    QK = 2 * D // P
    with st:
        norm, turn = Norm(st), Turn(st, F32R)
        wf = st.sb("wf", [P, DC, 3 * D], F32)
        w_hi = st.sb("w_hi", [P, DC, 3 * D], F32R)
        w_lo = st.sb("w_lo", [P, DC, 3 * D], F32R)
        bias = st.sb("bias", [P, QK], F32)
        bias_q = st.sb("bias_q", [P, QK], F32)
        bv = st.sb("bv", [P, D], F32)
        xn = st.sb("xn", [P, TPS, D], F32)
        full = st.sb("full", [P, 2, SEQ], F32)
        rest = st.sb("rest", [P, 2, SEQ], F32)
        qk_parts = st.sb("qk_parts", [P, QK, PARTS, SEQ], BF16)
        v_full = st.sb("v_full", [P, 2, D], F32)
        v_rest = st.sb("v_rest", [P, 2, D], F32)
        ps_qk = [st.ps(f"qk{m}", [P, SEQ]) for m in range(QK)]
        ps_v = [st.ps(f"v{i}", [P, D]) for i in range(2)] + [bank[:, 0:D] for bank in ps_qk[2:]]

        loaded, ones_set = st.sem("loaded"), st.sem("ones_set")
        bias_scaled = st.sem("bias_scaled")
        w_hi_ready, w_lo_ready = st.sem("w_hi_ready"), st.sem("w_lo_ready")
        qk_ps, v_ps = st.sem("qk_ps"), st.sem("v_ps")
        qk_full, qk_hi, qk_rest, qk_mid, qk_lo = (
            st.sem(f"qk_{s}") for s in ("full", "hi", "rest", "mid", "lo"))
        v_fulls, v_hi, v_rests, v_mid, v_lo = (
            st.sem(f"v_{s}") for s in ("fulls", "hi", "rests", "mid", "lo"))
        stored = [st.sem(f"stored{m}") for m in range(QK)]
        n_loads = len(w_parts) + len(b_qk) + 1

        out_of = qk_scratch.rearrange("b s (m p) t -> b m p s t", p=P)

        st.begin()
        with nc.Block() as block:
            @block.sync
            def _(sp):
                at = 0
                for w in w_parts:
                    n = w.shape[1]
                    sp.dma_start(wf[:, :, at:at + n], w.rearrange("(c p) n -> p c n", p=P)).then_inc(loaded, 16)
                    at += n
                at = 0
                for v in b_qk:
                    m = v.shape[0] // P
                    sp.dma_start(bias[:, at:at + m], v.rearrange("(m p) -> p m", p=P)).then_inc(loaded, 16)
                    at += m
                sp.dma_start(bv[:], row_on_all_partitions(b_v, D)).then_inc(loaded, 16)
                for b in range(SEQS):
                    for m in range(QK):
                        sp.wait_ge(qk_lo, count(QK * b + m + 1))
                        sp.dma_start(out_of[b, m], qk_parts[:, m]).then_inc(stored[m], 16)
                        if 1 <= b <= 2:
                            sp.wait_ge(stored[m], count(16 * b))
                    if 1 <= b <= 2:
                        stacks.load(sp, b - 1)
                for s in stored:
                    sp.wait_ge(s, count(16 * SEQS))

            @block.gpsimd
            def _(pool):
                norm.inverse_deviation(nc, pool)
                for x in range(PARTS):
                    nc.gpsimd.memset(v_parts[:, :, :, x, HD], 1.0 if x == 0 else 0.0).then_inc(ones_set, 1)

            @block.tensor
            def _(pe):
                turn.on_tensor(nc, pe, 0, lambda j: xn[:, j, :], ident)
                pe.wait_ge(w_lo_ready, count(1))

                def project(b, more):
                    pe.wait_ge(turn.lo_ready, count(DC * b + DC))
                    pe.wait_ge(v_fulls, count(TPS * b))
                    for j in range(TPS):
                        if j == 2:
                            pe.wait_ge(qk_full, count(QK * b))
                        n = 0
                        for pw, px in PRODUCTS:
                            for c in range(DC):
                                x = (turn.hi, turn.lo)[px][:, c, j * P:(j + 1) * P]
                                last = nc.tensor.matmul(ps_v[j][:], x, (w_hi, w_lo)[pw][:, c, 2 * D:3 * D],
                                                        start=n == 0, stop=n == 3 * DC - 1)
                                n += 1
                        last.then_inc(v_ps, 1)
                    for m in range(QK):
                        if m == 2:
                            if more:
                                turn.on_tensor(nc, pe, b + 1, lambda j: xn[:, j, :], ident)
                            pe.wait_ge(v_fulls, count(TPS * b + TPS))
                        n = 0
                        for pw, px in PRODUCTS:
                            for c in range(DC):
                                w = (w_hi, w_lo)[pw][:, c, m * P:(m + 1) * P]
                                last = nc.tensor.matmul(ps_qk[m][:], w, (turn.hi, turn.lo)[px][:, c, :],
                                                        start=n == 0, stop=n == 3 * DC - 1)
                                n += 1
                        last.then_inc(qk_ps, 1)

                with pe.Fori(0, SEQS - 1) as b:
                    project(b, True)
                project(SEQS - 1, False)

            @block.scalar
            def _(act):
                act.wait_ge(loaded, count(16 * n_loads))
                nc.scalar.activation(w_hi[:], wf[:], ACT.Copy).then_inc(w_hi_ready, 1)
                nc.scalar.activation(bias_q[:, 0:DC], bias[:, 0:DC], ACT.Copy, scale=-0.25).then_inc(bias_scaled, 1)
                nc.scalar.activation(bias_q[:, DC:QK], bias[:, DC:QK], ACT.Copy).then_inc(bias_scaled, 1)
                act.wait_ge(bias_scaled, count(2))
                turn.on_scalar(nc, act, 0)

                def evacuate(b, more):
                    def full_and_high(m):
                        k = m % 2
                        act.wait_ge(qk_ps, count(QK * b + m + 1))
                        act.wait_ge(qk_rest, count(QK * b + max(m - 1, 0)))
                        nc.scalar.activation(full[:, k, :], ps_qk[m][:], ACT.Identity, bias=bias_q[:, m:m + 1],
                                             scale=-0.25 if m < DC else 1.0).then_inc(qk_full, 1)
                        act.wait_ge(qk_full, count(QK * b + m + 1))
                        act.wait_ge(stored[m], count(16 * b))
                        nc.scalar.activation(qk_parts[:, m, 0, :], full[:, k, :], ACT.Copy).then_inc(qk_hi, 1)

                    def middle(m):
                        act.wait_ge(qk_rest, count(QK * b + m + 1))
                        nc.scalar.activation(qk_parts[:, m, 1, :], rest[:, m % 2, :], ACT.Copy).then_inc(qk_mid, 1)

                    heads = lambda x: x.rearrange("p (h d) -> p h d", d=HD)

                    def v_high(j):
                        act.wait_ge(v_fulls, count(TPS * b + j + 1))
                        nc.scalar.activation(v_parts[:, TPS * b + j, :, 0, 0:HD], heads(v_full[:, j % 2, :]), ACT.Copy
                                             ).then_inc(v_hi, 1)

                    def v_middle(j):
                        act.wait_ge(v_rests, count(TPS * b + j + 1))
                        nc.scalar.activation(v_parts[:, TPS * b + j, :, 1, 0:HD], heads(v_rest[:, j % 2, :]), ACT.Copy
                                             ).then_inc(v_mid, 1)

                    for j in range(TPS + 1):
                        if j < TPS:
                            v_high(j)
                        if j:
                            v_middle(j - 1)
                    for m in range(QK + 1):
                        if more and m == QK - 2:
                            act.wait_ge(qk_ps, count(QK * b + QK))
                            turn.on_scalar(nc, act, b + 1)
                        if m < QK:
                            full_and_high(m)
                        if m:
                            middle(m - 1)

                with act.Fori(0, SEQS - 1) as b:
                    evacuate(b, True)
                evacuate(SEQS - 1, False)

            @block.vector
            def _(dve):
                tile = lambda t: resid[:, t, :]

                def normalise(b):
                    dve.wait_ge(turn.turned, count(b))
                    norm.rows(nc, dve, resid, lambda j: xn[:, j, :], b, turn.row_ready)

                norm.statistics(nc, dve, tile, 0)
                norm.statistics(nc, dve, tile, 1)
                dve.wait_ge(norm.rstd_ready, count(1))
                normalise(0)
                dve.wait_ge(w_hi_ready, count(1))
                nc.vector.tensor_tensor(w_lo[:], wf[:], w_hi[:].bitcast(F32), ALU.subtract).then_inc(w_lo_ready, 1)
                turn.on_vector(nc, dve, 0)
                norm.statistics(nc, dve, tile, 2)
                norm.statistics(nc, dve, tile, 3)
                dve.wait_ge(norm.rstd_ready, count(SEQS))

                def evacuate(b, more):
                    def remainder(m):
                        dve.wait_ge(qk_hi, count(QK * b + m + 1))
                        dve.wait_ge(qk_lo, count(QK * b + max(m - 1, 0)))
                        nc.vector.tensor_tensor(rest[:, m % 2, :], full[:, m % 2, :], qk_parts[:, m, 0, :],
                                                ALU.subtract).then_inc(qk_rest, 1)

                    def lowest(m):
                        dve.wait_ge(qk_mid, count(QK * b + m + 1))
                        nc.vector.tensor_tensor(qk_parts[:, m, 2, :], rest[:, m % 2, :], qk_parts[:, m, 1, :],
                                                ALU.subtract).then_inc(qk_lo, 1)

                    heads = lambda x: x.rearrange("p (h d) -> p h d", d=HD)

                    def v_whole(j):
                        dve.wait_ge(v_ps, count(TPS * b + j + 1))
                        dve.wait_ge(v_rests, count(TPS * b + max(j - 1, 0)))
                        nc.vector.tensor_tensor(v_full[:, j % 2, :], ps_v[j][:], bv[:], ALU.add
                                                ).then_inc(v_fulls, 1)

                    def v_remainder(j):
                        dve.wait_ge(v_hi, count(TPS * b + j + 1))
                        dve.wait_ge(v_lo, count(TPS * b + max(j - 1, 0)))
                        nc.vector.tensor_tensor(heads(v_rest[:, j % 2, :]), heads(v_full[:, j % 2, :]),
                                                v_parts[:, TPS * b + j, :, 0, 0:HD], ALU.subtract).then_inc(v_rests, 1)

                    def v_lowest(j):
                        dve.wait_ge(v_mid, count(TPS * b + j + 1))
                        nc.vector.tensor_tensor(v_parts[:, TPS * b + j, :, 2, 0:HD], heads(v_rest[:, j % 2, :]),
                                                v_parts[:, TPS * b + j, :, 1, 0:HD], ALU.subtract).then_inc(v_lo, 1)

                    if more:
                        normalise(b + 1)
                    for j in range(TPS + 2):
                        if j < TPS:
                            v_whole(j)
                        if 1 <= j <= TPS:
                            v_remainder(j - 1)
                        if j >= 2:
                            v_lowest(j - 2)
                    for m in range(QK + 1):
                        if more and m == QK - 2:
                            dve.wait_ge(qk_ps, count(QK * b + QK))
                            turn.on_vector(nc, dve, b + 1)
                        if m < QK:
                            remainder(m)
                        if m:
                            lowest(m - 1)

                with dve.Fori(0, SEQS - 1) as b:
                    evacuate(b, True)
                evacuate(SEQS - 1, False)


class Stacks:
    LOADS = 2 * len(Q_PARTS)

    def __init__(self, nc, ctx, name, qk_scratch):
        self.q, self.k = ([ctx.enter_context(nc.sbuf_tensor(f"{name}_{x}{s}", [STACK, HEADS, SEQ], BF16))
                           for s in range(2)] for x in "qk")
        self.arrived = [ctx.enter_context(nc.semaphore(f"{name}_stack_in{s}")) for s in range(2)]
        self.scratch = qk_scratch

    def load(self, sp, b):
        for r, (pq, pk) in enumerate(zip(Q_PARTS, K_PARTS)):
            rows = slice(r * HD, (r + 1) * HD)
            for stack, part, at in ((self.q, pq, 0), (self.k, pk, D)):
                sp.dma_start(stack[b % 2][rows], self.scratch[b, part, at:at + D].rearrange("(h d) t -> d h t", d=HD)
                             ).then_inc(self.arrived[b % 2], 16)

    def wait(self, pe, b):
        pe.wait_ge(self.arrived[b % 2], 16 * self.LOADS * (b // 2 + 1))


def attention_stage(nc, name, ident, neg_bias, causal, stacks, v_parts, heads_out):
    st = Stage(nc, name)
    width = [(tile + 1) * P if causal else SEQ for tile in range(TPS)]
    ALL_HEADS = SEQS * HEADS
    with st:
        q, k = stacks.q, stacks.k
        neg = st.sb("neg", [P, TPS, SEQ], F32)
        row_min = st.sb("row_min", [P, TPS], F32)
        prob = st.sb("prob", [P, TPS, SEQ], F32)
        pt_hi = st.sb("pt_hi", [P, TPS, SEQ], FP16)
        pt_lo = st.sb("pt_lo", [P, TPS, SEQ], FP16)
        raw = st.sb("raw", [P, PAIRS, 2, PARTS, VC], F32)
        settle = st.sb("settle", [P, TPS], F32)
        two_parts = st.sb("two_parts", [P, PAIRS, 2, VC], F32)
        ps_s = [st.ps(f"s{i}", [P, SEQ]) for i in range(2)]
        ps_t = [st.ps(f"t{i}", [P, SEQ]) for i in range(TPS)]
        ps_o = [st.ps(f"o{i}", [P, 2, PARTS * VC]) for i in range(PAIRS)]

        scored = st.sem("scored")
        lowered = st.sem("lowered")
        exped = st.sem("exped")
        turned = st.sem("turned")
        hi_ready, lo_ready = st.sem("hi_ready"), st.sem("lo_ready")
        mixed = [st.sem(f"mixed{i}") for i in range(TPS)]
        left = [st.sem(f"left{p}") for p in range(PAIRS)]
        added = [st.sem(f"added{p}") for p in range(PAIRS)]
        summed = [st.sem(f"summed{p}") for p in range(PAIRS)]

        st.begin()
        with nc.Block() as block:
            @block.sync
            def _(sp):
                for b in range(2, SEQS):
                    sp.wait_ge(scored, count(TPS * HEADS * (b - 1)))
                    stacks.load(sp, b)

            @block.tensor
            def _(pe):
                def score(s, h, i):
                    nc.tensor.matmul(ps_s[i % 2][:, 0:width[i]], q[s][:, h, i * P:(i + 1) * P],
                                     k[s][:, h, 0:width[i]], start=True, stop=True).then_inc(scored, 1)

                def turn(n, i):
                    pe.wait_ge(exped, count(n + 1))
                    for kt in range(width[i] // P):
                        last = nc.tensor.transpose(ps_t[i][:, kt * P:(kt + 1) * P],
                                                   prob[:, i, kt * P:(kt + 1) * P], ident[:])
                    last.then_inc(turned, 1)

                def mix(b, g, h, i):
                    if i % 2 == 0:
                        pe.wait_ge(left[i // 2], count(g))
                    pe.wait_ge(lo_ready, count(TPS * g + i + 1))
                    tiles = width[i] // P
                    for kt in range(tiles):
                        for x, part in enumerate((pt_hi, pt_lo)):
                            last = nc.tensor.matmul(
                                ps_o[i // 2][:, i % 2], part[:, i, kt * P:(kt + 1) * P],
                                v_parts[:, TPS * b + kt, h].rearrange("p s d -> p (s d)"),
                                start=kt == 0 and x == 0, stop=kt == tiles - 1 and x == 1)
                    last.then_inc(mixed[i], 1)

                def step(b, h, i, scored_b, scored_h, turns=True):
                    g = HEADS * b + h
                    n = TPS * g + i
                    if turns:
                        turn(n + 2, (i + 2) % TPS)
                    if scored_b < SEQS:
                        pe.wait_ge(lowered, count(n + 4))
                        score(scored_b % 2, scored_h, (i + 1) % TPS)
                    mix(b, g, h, i)

                stacks.wait(pe, 0)
                for n in range(5):
                    if n >= 2:
                        pe.wait_ge(lowered, count(n - 1))
                    score(0, n // TPS, n % TPS)
                for i in range(2):
                    turn(i, i)
                for b in range(SEQS):
                    with pe.Fori(0, HEADS - 2) as h:
                        for i in range(TPS):
                            step(b, h, i, b, h + 1 + (i + 1) // TPS)
                    for h in range(HEADS - 2, HEADS):
                        for i in range(TPS):
                            ahead = HEADS * b + h + 1 + (i + 1) // TPS
                            if ahead == HEADS * (b + 1) and i == TPS - 1 and b + 1 < SEQS:
                                stacks.wait(pe, b + 1)
                            step(b, h, i, ahead // HEADS, ahead % HEADS,
                                 turns=TPS * (HEADS * b + h) + i + 2 < TPS * ALL_HEADS)

            @block.scalar
            def _(act):
                def exponential(n, i):
                    act.wait_ge(lowered, count(n + 1))
                    nc.scalar.activation(prob[:, i, 0:width[i]], neg[:, i, 0:width[i]], ACT.Exp,
                                         bias=row_min[:, i:i + 1], scale=-1.0).then_inc(exped, 1)

                def high(g, i):
                    act.wait_ge(turned, count(TPS * g + i + 1))
                    act.wait_ge(mixed[i], count(g))
                    nc.scalar.activation(pt_hi[:, i, 0:width[i]], ps_t[i][:, 0:width[i]], ACT.Copy
                                         ).then_inc(hi_ready, 1)

                def leave_psum(g, p):
                    act.wait_ge(mixed[2 * p + 1], count(g + 1))
                    act.wait_ge(summed[p], count(g))
                    nc.scalar.activation(raw[:, p].rearrange("p i s d -> p i (s d)"), ps_o[p][:], ACT.Copy
                                         ).then_inc(left[p], 1)

                def head(g, first, last):
                    for i in range(TPS):
                        high(g, i)
                        if not last or i + 2 < TPS:
                            exponential(TPS * g + i + 2, (i + 2) % TPS)
                        if i == 1 and not first:
                            leave_psum(g - 1, 1)
                        if i == 3:
                            leave_psum(g, 0)

                for i in range(2):
                    exponential(i, i)
                head(0, True, False)
                with act.Fori(1, ALL_HEADS - 1) as g:
                    head(g, False, False)
                head(ALL_HEADS - 1, False, True)
                leave_psum(ALL_HEADS - 1, 1)

            @block.gpsimd
            def _(pool):
                with pool.Fori(0, ALL_HEADS) as g:
                    for p in range(PAIRS):
                        pool.wait_ge(left[p], count(g + 1))
                        nc.gpsimd.tensor_tensor(two_parts[:, p], raw[:, p, :, 0], raw[:, p, :, 1], ALU.add
                                                ).then_inc(added[p], 1)
                        pool.wait_ge(added[p], count(g + 1))
                        nc.gpsimd.tensor_tensor(heads_out[:, bass.ds(g, 1), 2 * p:2 * p + 2].rearrange(
                            "p a i d -> p (a i) d"), two_parts[:, p], raw[:, p, :, 2], ALU.add).then_inc(summed[p], 1)

            @block.vector
            def _(dve):
                def lower(i):
                    lo = SEQ - P - i * P
                    nc.vector.tensor_tensor_reduce(
                        neg[:, i, 0:width[i]], ps_s[i % 2][:, 0:width[i]], neg_bias[:, lo:lo + width[i]],
                        1.0, BIG, ALU.add, ALU.min, row_min[:, i:i + 1]).then_inc(lowered, 1)

                def low(g, i):
                    dve.wait_ge(hi_ready, count(TPS * g + i + 1))
                    dve.wait_ge(mixed[i], count(g))
                    nc.vector.tensor_tensor(pt_lo[:, i, 0:width[i]], ps_t[i][:, 0:width[i]],
                                            pt_hi[:, i, 0:width[i]], ALU.subtract).then_inc(lo_ready, 1)

                def head(g, last):
                    for i in range(TPS):
                        n = TPS * g + i
                        low(g, i)
                        if not last:
                            dve.wait_ge(exped, count(n + 1))
                            dve.wait_ge(scored, count(n + 5))
                            nc.vector.memset(settle[:, i:i + 1], 0.0)
                            lower(i)

                for i in range(TPS):
                    dve.wait_ge(scored, count(i + 1))
                    lower(i)
                with dve.Fori(0, ALL_HEADS - 1) as g:
                    head(g, False)
                head(ALL_HEADS - 1, True)


def rows_out_stage(nc, name, ident, heads_out, w, bias, norm_after, gamma, beta, resid, prefetch=()):
    st = Stage(nc, name)
    with st:
        turn = Turn(st, F32R)
        wf = st.sb("wf", [P, DC, D], F32)
        w_hi = st.sb("w_hi", [P, DC, D], F32R)
        w_lo = st.sb("w_lo", [P, DC, D], F32R)
        rows_in = st.sb("rows_in", [P, TPS, D], F32)
        inv_sum = st.sb("inv_sum", [P, SEQS * HEADS, TPS], F32)
        rows = {n: st.sb(n, [P, D], F32) for n in ("bias", "gamma", "beta")}
        y = st.sb("y", [P, TPS, D], F32)
        stats = st.sb("stats", [P, TPS, 6], F32)
        mv = st.sb("mv", [P, TPS, 2], F32)
        var_eps = st.sb("var_eps", [P, TPS], F32)
        rstd = st.sb("rstd", [P, TPS], F32)
        minus_half, eps = st.sb("minus_half", [P, 1], F32), st.sb("eps", [P, 1], F32)
        settle = st.sb("settle", [P, 1], F32)
        ps_y = [st.ps(f"y{j}", [P, D]) for j in range(TPS)]
        loaded, inverted = st.sem("loaded"), st.sem("inverted")
        w_hi_ready, w_lo_ready = st.sem("w_hi_ready"), st.sem("w_lo_ready")
        y_ps, y_ready = st.sem("y_ps"), st.sem("y_ready")
        shifted, stats_ready, mv_ready, pool_step, rstd_ready, scaled, added = (
            st.sem(x) for x in ("shifted", "stats_ready", "mv_ready", "pool_step", "rstd_ready", "scaled", "added"))
        vectors = [("bias", bias)] + ([("gamma", gamma), ("beta", beta)] if norm_after else [])
        shift_by = "beta" if norm_after else "bias"

        st.begin()
        with nc.Block() as block:
            @block.sync
            def _(sp):
                sp.dma_start(wf[:], w.rearrange("(c p) n -> p c n", p=P)).then_inc(loaded, 16)
                for n, v in vectors:
                    sp.dma_start(rows[n][:], row_on_all_partitions(v, D)).then_inc(loaded, 16)
                for on_chip, dram, arrived in prefetch:
                    sp.dma_start(on_chip, dram).then_inc(arrived, 16)

            @block.gpsimd
            def _(pool):
                def heads_over_sums(b):
                    pool.wait_ge(turn.turned, count(b))
                    for j in range(TPS):
                        heads = bass.ds(HEADS * b, HEADS)
                        nc.gpsimd.tensor_tensor(rows_in[:, j].rearrange("p (h d) -> p h d", d=HD),
                                                heads_out[:, heads, j, 0:HD],
                                                inv_sum[:, heads, j].unsqueeze(2).to_broadcast([P, HEADS, HD]),
                                                ALU.mult).then_inc(turn.row_ready, 1)

                def shift(b):
                    seq = resid[:, bass.ds(TPS * b, TPS), :]
                    nc.gpsimd.tensor_tensor(seq, seq, rows[shift_by][:].unsqueeze(1).to_broadcast([P, TPS, D]),
                                            ALU.add).then_inc(shifted, 1)

                nc.gpsimd.memset(minus_half[:], -0.5).then_inc(pool_step, 1)
                nc.gpsimd.memset(eps[:], LN_EPS).then_inc(pool_step, 1)
                pool.wait_ge(pool_step, count(2))
                pool.wait_ge(inverted, count(1))
                heads_over_sums(0)
                pool.wait_ge(loaded, count(16 * (1 + len(vectors))))

                def step(b, more):
                    shift(b)
                    if more:
                        heads_over_sums(b + 1)
                    if norm_after:
                        pool.wait_ge(mv_ready, count(TPS * b + TPS))
                        pool.wait_ge(added, count(TPS * b))
                        nc.gpsimd.tensor_tensor(var_eps[:], mv[:, :, 1], eps[:, 0:1].to_broadcast([P, TPS]),
                                                ALU.add).then_inc(pool_step, 1)
                        pool.wait_ge(pool_step, count(b + 3))
                        nc.gpsimd.tensor_tensor(rstd[:], var_eps[:], minus_half[:, 0:1].to_broadcast([P, TPS]),
                                                ALU.pow).then_inc(rstd_ready, 1)

                with pool.Fori(0, SEQS - 1) as b:
                    step(b, True)
                step(SEQS - 1, False)

            @block.tensor
            def _(pe):
                turn.on_tensor(nc, pe, 0, lambda j: rows_in[:, j, :], ident)
                pe.wait_ge(w_lo_ready, count(1))

                def project(b, more):
                    pe.wait_ge(turn.lo_ready, count(DC * b + DC))
                    for j in range(TPS):
                        if more and j == TPS // 2:
                            turn.on_tensor(nc, pe, b + 1, lambda j: rows_in[:, j, :], ident)
                        if j == 0:
                            pe.wait_ge(y_ready, count(TPS * b))
                        n = 0
                        for pw, px in PRODUCTS:
                            for c in range(DC):
                                x = (turn.hi, turn.lo)[px][:, c, j * P:(j + 1) * P]
                                last = nc.tensor.matmul(ps_y[j][:], x, (w_hi, w_lo)[pw][:, c, :],
                                                        start=n == 0, stop=n == 3 * DC - 1)
                                n += 1
                        last.then_inc(y_ps, 1)

                with pe.Fori(0, SEQS - 1) as b:
                    project(b, True)
                project(SEQS - 1, False)

            @block.scalar
            def _(act):
                act.wait_ge(loaded, count(16 * (1 + len(vectors))))
                nc.scalar.activation(w_hi[:], wf[:], ACT.Copy).then_inc(w_hi_ready, 1)
                with act.Fori(0, SEQS) as b:
                    act.wait_ge(y_ps, count(TPS * b))
                    turn.on_scalar(nc, act, b)

            @block.vector
            def _(dve):
                nc.vector.reciprocal(inv_sum[:], heads_out[:, :, :, HD]).then_inc(inverted, 1)
                dve.wait_ge(w_hi_ready, count(1))
                nc.vector.tensor_tensor(w_lo[:], wf[:], w_hi[:].bitcast(F32), ALU.subtract).then_inc(w_lo_ready, 1)

                def low(b):
                    dve.wait_ge(y_ps, count(TPS * b))
                    turn.on_vector(nc, dve, b)

                def leave_psum(b):
                    for j in range(TPS):
                        dve.wait_ge(y_ps, count(TPS * b + j + 1))
                        if norm_after:
                            nc.vector.tensor_tensor(y[:, j, :], ps_y[j][:], rows["bias"][:], ALU.add
                                                    ).then_inc(y_ready, 1)
                        else:
                            nc.vector.tensor_tensor(resid[:, TPS * b + j, :], ps_y[j][:],
                                                    resid[:, TPS * b + j, :], ALU.add).then_inc(y_ready, 1)
                    if norm_after:
                        for j in range(TPS):
                            dve.wait_ge(y_ready, count(TPS * b + j + 1))
                            nc.vector.bn_stats(stats[:, j, :], y[:, j, :]).then_inc(stats_ready, 1)
                        dve.wait_ge(stats_ready, count(TPS * b + TPS))
                        nc.vector.memset(settle[:], 0.0)
                        for j in range(TPS):
                            nc.vector.bn_aggr(mv[:, j, :], stats[:, j, :]).then_inc(mv_ready, 1)

                def add_normed(b):
                    dve.wait_ge(mv_ready, count(TPS * b + TPS))
                    for j in range(TPS):
                        nc.vector.scalar_tensor_tensor(out=y[:, j, :], in0=y[:, j, :], scalar=mv[:, j, 0:1],
                                                       in1=rows["gamma"][:], op0=ALU.subtract, op1=ALU.mult
                                                       ).then_inc(scaled, 1)
                    dve.wait_ge(rstd_ready, count(b + 1))
                    for j in range(TPS):
                        dve.wait_ge(scaled, count(TPS * b + j + 1))
                        nc.vector.scalar_tensor_tensor(out=resid[:, TPS * b + j, :], in0=y[:, j, :],
                                                       scalar=rstd[:, j:j + 1], in1=resid[:, TPS * b + j, :],
                                                       op0=ALU.mult, op1=ALU.add).then_inc(added, 1)

                low(0)
                dve.wait_ge(shifted, count(1))
                leave_psum(0)
                with dve.Fori(1, SEQS) as b:
                    low(b)
                    if norm_after:
                        add_normed(b - 1)
                        dve.wait_ge(added, count(TPS * b))
                    dve.wait_ge(shifted, count(b + 1))
                    leave_psum(b)
                if norm_after:
                    add_normed(SEQS - 1)


def route_stage(nc, name, ident, resid, xn, gate_w, gate_b, gates, tile_expert, gather_row, scatter_row, x_rows):
    st = Stage(nc, name)
    n_tiles = tile_expert.shape[1]
    E = EXPERTS
    with st:
        norm = Norm(st)
        x_t = st.sb("x_t", [P, 2, DC, SEQ], F32)
        gw = st.sb("gw", [E, D], F32)
        gw_t = st.sb("gw_t", [P, DC, E], F32)
        gb = st.sb("gb", [P, E], F32)
        eid = st.sb("eid", [P, E], F32)
        tau = st.sb("tau", [P, n_tiles], F32)
        before = st.sb("before", [P, P], F32)
        ones = st.sb("ones", [P, P], F32)
        t8 = {n: st.sb(n, [P, TILES, E], F32) for n in (
            "logits", "shifted", "expd", "probs", "best", "wheref", "first", "second", "both", "tile_sum",
            "run_a", "run_b", "ahead", "based", "slot", "slot1", "slot2")}
        where = st.sb("where", [P, TILES, 8], U32)
        t1 = {n: st.sb(n, [P, TILES], F32) for n in ("gmax", "gsum", "ginv")}
        t2 = {n: st.sb(n, [P, 2, TILES], F32) for n in ("slot_of", "tile_of", "rest_of")}
        edge = st.sb("edge", [P, n_tiles + 1], F32)
        bth = st.sb("bth", [P, P], F32)
        token1 = st.sb("token1", [P, TILES], F32)
        spill = st.sb("spill", [P, 1], F32)
        past = st.sb("past", [P, 2, TILES, n_tiles + 1], FP16)
        in_tile = st.sb("in_tile", [P, 2, TILES, n_tiles], FP16)
        token_in = st.sb("token_in", [P, 2, TILES, n_tiles], FP16)
        at_rest = st.sb("at_rest", [P, 2, TILES, P], FP16)
        nt = {n: st.sb(n, [P, n_tiles], F32) for n in ("found", "row", "second_row", "to_spill", "target")}
        e1 = {n: st.sb(n, [P, E], F32) for n in ("tiles_f", "tiles", "start_a", "start_b", "start", "start_p")}
        tiles_i = st.sb("tiles_i", [P, E], mybir.dt.int32)
        passed = st.sb("passed", [P, n_tiles, E], F32)
        expert_f = st.sb("expert_f", [P, n_tiles], F32)
        ps_x = [[st.ps(f"x{s}{c}", [P, SEQ]) for c in range(DC)] for s in range(2)]
        ps_l = st.ps("l", [P, TILES, E])
        ps_r = st.ps("r", [P, TILES, E])
        ps_c = st.ps("c", [P, TILES, E])
        ps_w = ps_c[:, 0:DC, :]
        ps_token, ps_second = ps_x[0][0][:, 0:n_tiles], ps_x[0][1][:, 0:n_tiles]

        loaded, const, step = st.sem("loaded"), st.sem("const"), st.sem("step")
        gw_ps, gw_ready = st.sem("gw_ps"), st.sem("gw_ready")
        row_ready, turned, x_ready, logit_ps = (st.sem(x) for x in ("row_ready", "turned", "x_ready", "logit_ps"))
        shifted_ready, expd_ready = st.sem("shifted_ready"), st.sem("expd_ready")
        picked, counted, found_ps = (st.sem(x) for x in ("picked", "counted", "found_ps"))
        tiles_known, rests_known, max_ready, rows_stored = (
            st.sem(x) for x in ("tiles_known", "rests_known", "max_ready", "rows_stored"))

        st.begin()
        with nc.Block() as block:
            @block.sync
            def _(sp):
                sp.dma_start(gw[:], gate_w).then_inc(loaded, 16)
                sp.dma_start(gb[:], row_on_all_partitions(gate_b, E)).then_inc(loaded, 16)
                for b in range(SEQS):
                    sp.wait_ge(row_ready, count(TPS * b + TPS))
                    sp.dma_start(x_rows.rearrange("(b j p) d -> b p j d", b=SEQS, p=P)[b],
                                 xn[:, TPS * b:TPS * b + TPS, :]).then_inc(rows_stored, 16)
                sp.wait_ge(rows_stored, count(16 * SEQS))

            @block.gpsimd
            def _(pool):
                pool.memset(ones[:], 1.0).then_inc(const, 1)
                pool.wait_ge(const, count(1))
                pool.affine_select(out=before[:], in_=ones[:], compare_op=ALU.is_gt, fill=0.0, base=0,
                                   pattern=[[1, P]], channel_multiplier=-1).then_inc(const, 1)
                pool.iota(eid[:], pattern=[[1, E]], base=0, channel_multiplier=0,
                          allow_small_or_imprecise_dtypes=True).then_inc(const, 1)
                pool.iota(tau[:], pattern=[[1, n_tiles]], base=0, channel_multiplier=0,
                          allow_small_or_imprecise_dtypes=True).then_inc(const, 1)
                norm.inverse_deviation(nc, pool)
                for table, step_, base, by_row in ((edge, P, 0, 0), (bth, 1, 0, 0), (token1, P, 1, 1),
                                                   (spill, 1, 2 * TOKENS + 2, 1)):
                    pool.iota(table[:], pattern=[[step_, table.shape[1]]], base=base, channel_multiplier=by_row,
                              allow_small_or_imprecise_dtypes=True).then_inc(const, 1)

            @block.tensor
            def _(pe):
                pe.wait_ge(loaded, count(32))
                for c in range(DC):
                    last = nc.tensor.transpose(ps_w[:, c, :], gw[:, c * P:(c + 1) * P], ident[0:E, 0:E])
                last.then_inc(gw_ps, 1)
                pe.wait_ge(gw_ready, count(1))

                def turn(b):
                    if b >= 2:
                        pe.wait_ge(x_ready, count(DC * (b - 1)))
                    pe.wait_ge(row_ready, count(TPS * b + TPS))
                    for j in range(TPS):
                        for c in range(DC):
                            last = nc.tensor.transpose(ps_x[b % 2][c][:, j * P:(j + 1) * P],
                                                       xn[:, TPS * b + j, c * P:(c + 1) * P], ident[:])
                    last.then_inc(turned, 1)

                turn(0)
                for b in range(SEQS):
                    if b + 1 < SEQS:
                        turn(b + 1)
                    pe.wait_ge(x_ready, count(DC * b + DC))
                    for j in range(TPS):
                        for c in range(DC):
                            last = nc.tensor.matmul(ps_l[:, TPS * b + j, :], x_t[:, b % 2, c, j * P:(j + 1) * P],
                                                    gw_t[:, c, :], start=c == 0, stop=c == DC - 1)
                    last.then_inc(logit_ps, 1)
                pe.wait_ge(picked, count(1))
                pe.wait_ge(const, count(2))
                flat = lambda x: x.rearrange("p t e -> p (t e)")
                nc.tensor.matmul(flat(ps_r[:]), before[:], flat(t8["both"][:]), start=True, stop=True
                                 ).then_inc(counted, 1)
                nc.tensor.matmul(flat(ps_c[:]), ones[:], flat(t8["both"][:]), start=True, stop=True
                                 ).then_inc(counted, 1)
                pe.wait_ge(tiles_known, count(2))
                pe.wait_ge(rests_known, count(1))
                for k in range(2):
                    for t in range(TILES):
                        last = nc.tensor.matmul(ps_token[:], at_rest[:, k, t, :], token_in[:, k, t, :],
                                                start=k == 0 and t == 0, stop=k == 1 and t == TILES - 1)
                for t in range(TILES):
                    last = nc.tensor.matmul(ps_second[:], at_rest[:, 1, t, :], in_tile[:, 1, t, :],
                                            start=t == 0, stop=t == TILES - 1)
                last.then_inc(found_ps, 1)

            @block.scalar
            def _(act):
                act.wait_ge(gw_ps, count(1))
                nc.scalar.activation(gw_t[:], ps_w[:], ACT.Copy).then_inc(gw_ready, 1)
                for b in range(SEQS):
                    act.wait_ge(turned, count(b + 1))
                    if b >= 2:
                        act.wait_ge(logit_ps, count(b - 1))
                    for c in range(DC):
                        nc.scalar.activation(x_t[:, b % 2, c, :], ps_x[b % 2][c][:], ACT.Copy).then_inc(x_ready, 1)
                act.wait_ge(shifted_ready, count(1))
                nc.scalar.activation(t8["expd"][:], t8["shifted"][:], ACT.Exp).then_inc(expd_ready, 1)

            @block.vector
            def _(dve):
                v = nc.vector
                for b in range(SEQS + 1):
                    if b < SEQS:
                        norm.statistics(nc, dve, lambda t: resid[:, t, :], b)
                    if b:
                        dve.wait_ge(norm.rstd_ready, count(b))
                        norm.rows(nc, dve, resid, lambda j: xn[:, TPS * (b - 1) + j, :], b - 1, row_ready)
                over_e = lambda x: x.unsqueeze(2).to_broadcast([P, TILES, E])
                over_t = lambda x: x.unsqueeze(1).to_broadcast([P, TILES, E])
                done = 0

                def chain(ins):
                    nonlocal done
                    done += 1
                    ins.then_inc(step, 1)
                    dve.wait_ge(step, count(done))

                dve.wait_ge(logit_ps, count(SEQS))
                dve.wait_ge(loaded, count(32))
                chain(v.tensor_tensor(t8["logits"][:], ps_l[:], over_t(gb[:]), ALU.add))
                chain(v.tensor_reduce(t1["gmax"][:], t8["logits"][:], AX.X, ALU.max))
                v.tensor_tensor(t8["shifted"][:], t8["logits"][:], over_e(t1["gmax"][:]), ALU.subtract
                                ).then_inc(shifted_ready, 1)
                dve.wait_ge(expd_ready, count(1))
                chain(v.tensor_reduce(t1["gsum"][:], t8["expd"][:], AX.X, ALU.add))
                chain(v.reciprocal(t1["ginv"][:], t1["gsum"][:]))
                chain(v.tensor_tensor(t8["probs"][:], t8["expd"][:], over_e(t1["ginv"][:]), ALU.mult))
                for t in range(TILES):
                    v.max(out=t8["best"][:, t, :], in_=t8["probs"][:, t, :]).then_inc(max_ready, 1)
                for t in range(TILES):
                    dve.wait_ge(max_ready, count(t + 1))
                    v.max_index(out=where[:, t, :], in_max=t8["best"][:, t, :], in_values=t8["probs"][:, t, :]
                                ).then_inc(step, 1)
                done += TILES
                dve.wait_ge(step, count(done))
                chain(v.tensor_copy(t8["wheref"][:], where[:]))
                chain(v.tensor_copy(gates[0][:], t8["best"][:, :, 0]))
                chain(v.tensor_copy(gates[1][:], t8["best"][:, :, 1]))
                dve.wait_ge(const, count(8))
                for k, n in enumerate(("first", "second")):
                    chain(v.tensor_tensor(t8[n][:], over_t(eid[:]), over_e(t8["wheref"][:, :, k]), ALU.is_equal))
                v.tensor_tensor(t8["both"][:], t8["first"][:], t8["second"][:], ALU.add).then_inc(picked, 1)
                dve.wait_ge(counted, count(2))
                chain(v.tensor_copy(t8["tile_sum"][:], ps_c[:]))
                src, dst = "tile_sum", "run_a"
                for d in (1, 2, 4, 8):
                    chain(v.tensor_copy(t8[dst][:, 0:d], t8[src][:, 0:d]))
                    chain(v.tensor_tensor(t8[dst][:, d:], t8[src][:, d:], t8[src][:, :TILES - d], ALU.add))
                    src, dst = dst, "run_b" if dst == "run_a" else "run_a"
                chain(v.tensor_tensor(t8["ahead"][:], t8[src][:], t8["tile_sum"][:], ALU.subtract))
                chain(v.tensor_scalar(e1["tiles_f"][:], t8[src][:, TILES - 1, :], 1.0 / P, 0.5 - 0.5 / P,
                                      ALU.mult, ALU.add))
                chain(v.tensor_copy(tiles_i[:], e1["tiles_f"][:]))
                chain(v.tensor_copy(e1["tiles"][:], tiles_i[:]))
                src, dst = "tiles", "start_a"
                for d in (1, 2, 4):
                    chain(v.tensor_copy(e1[dst][:, 0:d], e1[src][:, 0:d]))
                    chain(v.tensor_tensor(e1[dst][:, d:], e1[src][:, d:], e1[src][:, :E - d], ALU.add))
                    src, dst = dst, "start_b" if dst == "start_a" else "start_a"
                chain(v.tensor_tensor(e1["start"][:], e1[src][:], e1["tiles"][:], ALU.subtract))
                chain(v.tensor_scalar(e1["start_p"][:], e1["start"][:], float(P), None, ALU.mult))
                chain(v.tensor_tensor(t8["based"][:], t8["ahead"][:], over_t(e1["start_p"][:]), ALU.add))
                chain(v.tensor_tensor(t8["slot"][:], ps_r[:], t8["based"][:], ALU.add))
                for k, n in enumerate(("first", "second")):
                    chain(v.tensor_tensor(t8[f"slot{k + 1}"][:], t8[n][:], t8["slot"][:], ALU.mult))
                    chain(v.tensor_reduce(t2["slot_of"][:, k], t8[f"slot{k + 1}"][:], AX.X, ALU.add))
                for k in range(2):
                    over = lambda x, n: x.unsqueeze(2).to_broadcast([P, TILES, n])
                    along = lambda x, n: x.unsqueeze(1).to_broadcast([P, TILES, n])
                    chain(v.tensor_tensor(past[:, k], over(t2["slot_of"][:, k], n_tiles + 1),
                                          along(edge[:], n_tiles + 1), ALU.is_ge))
                    v.tensor_reduce(t2["tile_of"][:, k], past[:, k, :, 1:], AX.X, ALU.add).then_inc(step, 1)
                    chain(v.tensor_tensor(in_tile[:, k], past[:, k, :, 0:n_tiles], past[:, k, :, 1:], ALU.subtract))
                    done += 1
                    dve.wait_ge(step, count(done))
                    v.tensor_tensor(token_in[:, k], in_tile[:, k], over(token1[:], n_tiles), ALU.mult
                                    ).then_inc(tiles_known, 1)
                chain(v.scalar_tensor_tensor(out=t2["rest_of"][:], in0=t2["tile_of"][:], scalar=-float(P),
                                             in1=t2["slot_of"][:], op0=ALU.mult, op1=ALU.add))
                v.tensor_tensor(at_rest[:], t2["rest_of"][:].unsqueeze(3).to_broadcast([P, 2, TILES, P]),
                                bth[:].unsqueeze(1).unsqueeze(1).to_broadcast([P, 2, TILES, P]), ALU.is_equal
                                ).then_inc(rests_known, 1)
                chain(v.tensor_tensor(passed[:], tau[:].unsqueeze(2).to_broadcast([P, n_tiles, E]),
                                      e1["start"][:].unsqueeze(1).to_broadcast([P, n_tiles, E]), ALU.is_ge))
                chain(v.tensor_reduce(expert_f[:], passed[:, :, 1:E], AX.X, ALU.add))
                chain(v.tensor_copy(tile_expert[:], expert_f[:]))
                dve.wait_ge(found_ps, count(1))
                chain(v.tensor_copy(nt["found"][:], ps_token[:]))
                chain(v.tensor_scalar(nt["row"][:], nt["found"][:], -1.0, 0.0, ALU.add, ALU.max))
                v.tensor_copy(gather_row[:], nt["row"][:]).then_inc(step, 1)
                chain(v.tensor_scalar(nt["to_spill"][:], nt["found"][:], 0.0, spill[:, 0:1], ALU.is_equal, ALU.mult))
                done += 1
                chain(v.scalar_tensor_tensor(out=nt["second_row"][:], in0=nt["found"][:], scalar=2.0,
                                             in1=ps_second[:], op0=ALU.mult, op1=ALU.add))
                chain(v.scalar_tensor_tensor(out=nt["target"][:], in0=nt["second_row"][:], scalar=-2.0,
                                             in1=nt["to_spill"][:], op0=ALU.add, op1=ALU.add))
                chain(v.tensor_copy(scatter_row[:], nt["target"][:]))


def experts_stage(nc, name, ident, wts, b1c, b2, tile_expert, gather_row, scatter_row, x_rows, y_rows, weights_in,
                  weights_all):
    st = Stage(nc, name)
    n_tiles = tile_expert.shape[1]
    HALF = 512
    with st:
        x_in = st.sb("x_in", [P, 2, D], F32)
        x_t = st.sb("x_t", [P, 2, DC, P], F32)
        h = st.sb("h", [P, 2, HIDDEN], F32)
        h_t = st.sb("h_t", [P, 2, HC, P], F32)
        y = st.sb("y", [P, 2, D], F32)
        b2r = st.sb("b2r", [P, EXPERTS, D], F32)
        ps_x = st.ps("x", [P, DC, P])
        ps_h = [st.ps(f"h{i}", [P, HALF]) for i in range(2)]
        ps_t = [st.ps(f"t{i}", [P, HC // 2, P]) for i in range(2)]
        ps_y = st.ps("y", [P, D])
        loaded = st.sem("loaded")
        x_loaded = [st.zero_sem(f"x_loaded{s}") for s in range(2)]
        x_ps, x_ready = st.sem("x_ps"), st.sem("x_ready")
        h_ps, h_ready = st.sem("h_ps"), st.sem("h_ready")
        t_ps, t_ready = st.sem("t_ps"), st.sem("t_ready")
        y_ps, y_ready = st.sem("y_ps"), st.sem("y_ready")
        y_stored = [st.zero_sem(f"y_stored{s}") for s in range(2)]
        w1, w2 = wts

        st.begin()
        with nc.Block() as block:
            @block.sync
            def _(sp):
                sp.dma_start(b2r[:], bass.AP(tensor=b2.tensor, offset=b2.offset, ap=[[0, P], [D, EXPERTS], [1, D]])
                             ).then_inc(loaded, 16)

            @block.gpsimd
            def _(pool):
                def gather(t):
                    pool.indirect_dma_start(out=x_in[:, t % 2, :], out_offset=None, in_=x_rows,
                                            in_offset=bass.IndirectOffsetOnAxis(ap=gather_row[:, t:t + 1], axis=0)
                                            ).then_inc(x_loaded[t % 2], 16)

                for t in range(2):
                    gather(t)
                pool.wait_ge(x_ps, count(1))
                gather(2)
                for t in range(n_tiles):
                    if t + 3 < n_tiles:
                        pool.wait_ge(x_ps, count(t + 2))
                        gather(t + 3)
                    pool.wait_ge(y_ready, count(t + 1))
                    if t:
                        pool.wait_ge(y_stored[(t - 1) % 2], 16 * ((t + 1) // 2))
                    pool.indirect_dma_start(out=y_rows, in_=y[:, t % 2, :], in_offset=None,
                                            out_offset=bass.IndirectOffsetOnAxis(ap=scatter_row[:, t:t + 1], axis=0)
                                            ).then_inc(y_stored[t % 2], 16)
                pool.wait_ge(y_stored[0], 16 * ((n_tiles + 1) // 2))
                pool.wait_ge(y_stored[1], 16 * (n_tiles // 2))

            @block.tensor
            def _(pe):
                def expert(t):
                    return pe.value_load(tile_expert[0:1, bass.ds(t, 1)], min_val=0, max_val=EXPERTS - 1)

                def turn_x(t, s, u):
                    pe.wait_ge(x_loaded[s], 16 * u + 16)
                    pe.wait_ge(x_ready, count(t))
                    for c in range(DC):
                        last = nc.tensor.transpose(ps_x[:, c, :], x_in[:, s, c * P:(c + 1) * P], ident[:])
                    last.then_inc(x_ps, 1)

                def hidden(t, s, e):
                    pe.wait_ge(x_ready, count(t + 1))
                    pe.wait_ge(h_ready, count(2 * t))
                    for half in range(2):
                        for c in range(DC):
                            last = nc.tensor.matmul(
                                ps_h[half][:], x_t[:, s, c, :],
                                w1[:, bass.ds(e, 1), c, half * HALF:(half + 1) * HALF].rearrange("p a n -> p (a n)"),
                                start=c == 0, stop=c == DC - 1)
                        last.then_inc(h_ps, 1)

                def turn_h(t, s):
                    pe.wait_ge(t_ready, count(t))
                    for half in range(2):
                        pe.wait_ge(h_ready, count(2 * t + half + 1))
                        for m in range(HC // 2):
                            at = (half * HC // 2 + m) * P
                            last = nc.tensor.transpose(ps_t[half][:, m, :], h[:, s, at:at + P], ident[:])
                        last.then_inc(t_ps, 1)

                def output(t, s, e):
                    pe.wait_ge(t_ready, count(t + 1))
                    pe.wait_ge(y_ready, count(t))
                    for m in range(HC):
                        last = nc.tensor.matmul(ps_y[:], h_t[:, s, m, :],
                                                w2[:, bass.ds(e, 1), m, :].rearrange("p a n -> p (a n)"),
                                                start=m == 0, stop=m == HC - 1)
                    last.then_inc(y_ps, 1)

                pe.wait_ge(weights_in, weights_all)
                turn_x(0, 0, 0)
                hidden(0, 0, expert(0))
                turn_x(1, 1, 0)
                turn_h(0, 0)
                with pe.Fori(0, (n_tiles - 2) // 2) as u:
                    for s in range(2):
                        t = 2 * u + s + 1
                        hidden(t, 1 - s, expert(t))
                        turn_x(t + 1, s, u + 1)
                        output(t - 1, s, expert(t - 1))
                        turn_h(t, 1 - s)
                for t in range((n_tiles - 2) // 2 * 2 + 1, n_tiles):
                    hidden(t, t % 2, expert(t))
                    if t + 1 < n_tiles:
                        turn_x(t + 1, (t + 1) % 2, (t + 1) // 2)
                    output(t - 1, (t - 1) % 2, expert(t - 1))
                    turn_h(t, t % 2)
                output(n_tiles - 1, (n_tiles - 1) % 2, expert(n_tiles - 1))

            @block.scalar
            def _(act):
                act.wait_ge(weights_in, weights_all)

                def step(t, s):
                    act.wait_ge(x_ps, count(t + 1))
                    act.wait_ge(h_ps, count(2 * t))
                    nc.scalar.activation(x_t[:, s, :, :], ps_x[:], ACT.Copy).then_inc(x_ready, 1)

                def relu(t, s, after_first=True):
                    e = act.value_load(tile_expert[0:1, bass.ds(t, 1)], min_val=0, max_val=EXPERTS - 1)
                    if after_first:
                        act.wait_ge(y_ps, count(t - 1))
                    for m in range(HC):
                        if m % (HC // 2) == 0:
                            act.wait_ge(t_ps, count(2 * t + m // (HC // 2) + 1))
                        last = nc.scalar.activation(h_t[:, s, m, :], ps_t[m // (HC // 2)][:, m % (HC // 2), :],
                                                    ACT.Relu, bias=b1c[:, bass.ds(e * HC + m, 1)])
                    last.then_inc(t_ready, 1)

                step(0, 0)
                step(1, 1)
                relu(0, 0, False)
                with act.Fori(0, (n_tiles - 2) // 2) as u:
                    for s in range(2):
                        t = 2 * u + s + 1
                        step(t + 1, s)
                        relu(t, 1 - s)
                for t in range((n_tiles - 2) // 2 * 2 + 1, n_tiles):
                    if t + 1 < n_tiles:
                        step(t + 1, (t + 1) % 2)
                    relu(t, t % 2)

            @block.vector
            def _(dve):
                dve.wait_ge(loaded, count(16))

                def rows_of_hidden(t, s):
                    for half in range(2):
                        dve.wait_ge(h_ps, count(2 * t + half + 1))
                        nc.vector.tensor_copy(h[:, s, half * HALF:(half + 1) * HALF], ps_h[half][:]
                                              ).then_inc(h_ready, 1)

                def rows_of_output(t, s, u, first=False):
                    e = dve.value_load(tile_expert[0:1, bass.ds(t, 1)], min_val=0, max_val=EXPERTS - 1)
                    dve.wait_ge(y_ps, count(t + 1))
                    if first is False:
                        dve.wait_ge(y_stored[s], 16 * u)
                    nc.vector.tensor_tensor(y[:, s, :], ps_y[:],
                                            b2r[:, bass.ds(e, 1), :].rearrange("p a n -> p (a n)"), ALU.add
                                            ).then_inc(y_ready, 1)

                def step(u, first):
                    for s in range(2):
                        t = 2 * u + s + 1
                        dve.wait_ge(t_ps, count(2 * t - 2))
                        rows_of_hidden(t, 1 - s)
                        rows_of_output(t - 1, s, u, first)

                rows_of_hidden(0, 0)
                step(0, True)
                with dve.Fori(1, (n_tiles - 1) // 2) as u:
                    step(u, False)
                for t in range((n_tiles - 1) // 2 * 2 + 1, n_tiles):
                    dve.wait_ge(t_ps, count(2 * t - 2))
                    rows_of_hidden(t, t % 2)
                    rows_of_output(t - 1, (t - 1) % 2, (t - 1) // 2)
                rows_of_output(n_tiles - 1, (n_tiles - 1) % 2, (n_tiles - 1) // 2)


def combine_stage(nc, name, gates, y_rows, resid):
    st = Stage(nc, name)
    with st:
        y = st.sb("y", [P, TILES, 2, D], F32)
        second = st.sb("second", [P, TILES, D], F32)
        loaded = [st.sem(f"loaded{b}") for b in range(SEQS)]
        first_added, gated, added = (st.sem(x) for x in ("first_added", "gated", "added"))
        rows = y_rows[0:2 * TOKENS].rearrange("(b j p k) d -> b p j k d", b=SEQS, p=P, k=2)
        st.begin()
        with nc.Block() as block:
            @block.sync
            def _(sp):
                for b in range(SEQS):
                    sp.dma_start(y[:, TPS * b:TPS * b + TPS], rows[b]).then_inc(loaded[b], 16)

            @block.scalar
            def _(act):
                for b in range(SEQS):
                    act.wait_ge(loaded[b], count(16))
                    for t in range(TPS * b, TPS * b + TPS):
                        nc.scalar.activation(second[:, t, :], y[:, t, 1, :], ACT.Copy, scale=gates[1][:, t:t + 1]
                                             ).then_inc(gated, 1)

            @block.vector
            def _(dve):
                for b in range(SEQS):
                    seq = slice(TPS * b, TPS * b + TPS)
                    dve.wait_ge(loaded[b], count(16))
                    for t in range(TPS * b, TPS * b + TPS):
                        nc.vector.scalar_tensor_tensor(out=resid[:, t, :], in0=y[:, t, 0, :],
                                                       scalar=gates[0][:, t:t + 1], in1=resid[:, t, :],
                                                       op0=ALU.mult, op1=ALU.add).then_inc(first_added, 1)
                    dve.wait_ge(gated, count(TPS * b + TPS))
                    dve.wait_ge(first_added, count(TPS * b + TPS))
                    nc.vector.tensor_tensor(resid[:, seq, :], resid[:, seq, :], second[:, seq, :], ALU.add
                                            ).then_inc(added, 1)


def signs_stage(nc, name, ident, resid, bits0, bits1, bits2, s_all, bits_in, bits_all, out):
    st = Stage(nc, name)
    EIGHTH = 0.125
    ON_ACT = 5
    with st:
        norm, turn = Norm(st), Turn(st, FP16)
        xn = st.sb("xn", [P, TPS, D], F32)
        diff = st.sb("diff", [P, DC, HIDDEN], FP16)
        wa = st.sb("wa", [P, DC, HIDDEN], FP16)
        wb_mul, wb_off = st.sb("wb_mul", [P, 1], F32), st.sb("wb_off", [P, 1], F32)
        wb = st.sb("wb", [P, HC, HIDDEN], FP16)
        wc = st.sb("wc", [P, HC, D], FP16)
        pos, neg = st.sb("pos", [P, 3], F32), st.sb("neg", [P, 3], F32)
        sign, size = st.sb("sign", [P, 3], F32), st.sb("size", [P, 3], F32)
        size01, factor = st.sb("size01", [P, 1], F32), st.sb("factor", [P, 1], F32)
        factor64 = st.sb("factor64", [P, 1], F32)
        ga = [st.sb(f"ga_{x}", [P, HC, SEQ], FP16) for x in ("hi", "lo")]
        gb = [st.sb(f"gb_{x}", [P, HC, SEQ], FP16) for x in ("hi", "lo")]
        rows = st.sb("rows", [P, TPS, D], F32)
        ps = [st.ps(f"layer{i}", [P, SEQ]) for i in range(4)]
        ps_y = [st.ps(f"y{i}", [P, D]) for i in range(2)]

        step, wa_r, wb_r, wc_r, factor_r, coefs_r = (
            st.sem(x) for x in ("step", "wa_r", "wb_r", "wc_r", "factor_r", "coefs_r"))
        layer_ps, hi_ready, lo_ready = (st.sem(x) for x in ("layer_ps", "hi_ready", "lo_ready"))
        y_ps, y_ready, stored = st.sem("y_ps"), st.sem("y_ready"), st.sem("stored")
        out_t = out.rearrange("b (j p) d -> b p j d", p=P)

        st.begin()
        with nc.Block() as block:
            @block.sync
            def _(sp):
                with sp.Fori(0, SEQS) as b:
                    sp.wait_ge(y_ready, count(TPS * b + TPS))
                    sp.dma_start(out_t[b], rows[:]).then_inc(stored, 16)
                sp.wait_ge(stored, count(16 * SEQS))

            @block.gpsimd
            def _(pool):
                norm.inverse_deviation(nc, pool)
                pool.wait_ge(bits_in, bits_all)
                nc.gpsimd.tensor_scalar(wc[:], bits2[:], 2.0, -1.0, ALU.mult, ALU.add).then_inc(wc_r, 1)

            @block.tensor
            def _(pe):
                def layer(b, which, src, w, chunks):
                    for m in range(HC):
                        n = 2 * HC * b + HC * which + m
                        if which == 0 and m < 4:
                            pe.wait_ge(lo_ready, count(2 * HC * b))
                        else:
                            pe.wait_ge(lo_ready, count(n - 3))
                        for k in range(chunks):
                            if which == 1 and m == 0:
                                pe.wait_ge(lo_ready, count(2 * HC * b + k + 1))
                            for x in range(2):
                                last = nc.tensor.matmul(ps[m % 4][:], w[:, k, m * P:(m + 1) * P], src[x][:, k, :],
                                                        start=k == 0 and x == 0, stop=k == chunks - 1 and x == 1)
                        last.then_inc(layer_ps, 1)

                def layers(b, more):
                    pe.wait_ge(turn.lo_ready, count(DC * b + DC))
                    layer(b, 0, (turn.hi, turn.lo), wa, DC)
                    pe.wait_ge(wb_r, count(HC))
                    layer(b, 1, ga, wb, HC)
                    if more:
                        turn.on_tensor(nc, pe, b + 1, lambda j: xn[:, j, :], ident)
                    pe.wait_ge(wc_r, count(1))
                    for j in range(TPS):
                        pe.wait_ge(y_ready, count(TPS * b + max(j - 1, 0)))
                        for k in range(HC):
                            if j == 0:
                                pe.wait_ge(lo_ready, count(2 * HC * b + HC + k + 1))
                            for x in range(2):
                                last = nc.tensor.matmul(ps_y[j % 2][:], gb[x][:, k, j * P:(j + 1) * P], wc[:, k, :],
                                                        start=k == 0 and x == 0, stop=k == HC - 1 and x == 1)
                        last.then_inc(y_ps, 1)

                turn.on_tensor(nc, pe, 0, lambda j: xn[:, j, :], ident)
                pe.wait_ge(wa_r, count(1))
                with pe.Fori(0, SEQS - 1) as b:
                    layers(b, True)
                layers(SEQS - 1, False)

            @block.scalar
            def _(act):
                act.wait_ge(coefs_r, count(2))
                act.wait_ge(bits_in, bits_all)
                for k in range(ON_ACT):
                    nc.scalar.activation(wb[:, k, :], bits1[:, k, :], ACT.Identity, bias=wb_off[:, 0:1],
                                         scale=wb_mul[:, 0:1]).then_inc(wb_r, 1)
                    if k == ON_ACT // 2:
                        turn.on_scalar(nc, act, 0)

                def layers(b, more):
                    for which, g in enumerate((ga, gb)):
                        if which:
                            act.wait_ge(y_ps, count(TPS * b))
                        else:
                            act.wait_ge(layer_ps, count(2 * HC * b))
                        for m in range(HC):
                            act.wait_ge(layer_ps, count(2 * HC * b + HC * which + m + 1))
                            nc.scalar.activation(g[0][:, m, :], ps[m % 4][:], ACT.Relu).then_inc(hi_ready, 1)
                    if more:
                        turn.on_scalar(nc, act, b + 1)

                with act.Fori(0, SEQS - 1) as b:
                    layers(b, True)
                layers(SEQS - 1, False)

            @block.vector
            def _(dve):
                v = nc.vector
                tile = lambda t: resid[:, t, :]

                def normalise(b):
                    dve.wait_ge(turn.turned, count(b))
                    norm.rows(nc, dve, resid, lambda j: xn[:, j, :], b, turn.row_ready)

                norm.statistics(nc, dve, tile, 0)
                dve.wait_ge(bits_in, bits_all)
                done = 0

                def chain(ins):
                    nonlocal done
                    done += 1
                    ins.then_inc(step, 1)
                    dve.wait_ge(step, count(done))

                chain(v.tensor_scalar(pos[:], s_all[:], 0.0, None, ALU.is_gt))
                chain(v.tensor_scalar(neg[:], s_all[:], 0.0, None, ALU.is_lt))
                chain(v.tensor_tensor(sign[:], pos[:], neg[:], ALU.subtract))
                v.tensor_scalar(wb_mul[:], sign[:, 1:2], 2 * EIGHTH, None, ALU.mult).then_inc(coefs_r, 1)
                v.tensor_scalar(wb_off[:], sign[:, 1:2], -EIGHTH, None, ALU.mult).then_inc(coefs_r, 1)
                chain(v.tensor_tensor(size[:], sign[:], s_all[:], ALU.mult))
                chain(v.tensor_tensor(size01[:], size[:, 0:1], size[:, 1:2], ALU.mult))
                chain(v.tensor_tensor(factor[:], size01[:], s_all[:, 2:3], ALU.mult))
                v.tensor_scalar(factor64[:], factor[:], 8.0 / EIGHTH, None, ALU.mult).then_inc(factor_r, 1)
                chain(v.tensor_tensor(diff[:], bits0[:, 0], bits0[:, 1], ALU.subtract))
                v.tensor_scalar(wa[:], diff[:], sign[:, 0:1], None, ALU.mult).then_inc(wa_r, 1)
                dve.wait_ge(norm.rstd_ready, count(1))
                normalise(0)
                norm.statistics(nc, dve, tile, 1)
                turn.on_vector(nc, dve, 0)
                dve.wait_ge(coefs_r, count(2))
                for k in range(ON_ACT, HC):
                    v.tensor_scalar(wb[:, k, :], bits1[:, k, :], wb_mul[:, 0:1], wb_off[:, 0:1], ALU.mult, ALU.add
                                    ).then_inc(wb_r, 1)
                norm.statistics(nc, dve, tile, 2)
                norm.statistics(nc, dve, tile, 3)
                dve.wait_ge(norm.rstd_ready, count(SEQS))
                dve.wait_ge(factor_r, count(1))

                def layers(b, more):
                    for which, g in enumerate((ga, gb)):
                        if which:
                            dve.wait_ge(y_ps, count(TPS * b))
                        for m in range(HC):
                            dve.wait_ge(hi_ready, count(2 * HC * b + HC * which + m + 1))
                            v.scalar_tensor_tensor(out=g[1][:, m, :], in0=ps[m % 4][:], scalar=0.0, in1=g[0][:, m, :],
                                                   op0=ALU.max, op1=ALU.subtract).then_inc(lo_ready, 1)
                        if more and not which:
                            normalise(b + 1)
                    if more:
                        turn.on_vector(nc, dve, b + 1)
                    dve.wait_ge(stored, count(16 * b))
                    for j in range(TPS):
                        dve.wait_ge(y_ps, count(TPS * b + j + 1))
                        v.scalar_tensor_tensor(out=rows[:, j, :], in0=ps_y[j % 2][:], scalar=factor64[:, 0:1],
                                               in1=resid[:, TPS * b + j, :], op0=ALU.mult, op1=ALU.add
                                               ).then_inc(y_ready, 1)

                with dve.Fori(0, SEQS - 1) as b:
                    layers(b, True)
                layers(SEQS - 1, False)


def tower(nc, x, L0_tok_weight, L0_attn_Wq, L0_attn_bq, L0_attn_Wk, L0_attn_bk, L0_attn_Wv, L0_attn_bv,
          L0_attn_Wo, L0_attn_bo, L0_attn_gamma, L0_attn_beta, L0_ffn_gate_w, L0_ffn_gate_b, L0_ffn_w1,
          L0_ffn_b1, L0_ffn_w2, L0_ffn_b2, L1_attn_Wqkv, L1_attn_bqkv, L1_attn_Wout, L1_attn_bout,
          L1_attn_rel_pos_bias, L1_ffn_k0, L1_ffn_k1, L1_ffn_k2, L1_ffn_s0, L1_ffn_s1, L1_ffn_s2, out):
    n_tiles = (2 * TOKENS + EXPERTS * (P - 1)) // P
    scratch = [nc.dram_tensor(f"qk_scratch{i}", (SEQS, PARTS, 2 * D, SEQ), BF16).ap() for i in range(2)]
    x_rows = nc.dram_tensor("x_rows", (TOKENS, D), F32).ap()
    y_rows = nc.dram_tensor("y_rows", (2 * TOKENS + P, D), F32).ap()
    with ExitStack() as forever:
        forever.enter_context(nc.allow_non_contiguous_dma(reason="token ids and bias columns, a few KB"))
        sb = lambda n, shape, dt: forever.enter_context(nc.sbuf_tensor(n, shape, dt))
        resid = sb("resid", [P, TILES, D], F32)
        ident = sb("ident", [P, P], F32)
        neg_causal = sb("neg_causal", [P, SEQ], F32)
        neg_rel = sb("neg_rel", [P, SPAN], F32)

        embed_stage(nc, x, L0_tok_weight, resid, L1_attn_rel_pos_bias, ident, neg_causal, neg_rel)

        shared = sb("shared", [P, SEQS * HEADS * TPS * VC], F32)
        heads_out = shared[:].rearrange("p (g i d) -> p g i d", i=TPS, d=VC)
        routed_rows = shared[:, 0:TILES * D].rearrange("p (t d) -> p t d", d=D)

        def attention(name, i, w_parts, b_qk, b_v, neg_bias, causal):
            with ExitStack() as ctx:
                v_parts = ctx.enter_context(nc.sbuf_tensor(f"{name}_v_parts", [P, TILES, HEADS, PARTS, VC], BF16))
                stacks = Stacks(nc, ctx, name, scratch[i])
                qkv_stage(nc, f"{name}_qkv", ident, resid, w_parts, b_qk, b_v, scratch[i], v_parts, stacks)
                attention_stage(nc, f"{name}_core", ident, neg_bias, causal, stacks, v_parts, heads_out)

        attention("attn0", 0, [L0_attn_Wq, L0_attn_Wk, L0_attn_Wv], [L0_attn_bq, L0_attn_bk], L0_attn_bv,
                  neg_causal, True)

        gather_row, scatter_row = (sb(x, [P, n_tiles], U32) for x in ("gather_row", "scatter_row"))
        gates = [sb(f"gates{k}", [P, TILES], F32) for k in range(2)]
        tile_expert = sb("tile_expert", [P, n_tiles], mybir.dt.int32)
        weights_in = forever.enter_context(nc.semaphore("weights_in"))
        with ExitStack() as ctx:
            wts = [ctx.enter_context(nc.sbuf_tensor("w1_all", [P, EXPERTS, DC, HIDDEN], F32)),
                   ctx.enter_context(nc.sbuf_tensor("w2_all", [P, EXPERTS, HC, D], F32))]
            loads = [(on_chip[:, e], w[e].rearrange("(c p) n -> p c n", p=P), weights_in)
                     for e in range(EXPERTS) for on_chip, w in zip(wts, (L0_ffn_w1, L0_ffn_w2))]
            b1c = ctx.enter_context(nc.sbuf_tensor("b1c", [P, EXPERTS * HC], F32))
            loads.append((b1c[:], L0_ffn_b1.rearrange("e (m p) -> p (e m)", p=P), weights_in))
            rows_out_stage(nc, "attn0_out", ident, heads_out, L0_attn_Wo, L0_attn_bo, True, L0_attn_gamma,
                           L0_attn_beta, resid, prefetch=loads)
            route_stage(nc, "route", ident, resid, routed_rows, L0_ffn_gate_w, L0_ffn_gate_b, gates, tile_expert, gather_row,
                        scatter_row, x_rows)
            experts_stage(nc, "experts", ident, wts, b1c, L0_ffn_b2, tile_expert, gather_row, scatter_row,
                          x_rows, y_rows, weights_in, 16 * len(loads))
        combine_stage(nc, "combine", gates, y_rows, resid)

        attention("attn1", 1, [L1_attn_Wqkv], [L1_attn_bqkv[0:2 * D]], L1_attn_bqkv[2 * D:3 * D], neg_rel, False)
        bits0 = sb("bits0", [P, 2, DC, HIDDEN], U8)
        bits1 = sb("bits1", [P, HC, HIDDEN], U8)
        bits2 = sb("bits2", [P, HC, D], U8)
        s_all = sb("s_all", [P, 3], F32)
        bits_in = forever.enter_context(nc.semaphore("bits_in"))
        loads = [(bits0[:], L1_ffn_k0.rearrange("(h c p) n -> p h c n", h=2, p=P), bits_in),
                 (bits1[:], L1_ffn_k1.rearrange("(m p) n -> p m n", p=P), bits_in),
                 (bits2[:], L1_ffn_k2.rearrange("(m p) n -> p m n", p=P), bits_in)]
        loads += [(s_all[:, i:i + 1], bass.AP(tensor=s.tensor, offset=s.offset, ap=[[0, P], [1, 1]]), bits_in)
                  for i, s in enumerate((L1_ffn_s0, L1_ffn_s1, L1_ffn_s2))]
        rows_out_stage(nc, "attn1_out", ident, heads_out, L1_attn_Wout, L1_attn_bout, False, None, None, resid,
                       prefetch=loads)
        signs_stage(nc, "signs", ident, resid, bits0, bits1, bits2, s_all, bits_in, 16 * len(loads), out)


_INS = ["x", "L0_tok_weight", "L0_attn_Wq", "L0_attn_bq", "L0_attn_Wk", "L0_attn_bk", "L0_attn_Wv", "L0_attn_bv",
        "L0_attn_Wo", "L0_attn_bo", "L0_attn_gamma", "L0_attn_beta", "L0_ffn_gate_w", "L0_ffn_gate_b", "L0_ffn_w1",
        "L0_ffn_b1", "L0_ffn_w2", "L0_ffn_b2", "L1_attn_Wqkv", "L1_attn_bqkv", "L1_attn_Wout", "L1_attn_bout",
        "L1_attn_rel_pos_bias", "L1_ffn_k0", "L1_ffn_k1", "L1_ffn_k2", "L1_ffn_s0", "L1_ffn_s1", "L1_ffn_s2"]


def kernel(**inputs):
    import numpy as _np
    import concourse.bacc as _bacc
    from concourse import mybir as _mybir
    from concourse.bass_utils import run_bass_kernel_spmd as _run

    nc = _bacc.Bacc("TRN2", target_bir_lowering=False, num_devices=1)
    arrays, args = {}, []
    for name in _INS:
        a = _np.ascontiguousarray(inputs[name])
        if a.ndim == 0:
            a = a.reshape(1)
        arrays[f"in_{name}"] = a
        args.append(nc.dram_tensor(f"in_{name}", a.shape, _mybir.dt.from_np(a.dtype), kind="ExternalInput").ap())
    out = nc.dram_tensor("out_0", (SEQS, SEQ, D), _mybir.dt.float32, kind="ExternalOutput").ap()
    tower(nc, *args, out)
    r = _run(nc, [arrays], core_ids=[0])
    return r.results[0]["out_0"]
```
